# Optimizing a Trainium2 kernel written in Bass

```python
import numpy as np
import jax
import jax.numpy as jnp

def _softmax(x, axis=-1):
    return jax.nn.softmax(x, axis=axis)

def _gelu(x):
    return jax.nn.gelu(x, approximate=True)

def _silu(x):
    return jax.nn.silu(x)

def _sigmoid(x):
    return jax.nn.sigmoid(x)

def _layernorm(x, axis=-1, eps=1e-05):
    m = jnp.mean(x, axis=axis, keepdims=True)
    v = jnp.var(x, axis=axis, keepdims=True)
    return (x - m) / jnp.sqrt(v + eps)

def _scatter_add(tgt, idx, src, axis=0):
    return tgt.at[idx].add(src)

def _segment_sum(src, seg, n):
    return jax.ops.segment_sum(src, seg, n)
kernel_name = 'mk_adaln_ffn_d4_seqx_r4_18e123'

def setup_inputs(seed: int=0):
    np.random.seed(seed)
    _w = jnp.asarray

    def _rec_inputs():
        import jax
        import jax.numpy as jnp
        _rk = jax.random.key(seed)
        x = -0.000125 + 0.9999 * jax.random.normal(jax.random.fold_in(_rk, 1), (8, 512, 256), jnp.float32)
        _lenS = 512 - jax.random.randint(jax.random.fold_in(_rk, 7), (8,), 0, max(1, 512 // 4) + 1, jnp.int32)
        _lenS2 = 512 - jax.random.randint(jax.random.fold_in(_rk, 8), (8,), 0, max(1, 512 // 4) + 1, jnp.int32)
        cond_1024 = -0.00493535 + 1.00056 * jax.random.normal(jax.random.fold_in(_rk, 11), (8, 256), jnp.float32)
        return (x, cond_1024)
    x, cond_1024 = _rec_inputs()

    def _L0_cond_setup():
        import jax, jax.numpy as jnp
        import numpy as np
        INPUT_DIM = 256
        HIDDEN_DIM = 256
        CHUNK_SIZE = 4

        def _linear_params(key, fan_in, fan_out):
            kw, kb = jax.random.split(key)
            bound = 1.0 / np.sqrt(fan_in)
            W = jax.random.uniform(kw, (fan_in, fan_out), jnp.float32, -bound, bound)
            b = jax.random.uniform(kb, (fan_out,), jnp.float32, -bound, bound)
            return (W, b)

        def _gru_forward(x, h0, Wz, bz, Wr, br, Wh, bh, Wp, bp):
            B, T, D = x.shape
            t = jnp.arange(T)
            do_prop = ((t + 1) % CHUNK_SIZE == 0) & (t < T - 1)
            xs = jnp.transpose(x, (1, 0, 2))

            def step(h, inp):
                x_t, prop = inp
                comb = jnp.concatenate([x_t, h], axis=-1)
                z = jax.nn.sigmoid(comb @ Wz + bz)
                r = jax.nn.sigmoid(comb @ Wr + br)
                comb2 = jnp.concatenate([x_t, r * h], axis=-1)
                h_cand = jnp.tanh(comb2 @ Wh + bh)
                h_new = (1.0 - z) * h + z * h_cand
                h_next = jnp.where(prop, jnp.tanh(h_new @ Wp + bp), h_new)
                return (h_next, h_new)
            _, ys = jax.lax.scan(step, h0, (xs, do_prop))
            return jnp.transpose(ys, (1, 0, 2))
        key = jax.random.key(seed)
        ks = jax.random.split(key, 6)
        x = jax.random.normal(ks[0], (64, 128, INPUT_DIM), jnp.float32)
        h0 = jax.random.normal(ks[1], (64, HIDDEN_DIM), jnp.float32)
        Wz, bz = _linear_params(ks[2], INPUT_DIM + HIDDEN_DIM, HIDDEN_DIM)
        Wr, br = _linear_params(ks[3], INPUT_DIM + HIDDEN_DIM, HIDDEN_DIM)
        Wh, bh = _linear_params(ks[4], INPUT_DIM + HIDDEN_DIM, HIDDEN_DIM)
        Wp, bp = _linear_params(ks[5], HIDDEN_DIM, HIDDEN_DIM)
        return {'x': x, 'h0': h0, 'Wz': Wz, 'bz': bz, 'Wr': Wr, 'br': br, 'Wh': Wh, 'bh': bh, 'Wp': Wp, 'bp': bp}
    _L0_cond_all = _L0_cond_setup()
    _L0_cond_in = {k: v for k, v in _L0_cond_all.items() if k in ('Wz', 'bz', 'Wr', 'br', 'Wh', 'bh', 'Wp', 'bp')}
    del _L0_cond_all

    def _L0_ffn_setup():
        import jax, jax.numpy as jnp
        import numpy as np
        from jax import lax
        D = 256
        E = 8
        F = 1024
        TOP_K = 2
        key = jax.random.key(seed)
        ks = jax.random.split(key, 8)
        s = 0.02
        return {'x': jax.random.normal(ks[0], (4, 512, D), dtype=jnp.float32), 'gate_w': jax.random.normal(ks[1], (D, E), dtype=jnp.float32) * s, 'gate_b': jnp.zeros((E,), dtype=jnp.float32), 'w1': jax.random.normal(ks[2], (E, D, F), dtype=jnp.float32) * s, 'b1': jnp.zeros((E, F), dtype=jnp.float32), 'w2': jax.random.normal(ks[3], (E, F, D), dtype=jnp.float32) * s, 'b2': jnp.zeros((E, D), dtype=jnp.float32)}
    _L0_ffn_all = _L0_ffn_setup()
    _L0_ffn_in = {k: v for k, v in _L0_ffn_all.items() if k in ('gate_w', 'gate_b', 'w1', 'b1', 'w2', 'b2')}
    del _L0_ffn_all

    def _L1_cond_setup():
        import jax, jax.numpy as jnp
        import numpy as np
        D, HS, HE, E, K = (256, 512, 256, 8, 2)
        B, T = (4, 256)
        N_SHARED = 1
        key = jax.random.key(seed)
        ks = jax.random.split(key, 9)
        g = lambda k, shape, s: jax.random.normal(k, shape, jnp.float32) * s
        return {'x': g(ks[0], (B, T, D), 1.0), 't_emb': g(ks[1], (B, D), 1.0), 'router_W': g(ks[2], (2 * D, E), 0.01), 'router_bias': jnp.zeros((E,), jnp.float32), 'w1': g(ks[3], (D, HS), 0.02), 'w3': g(ks[4], (D, HS), 0.02), 'w2': g(ks[5], (HS, D), 0.02), 'W1e': g(ks[6], (E, D, HE), 0.02), 'W2e': g(ks[7], (E, HE, D), 0.02)}
    _L1_cond_all = _L1_cond_setup()
    _L1_cond_in = {k: v for k, v in _L1_cond_all.items() if k in ('router_W', 'router_bias', 'w1', 'w3', 'w2', 'W1e', 'W2e')}
    del _L1_cond_all

    def _L1_ffn_setup():
        import jax, jax.numpy as jnp
        import numpy as np
        D_MODEL = 256
        D_FF = 1024
        N_EXPERTS = 8
        D_EXPERT = D_FF // N_EXPERTS
        TOP_K = 2
        LB_WEIGHT = 0.01
        B, S = (4, 512)

        def _top_k_softmax(logits, k):
            vals, _ = jax.lax.top_k(logits, k)
            thresh = vals[..., -1:]
            masked = jnp.where(logits >= thresh, logits, -jnp.inf)
            return jax.nn.softmax(masked, axis=-1)
        key = jax.random.key(seed)
        ks = jax.random.split(key, 8)
        x = jax.random.normal(ks[0], (B, S, D_MODEL), dtype=jnp.float32)
        w1 = jax.random.normal(ks[1], (N_EXPERTS, D_MODEL, D_EXPERT), dtype=jnp.float32) * (1.0 / np.sqrt(D_MODEL))
        b1 = jnp.zeros((N_EXPERTS, D_EXPERT), dtype=jnp.float32)
        w2 = jax.random.normal(ks[2], (N_EXPERTS, D_EXPERT, D_MODEL), dtype=jnp.float32) * (1.0 / np.sqrt(D_EXPERT))
        b2 = jnp.zeros((N_EXPERTS, D_MODEL), dtype=jnp.float32)
        centroids = jax.random.normal(ks[3], (N_EXPERTS, D_MODEL), dtype=jnp.float32) * 0.02
        w_route = jax.random.normal(ks[4], (N_EXPERTS, D_MODEL), dtype=jnp.float32) * (1.0 / np.sqrt(D_MODEL))
        return {'x': x, 'w1': w1, 'b1': b1, 'w2': w2, 'b2': b2, 'centroids': centroids, 'w_route': w_route}
    _L1_ffn_all = _L1_ffn_setup()
    _L1_ffn_in = {k: v for k, v in _L1_ffn_all.items() if k in ('w1', 'b1', 'w2', 'b2', 'centroids', 'w_route')}
    del _L1_ffn_all

    def _L2_cond_setup():
        import jax, jax.numpy as jnp
        import numpy as np
        key = jax.random.key(seed)
        ks = jax.random.split(key, 8)
        B, L, D, N, K = (4, 1024, 256, 64, 4)
        return {'x': jax.random.normal(ks[0], (B, L, D), dtype=jnp.float32), 'conv_w': jax.random.normal(ks[1], (K, 1, D), dtype=jnp.float32) * 0.1, 'conv_b': jnp.zeros((D,), dtype=jnp.float32), 'Wp': jax.random.normal(ks[2], (D, 2 * N), dtype=jnp.float32) * (1.0 / np.sqrt(D)), 'bp': jnp.zeros((2 * N,), dtype=jnp.float32), 'Ws': jax.random.normal(ks[3], (D, N), dtype=jnp.float32) * (1.0 / np.sqrt(D)), 'bs': jnp.zeros((N,), dtype=jnp.float32), 'A_log': jax.random.normal(ks[4], (N,), dtype=jnp.float32) * 0.02, 'dt_log': jax.random.normal(ks[5], (N,), dtype=jnp.float32) * 0.02, 'Wo': jax.random.normal(ks[6], (N, D), dtype=jnp.float32) * (1.0 / np.sqrt(N)), 'bo': jnp.zeros((D,), dtype=jnp.float32)}
    _L2_cond_all = _L2_cond_setup()
    _L2_cond_in = {k: v for k, v in _L2_cond_all.items() if k in ('conv_b', 'Wp', 'bp', 'Ws', 'bs', 'A_log', 'dt_log', 'Wo', 'bo')}
    del _L2_cond_all

    def _L2_ffn_setup():
        import jax, jax.numpy as jnp
        import numpy as np
        from jax import lax
        T, B, I, M, O = (64, 64, 256, 256, 256)

        def _xavier(key, shape):
            fan_out, fan_in = shape
            limit = float(np.sqrt(6.0 / (fan_in + fan_out)))
            return jax.random.uniform(key, shape, jnp.float32, -limit, limit)
        key = jax.random.key(seed)
        ks = jax.random.split(key, 9)
        x = jax.random.normal(ks[0], (T, B, I), jnp.float32)
        return {'x': x, 'wf': _xavier(ks[1], (M, I)), 'uf': _xavier(ks[2], (M, M)), 'bf': jnp.zeros((M,), jnp.float32), 'wi': _xavier(ks[3], (M, I)), 'ui': _xavier(ks[4], (M, M)), 'bi': jnp.zeros((M,), jnp.float32), 'wc': _xavier(ks[5], (M, I)), 'uc': _xavier(ks[6], (M, M)), 'bc': jnp.zeros((M,), jnp.float32), 'wo': _xavier(ks[7], (O, I)), 'uo': _xavier(ks[8], (O, M)), 'bo': jnp.zeros((O,), jnp.float32), 'in_c': jnp.zeros((M,), jnp.float32)}
    _L2_ffn_all = _L2_ffn_setup()
    _L2_ffn_in = {k: v for k, v in _L2_ffn_all.items() if k in ('wf', 'uf', 'bf', 'wi', 'ui', 'bi', 'wc', 'uc', 'bc', 'wo', 'uo', 'bo', 'in_c')}
    del _L2_ffn_all

    def _L3_cond_setup():
        import jax, jax.numpy as jnp
        import numpy as np
        IN_FEATURES = 256
        OUT_FEATURES = 256
        BATCH = 32
        SEQ = 256
        EPS = 1e-08
        key = jax.random.key(seed)
        k1, k2, k3 = jax.random.split(key, 3)
        Efou = jax.random.normal(k1, (BATCH, SEQ, IN_FEATURES), dtype=jnp.float32)
        y = jax.random.normal(k2, (BATCH, IN_FEATURES), dtype=jnp.float32)
        weight = jax.random.normal(k3, (IN_FEATURES, OUT_FEATURES), dtype=jnp.float32)
        return {'Efou': Efou, 'y': y, 'weight': weight}
    _L3_cond_all = _L3_cond_setup()
    _L3_cond_in = {k: v for k, v in _L3_cond_all.items() if k in ('weight',)}
    del _L3_cond_all

    def _L3_ffn_setup():
        import jax, jax.numpy as jnp
        import numpy as np
        CAPACITY_FACTOR = 0.5
        key = jax.random.key(seed)
        ks = jax.random.split(key, 5)
        B, S, D, F = (4, 1024, 256, 1024)
        scale_in = 1.0 / np.sqrt(D)
        scale_ff = 1.0 / np.sqrt(F)
        return {'hidden_states': jax.random.normal(ks[0], (B, S, D), dtype=jnp.float32), 'w_router': jax.random.normal(ks[1], (D,), dtype=jnp.float32) * scale_in, 'W1': jax.random.normal(ks[2], (D, F), dtype=jnp.float32) * scale_in, 'b1': jnp.zeros((F,), dtype=jnp.float32), 'W2': jax.random.normal(ks[3], (F, D), dtype=jnp.float32) * scale_ff, 'b2': jnp.zeros((D,), dtype=jnp.float32)}
    _L3_ffn_all = _L3_ffn_setup()
    _L3_ffn_in = {k: v for k, v in _L3_ffn_all.items() if k in ('w_router', 'W1', 'b1', 'W2', 'b2')}
    del _L3_ffn_all
    return {'x': x, 'cond_1024': cond_1024, 'L0_cond_Wz': _L0_cond_in['Wz'], 'L0_cond_bz': _L0_cond_in['bz'], 'L0_cond_Wr': _L0_cond_in['Wr'], 'L0_cond_br': _L0_cond_in['br'], 'L0_cond_Wh': _L0_cond_in['Wh'], 'L0_cond_bh': _L0_cond_in['bh'], 'L0_cond_Wp': _L0_cond_in['Wp'], 'L0_cond_bp': _L0_cond_in['bp'], 'L0_ffn_gate_w': _L0_ffn_in['gate_w'], 'L0_ffn_gate_b': _L0_ffn_in['gate_b'], 'L0_ffn_w1': _L0_ffn_in['w1'], 'L0_ffn_b1': _L0_ffn_in['b1'], 'L0_ffn_w2': _L0_ffn_in['w2'], 'L0_ffn_b2': _L0_ffn_in['b2'], 'L1_cond_router_W': _L1_cond_in['router_W'], 'L1_cond_router_bias': _L1_cond_in['router_bias'], 'L1_cond_w1': _L1_cond_in['w1'], 'L1_cond_w3': _L1_cond_in['w3'], 'L1_cond_w2': _L1_cond_in['w2'], 'L1_cond_W1e': _L1_cond_in['W1e'], 'L1_cond_W2e': _L1_cond_in['W2e'], 'L1_ffn_w1': _L1_ffn_in['w1'], 'L1_ffn_b1': _L1_ffn_in['b1'], 'L1_ffn_w2': _L1_ffn_in['w2'], 'L1_ffn_b2': _L1_ffn_in['b2'], 'L1_ffn_centroids': _L1_ffn_in['centroids'], 'L1_ffn_w_route': _L1_ffn_in['w_route'], 'L2_cond_conv_b': _L2_cond_in['conv_b'], 'L2_cond_Wp': _L2_cond_in['Wp'], 'L2_cond_bp': _L2_cond_in['bp'], 'L2_cond_Ws': _L2_cond_in['Ws'], 'L2_cond_bs': _L2_cond_in['bs'], 'L2_cond_A_log': _L2_cond_in['A_log'], 'L2_cond_dt_log': _L2_cond_in['dt_log'], 'L2_cond_Wo': _L2_cond_in['Wo'], 'L2_cond_bo': _L2_cond_in['bo'], 'L2_ffn_wf': _L2_ffn_in['wf'], 'L2_ffn_uf': _L2_ffn_in['uf'], 'L2_ffn_bf': _L2_ffn_in['bf'], 'L2_ffn_wi': _L2_ffn_in['wi'], 'L2_ffn_ui': _L2_ffn_in['ui'], 'L2_ffn_bi': _L2_ffn_in['bi'], 'L2_ffn_wc': _L2_ffn_in['wc'], 'L2_ffn_uc': _L2_ffn_in['uc'], 'L2_ffn_bc': _L2_ffn_in['bc'], 'L2_ffn_wo': _L2_ffn_in['wo'], 'L2_ffn_uo': _L2_ffn_in['uo'], 'L2_ffn_bo': _L2_ffn_in['bo'], 'L2_ffn_in_c': _L2_ffn_in['in_c'], 'L3_cond_weight': _L3_cond_in['weight'], 'L3_ffn_w_router': _L3_ffn_in['w_router'], 'L3_ffn_W1': _L3_ffn_in['W1'], 'L3_ffn_b1': _L3_ffn_in['b1'], 'L3_ffn_W2': _L3_ffn_in['W2'], 'L3_ffn_b2': _L3_ffn_in['b2']}

def reference(x, cond_1024, L0_cond_Wz, L0_cond_bz, L0_cond_Wr, L0_cond_br, L0_cond_Wh, L0_cond_bh, L0_cond_Wp, L0_cond_bp, L0_ffn_gate_w, L0_ffn_gate_b, L0_ffn_w1, L0_ffn_b1, L0_ffn_w2, L0_ffn_b2, L1_cond_router_W, L1_cond_router_bias, L1_cond_w1, L1_cond_w3, L1_cond_w2, L1_cond_W1e, L1_cond_W2e, L1_ffn_w1, L1_ffn_b1, L1_ffn_w2, L1_ffn_b2, L1_ffn_centroids, L1_ffn_w_route, L2_cond_conv_b, L2_cond_Wp, L2_cond_bp, L2_cond_Ws, L2_cond_bs, L2_cond_A_log, L2_cond_dt_log, L2_cond_Wo, L2_cond_bo, L2_ffn_wf, L2_ffn_uf, L2_ffn_bf, L2_ffn_wi, L2_ffn_ui, L2_ffn_bi, L2_ffn_wc, L2_ffn_uc, L2_ffn_bc, L2_ffn_wo, L2_ffn_uo, L2_ffn_bo, L2_ffn_in_c, L3_cond_weight, L3_ffn_w_router, L3_ffn_W1, L3_ffn_b1, L3_ffn_W2, L3_ffn_b2):
    import jax
    import jax.numpy as jnp

    def _L0_cond_ref(x, h0, Wz, bz, Wr, br, Wh, bh, Wp, bp):
        import jax, jax.numpy as jnp
        import numpy as np
        INPUT_DIM = 256
        HIDDEN_DIM = 256
        CHUNK_SIZE = 4

        def _linear_params(key, fan_in, fan_out):
            kw, kb = jax.random.split(key)
            bound = 1.0 / np.sqrt(fan_in)
            W = jax.random.uniform(kw, (fan_in, fan_out), jnp.float32, -bound, bound)
            b = jax.random.uniform(kb, (fan_out,), jnp.float32, -bound, bound)
            return (W, b)

        def _gru_forward(x, h0, Wz, bz, Wr, br, Wh, bh, Wp, bp):
            B, T, D = x.shape
            t = jnp.arange(T)
            do_prop = ((t + 1) % CHUNK_SIZE == 0) & (t < T - 1)
            xs = jnp.transpose(x, (1, 0, 2))

            def step(h, inp):
                x_t, prop = inp
                comb = jnp.concatenate([x_t, h], axis=-1)
                z = jax.nn.sigmoid(comb @ Wz + bz)
                r = jax.nn.sigmoid(comb @ Wr + br)
                comb2 = jnp.concatenate([x_t, r * h], axis=-1)
                h_cand = jnp.tanh(comb2 @ Wh + bh)
                h_new = (1.0 - z) * h + z * h_cand
                h_next = jnp.where(prop, jnp.tanh(h_new @ Wp + bp), h_new)
                return (h_next, h_new)
            _, ys = jax.lax.scan(step, h0, (xs, do_prop))
            return jnp.transpose(ys, (1, 0, 2))
        return _gru_forward(x, h0, Wz, bz, Wr, br, Wh, bh, Wp, bp)

    def _L0_ffn_ref(x, gate_w, gate_b, w1, b1, w2, b2):
        import jax, jax.numpy as jnp
        import numpy as np
        from jax import lax
        D = 256
        E = 8
        F = 1024
        TOP_K = 2
        B, S, _ = x.shape
        flat = x.reshape(-1, D)
        T = flat.shape[0]
        logits = flat @ gate_w + gate_b
        topv, topi = lax.top_k(logits, TOP_K)
        topw = jax.nn.softmax(topv.astype(jnp.float32), axis=-1).astype(x.dtype)
        routing = jnp.zeros_like(logits).at[jnp.arange(T)[:, None], topi].set(topw)

        def body(acc, params):
            W1e, b1e, W2e, b2e, we = params
            h = jax.nn.gelu(flat @ W1e + b1e, approximate=False)
            out = h @ W2e + b2e
            return (acc + out * we[:, None], None)
        init = jnp.zeros_like(flat)
        final, _ = lax.scan(body, init, (w1, b1, w2, b2, routing.T))
        return final.reshape(B, S, D)

    def _L1_cond_ref(x, t_emb, router_W, router_bias, w1, w3, w2, W1e, W2e):
        import jax, jax.numpy as jnp
        import numpy as np
        D, HS, HE, E, K = (256, 512, 256, 8, 2)
        B, T = (4, 256)
        N_SHARED = 1
        Bb, Tt, C = x.shape
        xf = x.reshape(-1, C)
        tf = jnp.broadcast_to(t_emb[:, None, :], (Bb, Tt, C)).reshape(-1, C)
        N = xf.shape[0]
        shared = jax.nn.silu(xf @ w1) * (xf @ w3) @ w2
        s = jax.nn.sigmoid((jnp.concatenate([xf, tf], axis=-1) @ router_W).astype(jnp.float32))
        sel_scores = s + router_bias
        _, topk_idx = jax.lax.top_k(sel_scores, K)
        s_sel = jnp.take_along_axis(s, topk_idx, axis=1)
        denom = s_sel.sum(axis=1, keepdims=True)
        gates = jnp.where(denom > 1e-09, s_sel / (denom + 1e-09), 1.0 / K).astype(x.dtype)
        combine = jnp.zeros((N, E), x.dtype).at[jnp.arange(N)[:, None], topk_idx].add(gates)
        h = jax.nn.gelu(jnp.einsum('nc,ech->enh', xf, W1e), approximate=False)
        y = jnp.einsum('enh,ehc->enc', h, W2e)
        routed = jnp.einsum('ne,enc->nc', combine, y)
        return ((shared + routed) / (N_SHARED + K)).reshape(Bb, Tt, C)

    def _L1_ffn_ref(x, w1, b1, w2, b2, centroids, w_route):
        import jax, jax.numpy as jnp
        import numpy as np
        D_MODEL = 256
        D_FF = 1024
        N_EXPERTS = 8
        D_EXPERT = D_FF // N_EXPERTS
        TOP_K = 2
        LB_WEIGHT = 0.01
        B, S = (4, 512)

        def _top_k_softmax(logits, k):
            vals, _ = jax.lax.top_k(logits, k)
            thresh = vals[..., -1:]
            masked = jnp.where(logits >= thresh, logits, -jnp.inf)
            return jax.nn.softmax(masked, axis=-1)
        eps = 1e-12
        x_norm = x / jnp.maximum(jnp.linalg.norm(x, axis=-1, keepdims=True), eps)
        c_norm = centroids / jnp.maximum(jnp.linalg.norm(centroids, axis=-1, keepdims=True), eps)
        cos_scores = jnp.einsum('bsd,ed->bse', x_norm, c_norm)
        route_scores = jnp.einsum('bsd,ed->bse', x, w_route)
        logits = cos_scores + route_scores
        gates = _top_k_softmax(logits, TOP_K)
        h = jax.nn.gelu(jnp.einsum('bsd,edh->bseh', x, w1) + b1, approximate=False)
        expert_out = jnp.einsum('bseh,ehd->bsed', h, w2) + b2
        out = jnp.einsum('bse,bsed->bsd', gates, expert_out)
        return out

    def _L2_cond_ref(x, conv_w, conv_b, Wp, bp, Ws, bs, A_log, dt_log, Wo, bo):
        import jax, jax.numpy as jnp
        import numpy as np
        B, L, D = x.shape
        K = conv_w.shape[0]
        N = Ws.shape[1]
        x_pad = jnp.pad(x, ((0, 0), (K - 1, 0), (0, 0)))
        conv = conv_b + sum((x_pad[:, k:k + L, :] * conv_w[k, 0] for k in range(K)))
        proj = conv @ Wp + bp
        B_t = jax.nn.softplus(proj[..., :N])
        C_t = jnp.tanh(proj[..., N:])
        u = x @ Ws + bs
        A = -jax.nn.softplus(A_log)
        dt = jax.nn.softplus(dt_log)
        decay = 1.0 + dt * A

        def step(state, inputs):
            u_t, b_t, c_t = inputs
            state = decay * state + dt * b_t * u_t
            return (state, c_t * state)
        init = jnp.zeros((B, N), dtype=x.dtype)
        xs = tuple((jnp.swapaxes(a, 0, 1) for a in (u, B_t, C_t)))
        _, ys = jax.lax.scan(step, init, xs, unroll=4)
        y = jnp.swapaxes(ys, 0, 1)
        return y @ Wo + bo

    def _L2_ffn_ref(x, wf, uf, bf, wi, ui, bi, wc, uc, bc, wo, uo, bo, in_c):
        import jax, jax.numpy as jnp
        import numpy as np
        from jax import lax
        T, B, I, M, O = (64, 64, 256, 256, 256)

        def _xavier(key, shape):
            fan_out, fan_in = shape
            limit = float(np.sqrt(6.0 / (fan_in + fan_out)))
            return jax.random.uniform(key, shape, jnp.float32, -limit, limit)
        batch = x.shape[1]
        c0 = jnp.broadcast_to(in_c, (batch, in_c.shape[0]))

        def step(c, xt):
            ft = jax.nn.sigmoid(xt @ wf.T + c @ uf.T + bf)
            it = jax.nn.sigmoid(xt @ wi.T + c @ ui.T + bi)
            gt = jnp.tanh(xt @ wc.T + c @ uc.T + bc)
            c = ft * c + it * gt
            return (c, None)
        c_final, _ = lax.scan(step, c0, x)
        h = jnp.tanh(jnp.einsum('tbi,oi->tbo', x, wo) + c_final @ uo.T + bo)
        return h

    def _L3_cond_ref(Efou, y, weight):
        import jax, jax.numpy as jnp
        import numpy as np
        IN_FEATURES = 256
        OUT_FEATURES = 256
        BATCH = 32
        SEQ = 256
        EPS = 1e-08
        scale = 1.0 / np.sqrt(np.float32(weight.shape[0]))
        ys = y * scale
        d = jax.lax.rsqrt(jnp.einsum('bi,io->bo', ys * ys, weight * weight) + EPS)
        out = jnp.einsum('bsi,io->bso', Efou * ys[:, None, :], weight) * d[:, None, :]
        return out

    def _L3_ffn_ref(hidden_states, w_router, W1, b1, W2, b2):
        import jax, jax.numpy as jnp
        import numpy as np
        CAPACITY_FACTOR = 0.5
        'Mixture-of-Depths block: route top-k tokens through an FFN inner block,\n            scatter back with sigmoid router weights; bypassed tokens pass through.'
        B, S, D = hidden_states.shape
        k = int(S * CAPACITY_FACTOR)
        scores = jnp.einsum('bsd,d->bs', hidden_states, w_router)
        top_scores, top_idx = jax.lax.top_k(scores, k)
        weights = jax.nn.sigmoid(top_scores)
        selected = jnp.take_along_axis(hidden_states, top_idx[:, :, None], axis=1)
        h = jax.nn.gelu(jnp.einsum('bkd,df->bkf', selected, W1) + b1)
        processed = jnp.einsum('bkf,fd->bkd', h, W2) + b2
        update = weights[:, :, None] * processed

        def scatter_one(xb, ib, ub):
            return xb.at[ib].add(ub)
        output = jax.vmap(scatter_one)(hidden_states, top_idx, update)
        return output
    x = x + _L0_ffn_ref(_L0_cond_ref(x, cond_1024, L0_cond_Wz, L0_cond_bz, L0_cond_Wr, L0_cond_br, L0_cond_Wh, L0_cond_bh, L0_cond_Wp, L0_cond_bp), L0_ffn_gate_w, L0_ffn_gate_b, L0_ffn_w1, L0_ffn_b1, L0_ffn_w2, L0_ffn_b2)
    x = x + _L1_ffn_ref(_L1_cond_ref(x, cond_1024, L1_cond_router_W, L1_cond_router_bias, L1_cond_w1, L1_cond_w3, L1_cond_w2, L1_cond_W1e, L1_cond_W2e), L1_ffn_w1, L1_ffn_b1, L1_ffn_w2, L1_ffn_b2, L1_ffn_centroids, L1_ffn_w_route)
    x = x + _L2_ffn_ref(_L2_cond_ref(x, cond_1024[:, None, :], L2_cond_conv_b, L2_cond_Wp, L2_cond_bp, L2_cond_Ws, L2_cond_bs, L2_cond_A_log, L2_cond_dt_log, L2_cond_Wo, L2_cond_bo), L2_ffn_wf, L2_ffn_uf, L2_ffn_bf, L2_ffn_wi, L2_ffn_ui, L2_ffn_bi, L2_ffn_wc, L2_ffn_uc, L2_ffn_bc, L2_ffn_wo, L2_ffn_uo, L2_ffn_bo, L2_ffn_in_c)
    x = x + _L3_ffn_ref(_L3_cond_ref(x, cond_1024, L3_cond_weight), L3_ffn_w_router, L3_ffn_W1, L3_ffn_b1, L3_ffn_W2, L3_ffn_b2)
    return x

_drawn_inputs = setup_inputs


def setup_inputs(seed=0):
    import zlib

    import numpy as np

    out = dict(_drawn_inputs(seed))
    spreads = {'L0_ffn_gate_b': (0.0, 0.1),
     'L0_ffn_b1': (0.0, 0.1),
     'L0_ffn_b2': (0.0, 0.1),
     'L1_cond_router_bias': (0.0, 0.1),
     'L1_ffn_b1': (0.0, 0.1),
     'L1_ffn_b2': (0.0, 0.1),
     'L2_cond_conv_b': (0.0, 0.1),
     'L2_cond_bp': (0.0, 0.1),
     'L2_cond_bs': (0.0, 0.1),
     'L2_cond_bo': (0.0, 0.1),
     'L2_ffn_bf': (0.0, 0.512),
     'L2_ffn_bi': (0.0, 0.571),
     'L2_ffn_bc': (0.0, 0.1),
     'L2_ffn_bo': (0.0, 0.1),
     'L2_ffn_in_c': (0.0, 0.8),
     'L3_ffn_b1': (0.0, 0.407),
     'L3_ffn_b2': (0.0, 0.279)}
    factors = {'L0_cond_bz': 4.866,
     'L0_cond_Wr': 4.304,
     'L0_cond_br': 8.0,
     'L1_ffn_w1': 4.472,
     'L2_cond_A_log': 4.224,
     'L2_cond_dt_log': 4.442}
    for name, (base, spread) in spreads.items():
        noise = np.random.default_rng([zlib.crc32(name.encode()), seed]).standard_normal(out[name].shape)
        drawn = base * np.exp(spread * noise) if base else spread * noise
        out[name] = jnp.asarray(drawn.astype(out[name].dtype))
    for name, factor in factors.items():
        out[name] = (out[name] * factor).astype(out[name].dtype)
    return out
```

```python
from contextlib import ExitStack

import numpy as np

import concourse.bass as bass
from concourse import mybir

F32 = mybir.dt.float32
F16 = mybir.dt.float16
ALU = mybir.AluOpType
ACT = mybir.ActivationFunctionType
AX_X = mybir.AxisListType.X

P = 128
B, T, D = 8, 512, 256
KD = D // P
NTOK = B * T
STEPS = 16
TURNS = T // STEPS
CHUNK = 4
HSCALE = 256.0
WSCALE = 256.0
GSCALE = HSCALE * WSCALE
E = 8
RING = 4
TILE = 512
NTILE = NTOK // TILE
NSUB = TILE // P
FAR = -3.0e38
F0 = 1024 // P
FS = 512 // P
FE = 256 // P
N1C = FS + E * FE
F3 = 1024 // P
TOPK3 = T // 2
NS = 64


def build_program(nc, t, out, stop=None, dbg=None):
    ctx = ExitStack()
    with ctx:
        def sb(name, shape, dt=F32):
            return ctx.enter_context(nc.sbuf_tensor(name, shape, dt))

        def sem(name):
            return ctx.enter_context(nc.semaphore(name))

        XT = sb("XT", [P, KD, NTOK])
        HT = sb("HT", [P, KD, NTOK])
        WA = sb("WA", [P, 8192])
        WB = sb("WB", [P, 11264])
        GB = sb("GB", [P, 8192])
        ident = sb("ident", [P, P])
        ones = sb("ones", [P, P])
        condrow = sb("condrow", [B, D])
        condT = sb("condT", [P, KD, B])

        banks = [ctx.enter_context(nc.psum_tensor(f"bank{i}", [P, 512], F32)) for i in range(8)]

        xstage = GB[:, 0:2048].rearrange("p (n s d) -> p n s d", n=2, s=4)
        wx = WB[:, 0:1536].rearrange("p (g k m) -> p g k m", g=3, k=KD)
        wraw = WB[:, 1536:3584].rearrange("p (g k m) -> p g k m", g=4, k=KD)
        wpart = WB[:, 4096:6144].bitcast(F16).rearrange("p (g n k m) -> p g n k m", g=4, n=2, k=KD)
        gbias = sb("gbias", [1, 4, D])
        hid = sb("hid", [P, RING, TILE])
        hidf = hid[:].rearrange("p r c -> p (r c)")
        w0 = [WA[:, i * 4096:(i + 1) * 4096] for i in range(2)]
        w0_up = [w[:, 0:2048].rearrange("p (k f) -> p k f", k=KD) for w in w0]
        w0_down = [w[:, 2048:4096].rearrange("p (f d) -> p f d", f=F0) for w in w0]
        b0_up = sb("b0_up", [P, 2, F0])
        b0_down = sb("b0_down", [P, 2, KD])
        g0 = GB[:].rearrange("p (n c) -> p n c", n=2)
        outt = sb("outt", [P, KD, TILE])
        RL = 17
        NBLK = NTOK // P
        logitT = hid[0:RL, 0:2]
        gT = hid[0:NSUB * E, 2:4].rearrange("p r (g c) -> p (r g) c", c=P)
        rw = sb("rw", [P, 3, KD, RL])
        rsq = sb("rsq", [P, KD, RL])
        rcond = sb("rcond", [P, KD, E])
        rcol = sb("rcol", [E, B])
        rbias0 = sb("rbias0", [E, 1])
        rbias1 = sb("rbias1", [P, E])
        def rt(i, n=E):
            o = i * NBLK * E
            return GB[:, o:o + NBLK * n].rearrange("p (b n) -> p b n", n=n)
        r_log, r_sel, r_eq, r_mask1, r_mask2, r_w, r_tmp = (rt(i) for i in range(7))
        r_m1, r_m2, r_p1, r_p2, r_x, r_y, r_z, r_v = (rt(7 + i, 1) for i in range(8))
        r_raw = GB[:, 4096:4096 + NBLK * RL].rearrange("p (b n) -> p b n", n=RL)
        prefer = sb("prefer", [P, E])
        cent = sb("cent", [E, D])
        cent_sq = sb("cent_sq", [E, D])
        cent_n = sb("cent_n", [E, 4])
        route = sb("route", [E, D])
        wsh1 = WB[:, 0:1024].rearrange("p (k f) -> p k f", k=KD)
        wsh3 = WB[:, 1024:2048].rearrange("p (k f) -> p k f", k=KD)
        wsh2 = WB[:, 2048:3072].rearrange("p (f d) -> p f d", f=FS)
        w1e = WB[:, 3072:7168].rearrange("p (e k f) -> p e k f", e=E, k=KD)
        w2e = WB[:, 7168:11264].rearrange("p (e f d) -> p e f d", e=E, f=FE)
        g1 = GB[:].rearrange("p (n e c) -> p n e c", n=2, e=E)
        v1 = WA[:, 0:2048].rearrange("p (e k f) -> p e k f", e=E, k=KD)
        v2 = WA[:, 2048:4096].rearrange("p (e d) -> p e d", e=E)
        v1b = sb("v1b", [P, E])
        v2b = sb("v2b", [E, D])
        g1T = sb("g1T", [E, 2, TILE])
        uraw = WA[:, 4096:8192].rearrange("p (g k m) -> p g k m", g=8, k=KD)
        uT = WA[:, 0:4096].rearrange("p (g k m) -> p g k m", g=8, k=KD)
        wp2 = WB[:, 5120:5376].rearrange("p (k m) -> p k m", k=KD)
        ws2 = WB[:, 5376:5504].rearrange("p (k m) -> p k m", k=KD)
        wo2 = WB[0:NS, 5504:5760]
        ssm = WB[0:NS, 6144:10240]
        ssm_c, ssm_b, ssm_u = GB[0:NS, 0:4096], GB[0:NS, 4096:8192], HT[0:NS, 0]
        small2 = sb("small2", [NS, 12])
        cb2 = sb("cb2", [P, KD])
        bo2 = sb("bo2", [P, KD])
        decay = WB[0:NS, 10240:10752]
        gb2 = sb("gb2", [P, 4, KD])
        cinit = sb("cinit", [P, KD])
        c2 = WB[:, 7168:8192].rearrange("p (k c) -> p k c", k=KD)
        lstm = GB[:, 0:5120].rearrange("p (h g k c) -> p h g k c", h=2, g=5, k=KD)
        y2 = GB[:, 5120:7168].rearrange("p (n k c) -> p n k c", n=2, k=KD)
        cpart = WB[:, 8192:9216].rearrange("p (k c) -> p k c", k=KD)
        w3_up = WB[:, 0:2048].rearrange("p (k f) -> p k f", k=KD)
        w3_down = WB[:, 2048:4096].rearrange("p (f d) -> p f d", f=F3)
        w3c = WB[:, 4096:4608].rearrange("p (k m) -> p k m", k=KD)
        w3sq = WB[:, 4608:5120].rearrange("p (k m) -> p k m", k=KD)
        b3_up = sb("b3_up", [P, F3])
        b3_down = sb("b3_down", [P, KD])
        ys3 = sb("ys3", [P, KD, B])
        ysq3 = sb("ysq3", [P, KD, B])
        d3 = sb("d3", [P, KD, B])
        wr3 = sb("wr3", [P, KD])
        wr3b = sb("wr3b", [P, KD, P])
        before = GB[:, 0:1024].bitcast(F16).rearrange("p (s c) -> p s c", s=NSUB)
        beats = GB[:, 1024:3072].bitcast(F16).rearrange("p (n s c) -> p n s c", n=2, s=NSUB)
        srow = GB[:, 3072:3584]
        th3 = GB[:, 3584:4096]
        mask3 = GB[:, 4096:4608]
        gate3 = GB[:, 4608:5120]
        o3 = GB[:, 5120:7168].rearrange("p (n k c) -> p n k c", n=2, k=KD)
        otok = GB[:, 7168:8192].rearrange("p (s d) -> p s d", s=NSUB)
        scol = sb("scol", [P, NSUB])
        smask = WB[:, 5120:5632].rearrange("p (s c) -> p s c", s=NSUB)
        ones16 = sb("ones16", [P, P], F16)
        gdram = [nc.dram_tensor(f"gates{i}", [E, NTOK], F32, kind="Internal").ap() for i in range(3)]
        unscale = sb("unscale", [P, STEPS // 2, KD, B])
        hist = sb("hist", [P, STEPS, KD * B])
        entry = sb("entry", [P, KD * B])
        entry_s = sb("entry_s", [P, KD * B])
        hpart = sb("hpart", [P, 2, KD * B], F16)
        rhpart = sb("rhpart", [P, 2, KD * B], F16)
        rfull = sb("rfull", [P, KD * B])
        gate_r = sb("gate_r", [P, KD * B])
        gate_z = sb("gate_z", [P, KD * B])
        cand = sb("cand", [P, KD * B])
        keep = sb("keep", [P, KD * B])
        keep_h = sb("keep_h", [P, KD * B])
        upd = sb("upd", [P, KD * B])

        const_ready = sem("const_ready")
        ident_zero = sem("ident_zero")
        cond_loaded = sem("cond_loaded")
        x_loaded = [sem(f"x_loaded{i}") for i in range(2)]
        x_stage_free = sem("x_stage_free")
        xT_psum = [sem(f"xT_psum{k}") for k in range(KD)]
        xT_copied = [sem(f"xT_copied{k}") for k in range(KD)]
        gru_w_loaded = sem("gru_w_loaded")
        gru_b_loaded = sem("gru_b_loaded")
        wsplit = sem("wsplit")
        condT_psum = sem("condT_psum")
        condT_ready = sem("condT_ready")
        r_psum, z_psum, c_psum, p_psum = (sem(f"{n}_psum") for n in "rzcp")
        r_ready, z_ready, c_ready, p_ready = (sem(f"{n}_ready") for n in "rzcp")
        rh_part, rh_full = sem("rh_part"), sem("rh_full")
        h_part, h_full = sem("h_part"), sem("h_full")
        e_part, e_full = sem("e_part"), sem("e_full")
        keep_ready, keep_h_ready, upd_ready = sem("keep_ready"), sem("keep_h_ready"), sem("upd_ready")
        hist_copied = sem("hist_copied")
        dbg_done = sem("dbg_done")
        vc, ac = sem("vector_link"), sem("scalar_link")
        prefer_ready = sem("prefer_ready")
        rw_loaded = sem("rw_loaded")
        rw_ready = sem("rw_ready")
        rcol_psum = sem("rcol_psum")
        rcol_ready = sem("rcol_ready")
        cent_psum = sem("cent_psum")
        logit_psum, logitT_ready, logit_turned = sem("logit_psum"), sem("logitT_ready"), sem("logit_turned")
        sq_ready = sem("sq_ready")
        gates_ready, gT_psum, gT_ready, gates_stored = (sem(n) for n in ("gates_ready", "gT_psum", "gT_ready", "gates_stored"))
        w0_loaded = [sem(f"w0_loaded{i}") for i in range(2)]
        g_loaded = [sem(f"g_loaded{i}") for i in range(2)]
        ffn = [{n: sem(f"ffn{i}_{n}") for n in ("up_psum", "act_hid", "hid_ready", "hid_used", "out_free", "out_done")}
               for i in range(4)]
        w1_loaded, w1f_loaded, w2_loaded, w3_loaded = (sem(n) for n in ("w1_loaded", "w1f_loaded", "w2_loaded", "w3_loaded"))
        wsh_ready = sem("wsh_ready")
        p2_psum, ssm_taken, conv_ready = sem("p2_psum"), [sem(f"ssm_taken{i}") for i in range(3)], sem("conv_ready")
        softplus_log, ssm_y, y_psum, z_ready2 = sem("softplus_log"), sem("ssm_y"), sem("y_psum"), sem("z_ready2")
        param_log = sem("param_log")
        uT_psum, uT_ready = sem("uT_psum"), sem("uT_ready")
        gate2_psum, gate2_ready, cell_ready = sem("gate2_psum"), sem("gate2_ready"), sem("cell_ready")
        cpart_psum, cpart_ready = sem("cpart_psum"), sem("cpart_ready")
        o2_psum, o2_sum, o2_tanh, o2_added = (sem(n) for n in ("o2_psum", "o2_sum", "o2_tanh", "o2_added"))
        d3_psum, d3_recip, d3_ready = sem("d3_psum"), sem("d3_recip"), sem("d3_ready")
        xs3_ready, c3_psum, c3_ready = sem("xs3_ready"), sem("c3_psum"), sem("c3_ready")
        s3_psum, s3_row, s3_th, beats_ready, rank_psum, rank_taken = (
            sem(n) for n in ("s3_psum", "s3_row", "s3_th", "beats_ready", "rank_psum", "rank_taken"))
        o3_ready, o3_psum, otok_ready, stored = (sem(n) for n in ("o3_ready", "o3_psum", "otok_ready", "stored"))
        before_ready = sem("before_ready")
        exp_in, exp_done = sem("exp_in"), sem("exp_done")
        cent_sum, cent_root, cent_ready = sem("cent_sum"), sem("cent_root"), sem("cent_ready")
        norm_sum, norm_root = sem("norm_sum"), sem("norm_root")
        silu_half = sem("silu_half")
        conv_step = [sem(f"conv_step{k}") for k in range(KD)]
        cell_init, cell_step = sem("cell_init"), sem("cell_step")
        d3_in, own, mask_ready, o3_part = sem("d3_in"), sem("own"), sem("mask_ready"), sem("o3_part")
        w2s_loaded, uraw_loaded = sem("w2s_loaded"), sem("uraw_loaded")

        NU1 = 2 * FS + E * FE
        G1 = 16 * E // 2
        G2 = G1 + 16 * NTILE // 2
        LAG = 2
        STAGES = ["gru", "L0", "L1c", "L1", "L2c", "L2", "L3c", "L3"]

        def upto(stage):
            return stop is None or STAGES.index(stage) <= STAGES.index(stop)

        def cols(j, n=TILE):
            return bass.ds(j * TILE, n)

        class Link:

            def __init__(self, eng, link_sem):
                self.eng, self.sem, self.n = eng, link_sem, 0

            def __call__(self, ins):
                ins.then_inc(self.sem, 1)
                self.n += 1
                self.eng.wait_ge(self.sem, self.n)

        NSPLIT = 4 * 3 + 4

        block = ctx.enter_context(nc.Block())

        @block.sync
        def _(sp):
            xrows = t["x"].rearrange("b (s p) d -> p b s d", p=P)
            for i in range(2):
                sp.dma_start(xstage[:, i], xrows[:, i]).then_inc(x_loaded[i], 16)
            sp.dma_start(condrow[:], t["cond_1024"]).then_inc(cond_loaded, 16)
            for g, n in enumerate(("Wr", "Wz", "Wh")):
                w = t["L0_cond_" + n].rearrange("(k p) m -> p k m", p=P)
                sp.dma_start(wx[:, g], w[:, 0:KD]).then_inc(gru_w_loaded, 16)
                sp.dma_start(wraw[:, g], w[:, KD:]).then_inc(gru_w_loaded, 16)
            sp.dma_start(wraw[:, 3], t["L0_cond_Wp"].rearrange("(k p) m -> p k m", p=P)).then_inc(gru_w_loaded, 16)
            for g, n in enumerate(("br", "bz", "bh", "bp")):
                sp.dma_start(gbias[0:1, g], t["L0_cond_" + n].rearrange("(a m) -> a m", a=1)).then_inc(gru_b_loaded, 16)
            with sp.Fori(1, B // 2) as j2:
                for i in range(2):
                    sp.wait_ge(x_stage_free, j2 * 2 + i - 1)
                    sp.dma_start(xstage[:, i], xrows[:, bass.ds(j2 * 2 + i, 1)]).then_inc(x_loaded[i], 16)

            def column(dst, src):
                return sp.dma_start(dst, src, allow_slow_non_contiguous=True)

            def load_expert(i, e):
                one = bass.ds(e, 1)
                sp.dma_start(w0_up[i], t["L0_ffn_w1"].rearrange("e (k p) f -> p e k f", p=P)[:, one]).then_inc(w0_loaded[i], 16)
                sp.dma_start(w0_down[i], t["L0_ffn_w2"].rearrange("e (f p) d -> p e f d", p=P)[:, one]).then_inc(w0_loaded[i], 16)
                column(b0_up[:, i], t["L0_ffn_b1"].rearrange("e (f p) -> p e f", p=P)[:, one]).then_inc(w0_loaded[i], 16)
                column(b0_down[:, i], t["L0_ffn_b2"].rearrange("e (k p) -> p e k", p=P)[:, one]).then_inc(w0_loaded[i], 16)

            for i in range(2):
                load_expert(i, i)
            sp.dma_start(rw[:, 0, :, 0:E], t["L0_ffn_gate_w"].rearrange("(k p) e -> p k e", p=P)).then_inc(rw_loaded, 16)
            column(rbias0[:], t["L0_ffn_gate_b"].rearrange("(e a) -> e a", a=1)).then_inc(rw_loaded, 16)
            r1 = t["L1_cond_router_W"].rearrange("(h k p) e -> p h k e", p=P, h=2)
            sp.dma_start(rw[:, 1, :, 0:E], r1[:, 0]).then_inc(rw_loaded, 16)
            sp.dma_start(rcond[:], r1[:, 1]).then_inc(rw_loaded, 16)
            sp.dma_start(rbias1[:], t["L1_cond_router_bias"].rearrange("(a e) -> a e", a=1).partition_broadcast(P)).then_inc(rw_loaded, 16)
            sp.dma_start(cent[:], t["L1_ffn_centroids"]).then_inc(rw_loaded, 16)
            sp.dma_start(route[:], t["L1_ffn_w_route"]).then_inc(rw_loaded, 16)
            column(v1b[:], t["L1_ffn_b1"].rearrange("e p -> p e")).then_inc(rw_loaded, 16)
            sp.dma_start(v2b[:], t["L1_ffn_b2"]).then_inc(rw_loaded, 16)
            halves = lambda name: t[name].rearrange("(k p) -> p k", p=P)
            col = lambda name, a, n: t[name].rearrange("(p a) -> p a", a=1)[a:a + n]
            column(cb2[:], halves("L2_cond_conv_b")).then_inc(w2s_loaded, 16)
            column(bo2[:], halves("L2_cond_bo")).then_inc(w2s_loaded, 16)
            for i, (name, a) in enumerate((("L2_cond_A_log", 0), ("L2_cond_dt_log", 0), ("L2_cond_bp", 0),
                                           ("L2_cond_bp", NS), ("L2_cond_bs", 0))):
                column(small2[:, i:i + 1], col(name, a, NS)).then_inc(w2s_loaded, 16)
            for g, name in enumerate(("bf", "bi", "bc", "bo")):
                column(gb2[:, g], halves("L2_ffn_" + name)).then_inc(w2s_loaded, 16)
            column(cinit[:], halves("L2_ffn_in_c")).then_inc(w2s_loaded, 16)
            column(b3_up[:], t["L3_ffn_b1"].rearrange("(f p) -> p f", p=P)).then_inc(w3_loaded, 16)
            column(b3_down[:], halves("L3_ffn_b2")).then_inc(w3_loaded, 16)
            column(wr3[:], halves("L3_ffn_w_router")).then_inc(w3_loaded, 16)

            def finish(src, waits):
                for sm, v in waits:
                    sp.wait_ge(sm, v)
                sp.dma_start(dbg, src).then_inc(dbg_done, 16)
                sp.wait_ge(dbg_done, 16)

            if stop == "gru":
                finish(HT[:], [(hist_copied, 2 * TURNS + 2)])
                return
            sp.wait_ge(p_psum, TURNS * STEPS // CHUNK)
            for dst, name in ((wsh1, "w1"), (wsh3, "w3"), (wsh2, "w2")):
                sp.dma_start(dst, t["L1_cond_" + name].rearrange("(k p) f -> p k f", p=P)).then_inc(w1_loaded, 16)
            sp.dma_start(w1e, t["L1_cond_W1e"].rearrange("e (k p) f -> p e k f", p=P)).then_inc(w1_loaded, 16)
            sp.dma_start(w2e, t["L1_cond_W2e"].rearrange("e (f p) d -> p e f d", p=P)).then_inc(w1_loaded, 16)

            def store_gates(l):
                sp.wait_ge(gT_ready, 2 * (l + 1))
                rows = gdram[l].rearrange("e (g q c) -> q e g c", q=NSUB, c=P)
                for q in range(NSUB):
                    sp.dma_start(rows[q], gT[q * E:(q + 1) * E]).then_inc(gates_stored, 16)
                sp.wait_ge(gates_stored, 16 * NSUB * (l + 1))

            def load_gates0(i, e):
                sp.dma_start(g0[:, i], gdram[0][bass.ds(e, 1)].partition_broadcast(P)).then_inc(g_loaded[i], 16)

            def load_gates(l, i, j):
                src = gdram[l][:, cols(j)]
                sp.dma_start(g1[:, i], src.partition_broadcast(P)).then_inc(g_loaded[i], 16)
                if l == 2:
                    sp.dma_start(g1T[:, i], src).then_inc(g_loaded[i], 16)

            store_gates(0)
            for i in range(2):
                load_gates0(i, i)
            with sp.Fori(1, E // 2) as e2:
                for i in range(2):
                    sp.wait_ge(ffn[0]["out_done"], (e2 * 2 + i - 1) * NTILE)
                    load_expert(i, e2 * 2 + i)
                    load_gates0(i, e2 * 2 + i)
            sp.wait_ge(ffn[0]["out_done"], E * NTILE)
            if stop == "L0":
                return finish(XT[:], [])
            sp.dma_start(v1, t["L1_ffn_w1"].rearrange("e (k p) f -> p e k f", p=P)).then_inc(w1f_loaded, 16)
            sp.dma_start(v2, t["L1_ffn_w2"].rearrange("e p d -> p e d")).then_inc(w1f_loaded, 16)
            for g, name in enumerate(("wf", "wi", "wc", "wo", "uf", "ui", "uc", "uo")):
                sp.dma_start(uraw[:, g], t["L2_ffn_" + name].rearrange("(k p) m -> p k m", p=P)).then_inc(uraw_loaded, 16)
            for l, f in ((1, 1), (2, 2)):
                store_gates(l)
                for i in range(2):
                    load_gates(l, i, i)
                with sp.Fori(1, NTILE // 2) as j2:
                    for i in range(2):
                        sp.wait_ge(ffn[f]["out_done"], j2 * 2 + i - 1)
                        load_gates(l, i, j2 * 2 + i)
                sp.wait_ge(ffn[f]["out_done"], NTILE)
                if l == 1:
                    if stop == "L1c":
                        return finish(HT[:], [])
                    sp.dma_start(w3_up, t["L3_ffn_W1"].rearrange("(k p) f -> p k f", p=P)).then_inc(w3_loaded, 16)
                    sp.dma_start(w3_down, t["L3_ffn_W2"].rearrange("(f p) d -> p f d", p=P)).then_inc(w3_loaded, 16)
                    sp.dma_start(w3c, t["L3_cond_weight"].rearrange("(k p) d -> p k d", p=P)).then_inc(w3_loaded, 16)
                    sp.dma_start(wp2, t["L2_cond_Wp"].rearrange("(k p) d -> p k d", p=P)).then_inc(w2_loaded, 16)
                    sp.dma_start(ws2, t["L2_cond_Ws"].rearrange("(k p) d -> p k d", p=P)).then_inc(w2_loaded, 16)
                    sp.dma_start(wo2, t["L2_cond_Wo"]).then_inc(w2_loaded, 16)
            if stop == "L1":
                return finish(XT[:], [])
            if stop == "L2c":
                return finish(HT[:], [(z_ready2, 2 * B)])
            if stop == "L2":
                return finish(XT[:], [(o2_added, 2 * B + 4)])
            if stop == "L3c":
                return finish(HT[:], [(c3_ready, 2 * B + 2)])
            sp.sem_inc(stored, 32)
            orows = out.rearrange("b (s p) d -> p b s d", p=P)
            with sp.Fori(0, B) as j:
                sp.wait_ge(otok_ready, j * 2 + 6)
                sp.dma_start(orows[:, bass.ds(j, 1)], otok).then_inc(stored, 16)
            sp.wait_ge(stored, B * 16 + 32)

        @block.gpsimd
        def _(pool):
            nc.gpsimd.memset(ident[:], 0.0).then_inc(ident_zero, 1)
            nc.gpsimd.memset(ones[:], 1.0).then_inc(const_ready, 1)
            for e in range(E):
                nc.gpsimd.memset(prefer[:, e:e + 1], float(E - e)).then_inc(prefer_ready, 1)
            nc.gpsimd.memset(unscale[:], 1.0 / HSCALE).then_inc(prefer_ready, 1)
            nc.gpsimd.memset(rw[:, 2], 0.0).then_inc(prefer_ready, 1)
            nc.gpsimd.memset(rsq[:], 0.0).then_inc(prefer_ready, 1)
            nc.gpsimd.memset(ones16[:], 1.0).then_inc(prefer_ready, 1)
            pool.wait_ge(prefer_ready, E + 4)
            nc.gpsimd.memset(rsq[:, :, RL - 1:RL], 1.0).then_inc(prefer_ready, 1)
            pool.wait_ge(ident_zero, 1)
            nc.gpsimd.affine_select(out=ident[:], in_=ident[:], compare_op=ALU.not_equal, fill=1.0, base=0,
                                    pattern=[[-1, P]], channel_multiplier=1).then_inc(const_ready, 1)
            pool.sem_inc(hist_copied, 2)
            hview = HT[:].rearrange("p k (b t) -> p t k b", b=B)
            with pool.Fori(0, TURNS) as it:
                for half in range(2):
                    n = STEPS // 2
                    pool.wait_ge(h_full, it * STEPS + (half + 1) * n)
                    nc.gpsimd.tensor_tensor(hview[:, bass.ds(it * STEPS + half * n, n)],
                                            hist[:, half * n:(half + 1) * n].rearrange("p s (k b) -> p s k b", k=KD),
                                            unscale[:], ALU.mult).then_inc(hist_copied, 1)
            if upto("L2"):
                pool.sem_inc(o2_added, 4)
                with pool.Fori(0, NTILE // 2) as j2:
                    for i in range(2):
                        for m in range(KD):
                            n = j2 * 4 + i * 2 + m
                            pool.wait_ge(o2_tanh, n + 1)
                            x_t = XT[:, m, cols(j2 * 2 + i)]
                            nc.gpsimd.tensor_tensor(x_t, x_t, y2[:, i, m], ALU.add).then_inc(o2_added, 1)
            if upto("L3"):
                pool.wait_ge(o2_added, 2 * B + 4)
                nc.gpsimd.memset(before[:], 1.0).then_inc(before_ready, 1)
                nc.gpsimd.memset(o3[:, 1], 0.0).then_inc(before_ready, 1)
                pool.wait_ge(before_ready, 2)
                nc.gpsimd.affine_select(out=before, in_=before, compare_op=ALU.is_gt, fill=0.0, base=0,
                                        pattern=[[-P, NSUB], [1, TILE]], channel_multiplier=-1).then_inc(before_ready, 1)

        @block.scalar
        def _(act):
            act.sem_inc(xT_copied[1], 1)
            xv = XT[:]
            with act.Fori(0, B) as j:
                act.wait_ge(xT_psum[1], j + 1)
                nc.scalar.copy(xv[:, 1, bass.ds(j * T, T)], banks[5][:]).then_inc(xT_copied[1], 1)
            bank = {"r": banks[0], "z": banks[1], "c": banks[2]}

            def gate_in(b, s):
                return b[:, 0:2 * STEPS * B].rearrange("p (m c) -> p m c", m=KD)[:, :, s * B:(s + 1) * B]

            def flat(x):
                return x[:].rearrange("p (k b) -> p k b", k=KD)

            with act.Fori(0, TURNS) as it:
                for s in range(STEPS):
                    n = it * STEPS + s + 1
                    act.wait_ge(r_psum, n)
                    nc.scalar.activation(flat(gate_r), gate_in(bank["r"], s), ACT.Tanh, scale=0.5 / GSCALE).then_inc(r_ready, 1)
                    act.wait_ge(z_psum, n)
                    nc.scalar.activation(flat(gate_z), gate_in(bank["z"], s), ACT.Tanh, scale=0.5 / GSCALE).then_inc(z_ready, 1)
                    act.wait_ge(c_psum, n)
                    nc.scalar.activation(flat(cand), gate_in(bank["c"], s), ACT.Tanh, scale=1.0 / GSCALE).then_inc(c_ready, 1)
                    if (s + 1) % CHUNK == 0:
                        q = s // CHUNK
                        act.wait_ge(p_psum, it * (STEPS // CHUNK) + q + 1)
                        pin = banks[3][:, 0:KD * (STEPS // CHUNK) * B].rearrange("p (m c) -> p m c", m=KD)
                        nc.scalar.activation(flat(entry), pin[:, :, q * B:(q + 1) * B], ACT.Tanh, scale=1.0 / GSCALE).then_inc(p_ready, 1)

            if not upto("L0"):
                return
            link = Link(act, ac)

            def routing_copies(l, first, square=None):
                for g in range(NTILE):
                    act.wait_ge(logit_psum, first + g + 1)
                    if square and g + 4 < NTILE:
                        square(g + 4)
                    if g >= 2:
                        act.wait_ge(logit_turned, first + g - 1)
                    n = RL if l == 2 else E
                    dst, src = logitT[0:n, g % 2], banks[6 + g % 2][0:n]
                    if l == 0:
                        i = nc.scalar.activation(dst, src, ACT.Identity, bias=rbias0[:])
                    elif l == 1:
                        i = nc.scalar.activation(dst, src, ACT.Sigmoid, bias=rcol[:, g:g + 1])
                    else:
                        i = nc.scalar.activation(dst, src, ACT.Identity)
                    i.then_inc(logitT_ready, 1)

            def gates_copy(l):
                for h in range(2):
                    act.wait_ge(gT_psum, 2 * l + h + 1)
                    nc.scalar.copy(gT[:, h * 4:h * 4 + 4], banks[6 + h][0:NSUB * E].rearrange("p (g c) -> p g c", c=P)
                                   ).then_inc(gT_ready, 1)

            def hidden(S, n, count, func, bias, done):
                act.wait_ge(S["up_psum"], count + 1)
                act.wait_ge(S["hid_used"], count + 1)
                nc.scalar.activation(hid[:, n], banks[n][:], func, bias=bias).then_inc(S[done], 1)

            act.wait_ge(rw_loaded, 9 * 16)
            routing_copies(0, 0)
            act.wait_ge(exp_in, 1)
            nc.scalar.activation(r_y, r_x, ACT.Exp).then_inc(exp_done, 1)
            gates_copy(0)
            act.sem_inc(ffn[0]["hid_ready"], RING)
            act.wait_ge(gates_stored, 16 * NSUB)
            with act.Fori(0, E // 2) as e2:
                for i in range(2):
                    with act.Fori(0, NTILE) as j:
                        act.wait_ge(w0_loaded[i], e2 * 64 + 64)
                        for f in range(F0):
                            hidden(ffn[0], f % RING, ((e2 * 2 + i) * NTILE + j) * F0 + f, ACT.Gelu,
                                   b0_up[:, i, f:f + 1], "hid_ready")
            if not upto("L1c"):
                return
            act.wait_ge(cent_sum, 1)
            nc.scalar.activation(cent_n[:, 1:2], cent_n[:, 0:1], ACT.Sqrt).then_inc(cent_root, 1)
            act.wait_ge(rcol_ready, 1)
            act.wait_ge(ffn[0]["out_done"], E * NTILE)
            routing_copies(1, NTILE)
            gates_copy(1)
            act.wait_ge(gates_stored, 2 * 16 * NSUB)
            with act.Fori(0, NTILE) as j:
                for f in range(FS):
                    act.wait_ge(ffn[1]["up_psum"], j * NU1 + 2 * f + 1)
                    act.wait_ge(ffn[1]["hid_used"], j * N1C + f + 1)
                    nc.scalar.activation(hid[:, f % RING], banks[2 * f % RING][:], ACT.Tanh, scale=0.5).then_inc(ffn[1]["act_hid"], 1)
                for f in range(FS, N1C):
                    act.wait_ge(ffn[1]["up_psum"], j * NU1 + FS + f + 1)
                    act.wait_ge(ffn[1]["hid_used"], j * N1C + f + 1)
                    nc.scalar.activation(hid[:, f % RING], banks[f % RING][:], ACT.Gelu).then_inc(ffn[1]["act_hid"], 1)
            if not upto("L1"):
                return
            act.wait_ge(ffn[1]["out_done"], NTILE)
            sqt = WB[:, 5760:9856].rearrange("p (n k c) -> p n k c", n=4, k=KD)

            def square(g):
                for k in range(KD):
                    i = nc.scalar.activation(sqt[:, g % 4, k], HT[:, k, g * TILE:(g + 1) * TILE], ACT.Square)
                i.then_inc(sq_ready, 1)

            for g in range(4):
                square(g)
            routing_copies(2, 2 * NTILE, square)
            act.wait_ge(norm_sum, 1)
            nc.scalar.activation(r_y, r_x, ACT.Sqrt).then_inc(norm_root, 1)
            act.wait_ge(exp_in, 2)
            nc.scalar.activation(r_eq, r_sel, ACT.Exp).then_inc(exp_done, 1)
            gates_copy(2)
            act.wait_ge(gates_stored, 3 * 16 * NSUB)
            with act.Fori(0, NTILE) as j:
                for f in range(E):
                    hidden(ffn[2], f % RING, j * E + f, ACT.Gelu, v1b[:, f:f + 1], "act_hid")
            if not upto("L2c"):
                return
            act.wait_ge(w2s_loaded, 12 * 16)
            link(nc.scalar.activation(small2[:, 5:7], small2[:, 0:2], ACT.Abs))
            link(nc.scalar.activation(small2[:, 5:7], small2[:, 5:7], ACT.Exp, scale=-1.0))
            nc.scalar.activation(small2[:, 5:7], small2[:, 5:7], ACT.Ln, bias=1.0).then_inc(param_log, 1)
            act.sem_inc(ssm_taken[1], 1)
            with act.Fori(0, B) as j:
                act.wait_ge(p2_psum, j * 3 + 2 + 6)
                nc.scalar.activation(ssm_c[:, cols(j)], banks[1][0:NS], ACT.Tanh, bias=small2[:, 3:4]).then_inc(ssm_taken[1], 1)
            act.wait_ge(ssm_taken[0], B + 1)
            link(nc.scalar.activation(ssm[:], ssm_b[:], ACT.Abs))
            link(nc.scalar.activation(ssm[:], ssm[:], ACT.Exp, scale=-1.0))
            nc.scalar.activation(ssm[:], ssm[:], ACT.Ln, bias=1.0).then_inc(softplus_log, 1)
            for j in range(B):
                for m in range(KD):
                    n = j * KD + m
                    act.wait_ge(y_psum, n + 1)
                    nc.scalar.activation(HT[:, m, j * TILE:(j + 1) * TILE], banks[n % 4][:], ACT.Identity,
                                         bias=bo2[:, m:m + 1]).then_inc(z_ready2, 1)
            if not upto("L2"):
                return
            act.wait_ge(cell_ready, 2)
            act.sem_inc(gate2_ready, 6)
            with act.Fori(0, B) as j:
                for h in range(2):
                    for g in range(3):
                        act.wait_ge(gate2_psum, j * 6 + h * 3 + g + 1)
                        for m in range(KD):
                            i = nc.scalar.activation(lstm[:, h, g, m], banks[h * 3 + g][:, m * 256:(m + 1) * 256], ACT.Tanh,
                                                     scale=0.5 if g < 2 else 1.0, bias=gb2[:, g, m:m + 1])
                        i.then_inc(gate2_ready, 1)
            for m in range(KD):
                act.wait_ge(cpart_psum, m + 1)
                nc.scalar.activation(cpart[:, m], banks[6 + m][:], ACT.Identity, bias=gb2[:, 3, m:m + 1]).then_inc(cpart_ready, 1)
            with act.Fori(0, B // 2) as j2:
                for i in range(2):
                    for m in range(KD):
                        act.wait_ge(o2_sum, j2 * 4 + i * 2 + m + 1 + 4)
                        nc.scalar.activation(y2[:, i, m], y2[:, i, m], ACT.Tanh).then_inc(o2_tanh, 1)
            if not upto("L3c"):
                return
            act.wait_ge(d3_recip, 1)
            nc.scalar.activation(d3[:], d3[:], ACT.Sqrt).then_inc(d3_ready, 1)
            act.wait_ge(d3_ready, 1)
            act.sem_inc(c3_ready, 2)
            with act.Fori(0, B) as j:
                for m in range(KD):
                    act.wait_ge(c3_psum, j * 2 + m + 1 + 4)
                    nc.scalar.activation(HT[:, m, cols(j)], banks[m][:], ACT.Identity, scale=d3[:, m, bass.ds(j, 1)]).then_inc(c3_ready, 1)
            if not upto("L3"):
                return
            S = ffn[3]
            act.sem_inc(S["hid_ready"], RING)
            act.sem_inc(otok_ready, 2)
            with act.Fori(0, B) as j:
                act.wait_ge(s3_psum, j + 1)
                act.wait_ge(rank_taken, j + 1)
                nc.scalar.copy(srow, banks[6][:]).then_inc(s3_row, 1)
                act.wait_ge(s3_row, j + 1)
                nc.scalar.activation(th3, srow, ACT.Tanh, scale=0.5).then_inc(s3_th, 1)
                for f in range(F3):
                    hidden(S, f % RING, j * F3 + f, ACT.Gelu_apprx_tanh, b3_up[:, f:f + 1], "hid_ready")
                for h in range(2):
                    act.wait_ge(o3_psum, j * 2 + h + 3)
                    if h == 0:
                        act.wait_ge(stored, j * 16 + 16)
                    nc.scalar.copy(otok[:, 2 * h:2 * h + 2], banks[6][:].rearrange("p (s d) -> p s d", s=2)).then_inc(otok_ready, 1)
            for h in range(2):
                act.wait_ge(o3_psum, B * 2 + h + 3)
                if h == 0:
                    act.wait_ge(stored, B * 16 + 16)
                nc.scalar.copy(otok[:, 2 * h:2 * h + 2], banks[6][:].rearrange("p (s d) -> p s d", s=2)).then_inc(otok_ready, 1)

        @block.vector
        def _(dve):
            dve.sem_inc(xT_copied[0], 1)
            with dve.Fori(0, B) as j:
                dve.wait_ge(xT_psum[0], j + 1)
                nc.vector.tensor_copy(XT[:, 0, bass.ds(j * T, T)], banks[4][:]).then_inc(xT_copied[0], 1)
            dve.wait_ge(gru_w_loaded, 7 * 16)
            done = 0
            for g in range(4):
                nc.vector.tensor_scalar(wraw[:, g], wraw[:, g], WSCALE / (2 if g == 2 else 1), None, ALU.mult).then_inc(wsplit, 1)
                done += 1
                dve.wait_ge(wsplit, done)
                nc.vector.tensor_copy(wpart[:, g, 0], wraw[:, g]).then_inc(wsplit, 1)
                done += 1
                dve.wait_ge(wsplit, done)
                nc.vector.tensor_tensor(wpart[:, g, 1], wraw[:, g], wpart[:, g, 0], ALU.subtract).then_inc(wsplit, 1)
                done += 1
            for g in range(3):
                nc.vector.tensor_scalar(wx[:, g], wx[:, g], GSCALE, None, ALU.mult).then_inc(wsplit, 1)
            dve.wait_ge(gru_b_loaded, 4 * 16)
            nc.vector.tensor_scalar(gbias[:], gbias[:], GSCALE, None, ALU.mult).then_inc(wsplit, 1)
            dve.wait_ge(condT_psum, 1)
            nc.vector.tensor_copy(condT[:].rearrange("p k b -> p (k b)"), banks[6][:, 0:KD * B]).then_inc(condT_ready, 1)
            nc.vector.tensor_copy(entry[:], banks[6][:, 0:KD * B]).then_inc(p_ready, 1)

            def split_entry(n):
                dve.wait_ge(p_ready, n)
                nc.vector.tensor_scalar(hpart[:, 0], entry[:], HSCALE, None, ALU.mult).then_inc(e_part, 1)
                nc.vector.tensor_scalar(entry_s[:], entry[:], HSCALE, None, ALU.mult).then_inc(e_full, 1)
                dve.wait_ge(e_full, n)
                nc.vector.tensor_tensor(hpart[:, 1], entry_s[:], hpart[:, 0], ALU.subtract).then_inc(e_part, 1)

            NP = STEPS // CHUNK
            split_entry(1)
            with dve.Fori(0, TURNS) as it:
                for s in range(STEPS):
                    n = it * STEPS + s
                    h = entry_s[:] if s % CHUNK == 0 else hist[:, s - 1]
                    dve.wait_ge(r_ready, n + 1)
                    nc.vector.scalar_tensor_tensor(rhpart[:, 0], gate_r[:], 1.0, h, ALU.add, ALU.mult).then_inc(rh_part, 1)
                    nc.vector.scalar_tensor_tensor(rfull[:], gate_r[:], 1.0, h, ALU.add, ALU.mult).then_inc(rh_full, 1)
                    dve.wait_ge(rh_full, n + 1)
                    nc.vector.tensor_tensor(rhpart[:, 1], rfull[:], rhpart[:, 0], ALU.subtract).then_inc(rh_part, 1)
                    dve.wait_ge(z_ready, n + 1)
                    nc.vector.tensor_scalar(keep[:], gate_z[:], -0.5, 0.5, ALU.mult, ALU.add).then_inc(keep_ready, 1)
                    dve.wait_ge(keep_ready, n + 1)
                    nc.vector.tensor_tensor(keep_h[:], keep[:], h, ALU.mult).then_inc(keep_h_ready, 1)
                    if s % (STEPS // 2) == 0:
                        dve.wait_ge(hist_copied, it * 2 + 1 + s // (STEPS // 2))
                    dve.wait_ge(c_ready, n + 1)
                    nc.vector.scalar_tensor_tensor(upd[:], gate_z[:], 1.0, cand[:], ALU.add, ALU.mult).then_inc(upd_ready, 1)
                    dve.wait_ge(upd_ready, n + 1)
                    nc.vector.scalar_tensor_tensor(hpart[:, 0], upd[:], 0.5 * HSCALE, keep_h[:], ALU.mult, ALU.add).then_inc(h_part, 1)
                    nc.vector.scalar_tensor_tensor(hist[:, s], upd[:], 0.5 * HSCALE, keep_h[:], ALU.mult, ALU.add).then_inc(h_full, 1)
                    dve.wait_ge(h_full, n + 1)
                    nc.vector.tensor_tensor(hpart[:, 1], hist[:, s], hpart[:, 0], ALU.subtract).then_inc(h_part, 1)
                    if (s + 1) % CHUNK == 0:
                        split_entry(it * NP + (s // CHUNK + 2))

            if not upto("L0"):
                return
            link = Link(dve, vc)
            V = nc.vector
            wide = lambda x: x.to_broadcast([P, NBLK, E])
            pref = prefer[:].rearrange("p (a e) -> p a e", a=1).to_broadcast([P, NBLK, E])

            def top2(x):
                for m, p, mask in ((r_m1, r_p1, r_mask1), (r_m2, r_p2, r_mask2)):
                    link(V.tensor_reduce(m, x, AX_X, ALU.max))
                    link(V.tensor_tensor(r_eq, x, wide(m), ALU.is_equal))
                    link(V.tensor_tensor(r_tmp, r_eq, pref, ALU.mult))
                    link(V.tensor_reduce(p, r_tmp, AX_X, ALU.max))
                    link(V.tensor_tensor(mask, r_tmp, wide(p), ALU.is_equal))
                    if m is r_m1:
                        link(V.scalar_tensor_tensor(r_sel, mask, FAR, x, ALU.mult, ALU.add))
                        x = r_sel

            def take_logits(l, dst, n):
                dve.wait_ge(logit_turned, (l + 1) * NTILE)
                half = NBLK // 2
                for h, bank in ((0, banks[5]), (1, banks[4])):
                    link(V.tensor_copy(dst[:, h * half:(h + 1) * half], bank[:, 0:half * n].rearrange("p (b n) -> p b n", n=n)))

            dve.wait_ge(prefer_ready, E + 5)
            take_logits(0, r_log, E)
            top2(r_log)
            V.tensor_tensor(r_x, r_m2, r_m1, ALU.subtract).then_inc(exp_in, 1)
            dve.wait_ge(exp_done, 1)
            link(V.tensor_scalar(r_z, r_y, 1.0, None, ALU.add))
            link(V.reciprocal(r_x, r_z))
            link(V.tensor_tensor(r_z, r_x, r_y, ALU.mult))
            link(V.tensor_tensor(r_w, r_mask1, wide(r_x), ALU.mult))
            link(V.tensor_tensor(r_tmp, r_mask2, wide(r_z), ALU.mult))
            V.tensor_tensor(r_w, r_w, r_tmp, ALU.add).then_inc(gates_ready, 1)

            S = ffn[0]
            dve.sem_inc(S["out_free"], 1)
            with dve.Fori(0, E // 2) as e2:
                for i in range(2):
                    with dve.Fori(0, NTILE) as j:
                        dve.wait_ge(w0_loaded[i], e2 * 64 + 64)
                        dve.wait_ge(g_loaded[i], e2 * 16 + 16)
                        n = (e2 * 2 + i) * NTILE + j
                        dve.wait_ge(S["hid_used"], n * F0 + F0 + RING)
                        for m in range(KD):
                            ins = V.scalar_tensor_tensor(outt[:, m], banks[4 + m][:], b0_down[:, i, m:m + 1], g0[:, i, cols(j)],
                                                         ALU.add, ALU.mult)
                        ins.then_inc(S["out_free"], 1)
                        dve.wait_ge(S["out_free"], n + 2)
                        x_t = XT[:, :, cols(j)]
                        V.tensor_tensor(x_t, x_t, outt[:], ALU.add).then_inc(S["out_done"], 1)
                        dve.wait_ge(S["out_done"], n + 1)
            if not upto("L1c"):
                return
            link(V.tensor_tensor(cent_sq[:], cent[:], cent[:], ALU.mult))
            link(V.tensor_reduce(cent_n[:, 0:1], cent_sq[:], AX_X, ALU.add))
            V.tensor_copy(cent_n[:, 2:3], cent_n[:, 0:1]).then_inc(cent_sum, 1)
            dve.wait_ge(cent_root, 1)
            link(V.tensor_scalar(cent_n[:, 2:3], cent_n[:, 1:2], 1e-12, None, ALU.max))
            link(V.reciprocal(cent_n[:, 3:4], cent_n[:, 2:3]))
            V.tensor_scalar(cent[:], cent[:], cent_n[:, 3:4], None, ALU.mult).then_inc(cent_ready, 1)
            dve.wait_ge(cent_psum, 1)
            for k in range(KD):
                i = V.tensor_copy(rw[:, 2, k, 0:2 * E], banks[3][:, 64 + k * 2 * E:64 + (k + 1) * 2 * E])
            i.then_inc(rw_ready, 1)
            dve.wait_ge(rcol_psum, 1)
            V.tensor_copy(rcol[:], banks[3][0:E, 0:B]).then_inc(rcol_ready, 1)
            dve.wait_ge(w1_loaded, 5 * 16)
            V.tensor_scalar(wsh2, wsh2, 0.5, None, ALU.mult).then_inc(wsh_ready, 1)

            take_logits(1, r_log, E)
            bias = rbias1[:].rearrange("p (a e) -> p a e", a=1).to_broadcast([P, NBLK, E])
            link(V.tensor_tensor(r_w, r_log, bias, ALU.add))
            top2(r_w)
            link(V.tensor_tensor(r_mask1, r_mask1, r_mask2, ALU.add))
            link(V.tensor_tensor(r_sel, r_mask1, r_log, ALU.mult))
            link(V.tensor_reduce(r_x, r_sel, AX_X, ALU.add))
            link(V.tensor_scalar(r_y, r_x, 1e-9, None, ALU.is_gt))
            link(V.tensor_scalar(r_z, r_x, 1e-9, None, ALU.add))
            link(V.reciprocal(r_x, r_z))
            link(V.tensor_tensor(r_x, r_x, r_y, ALU.mult))
            link(V.tensor_scalar(r_y, r_y, -0.5, 0.5, ALU.mult, ALU.add))
            link(V.tensor_tensor(r_sel, r_sel, wide(r_x), ALU.mult))
            link(V.tensor_tensor(r_tmp, r_mask1, wide(r_y), ALU.mult))
            V.tensor_tensor(r_w, r_sel, r_tmp, ALU.add).then_inc(gates_ready, 1)

            S = ffn[1]
            dve.sem_inc(S["out_free"], 1)
            dve.sem_inc(S["hid_ready"], RING)
            with dve.Fori(0, NTILE // 2) as j2:
                for i in range(2):
                    j = j2 * 2 + i
                    for f in range(FS):
                        dve.wait_ge(S["act_hid"], j * N1C + f + 1)
                        V.scalar_tensor_tensor(hid[:, f % RING], hid[:, f % RING], 1.0, banks[2 * f % RING][:], ALU.add,
                                               ALU.mult).then_inc(silu_half, 1)
                        dve.wait_ge(silu_half, j * FS + f + 1)
                        dve.wait_ge(S["up_psum"], j * NU1 + 2 * f + 2)
                        V.tensor_tensor(hid[:, f % RING], hid[:, f % RING], banks[(2 * f + 1) % RING][:], ALU.mult
                                        ).then_inc(S["hid_ready"], 1)
                    dve.wait_ge(g_loaded[i], G1 + j2 * 16 + 16)
                    for f in range(FS, N1C):
                        dve.wait_ge(S["act_hid"], j * N1C + f + 1)
                        V.tensor_tensor(hid[:, f % RING], hid[:, f % RING], g1[:, i, (f - FS) // FE], ALU.mult
                                        ).then_inc(S["hid_ready"], 1)
                    dve.wait_ge(S["hid_used"], (j + 1) * N1C + RING)
                    for m in range(KD):
                        ins = V.tensor_scalar(HT[:, m, cols(j)], banks[4 + m][:], 1.0 / 3.0, None, ALU.mult)
                    ins.then_inc(S["out_free"], 1)
                    dve.wait_ge(S["out_free"], j + 2)
                    dve.sem_inc(S["out_done"], 1)
            if not upto("L1"):
                return
            take_logits(2, r_raw, RL)
            V.tensor_copy(r_x, r_raw[:, :, RL - 1:RL]).then_inc(norm_sum, 1)
            dve.wait_ge(norm_root, 1)
            link(V.tensor_scalar(r_z, r_y, 1e-12, None, ALU.max))
            link(V.reciprocal(r_x, r_z))
            link(V.tensor_tensor(r_tmp, r_raw[:, :, 0:E], wide(r_x), ALU.mult))
            link(V.tensor_tensor(r_log, r_tmp, r_raw[:, :, E:2 * E], ALU.add))
            top2(r_log)
            link(V.tensor_tensor(r_mask1, r_log, wide(r_m2), ALU.is_ge))
            V.tensor_tensor(r_sel, r_log, wide(r_m1), ALU.subtract).then_inc(exp_in, 1)
            dve.wait_ge(exp_done, 2)
            link(V.tensor_tensor(r_tmp, r_eq, r_mask1, ALU.mult))
            link(V.tensor_reduce(r_x, r_tmp, AX_X, ALU.add))
            link(V.reciprocal(r_y, r_x))
            V.tensor_tensor(r_w, r_tmp, wide(r_y), ALU.mult).then_inc(gates_ready, 1)

            S = ffn[2]
            dve.sem_inc(S["out_free"], 1)
            dve.sem_inc(S["hid_ready"], RING)
            with dve.Fori(0, NTILE // 2) as j2:
                for i in range(2):
                    j = j2 * 2 + i
                    dve.wait_ge(g_loaded[i], G2 + j2 * 32 + 32)
                    for f in range(E):
                        dve.wait_ge(S["act_hid"], j * E + f + 1)
                        V.tensor_tensor(hid[:, f % RING], hid[:, f % RING], g1[:, i, f], ALU.mult).then_inc(S["hid_ready"], 1)
                    dve.wait_ge(S["hid_used"], (j + 1) * E + RING)
                    for m in range(KD):
                        x_t = XT[:, m, cols(j)]
                        ins = V.tensor_tensor(x_t, x_t, banks[4 + m][:], ALU.add)
                    ins.then_inc(S["out_free"], 1)
                    dve.wait_ge(S["out_free"], j + 2)
                    dve.sem_inc(S["out_done"], 1)
            if not upto("L2c"):
                return
            dve.wait_ge(param_log, 1)
            link(V.tensor_scalar(small2[:, 7:9], small2[:, 0:2], 0.0, None, ALU.max))
            link(V.tensor_tensor(small2[:, 7:9], small2[:, 7:9], small2[:, 5:7], ALU.add))
            link(V.tensor_tensor(small2[:, 9:10], small2[:, 7:8], small2[:, 8:9], ALU.mult))
            link(V.tensor_scalar(small2[:, 10:11], small2[:, 9:10], -1.0, 1.0, ALU.mult, ALU.add))
            link(V.memset(decay[:], 1.0))
            link(V.tensor_scalar(decay[:], decay[:], small2[:, 10:11], None, ALU.mult))
            dt = small2[:, 8:9]
            dve.sem_inc(ssm_taken[0], 1)
            dve.sem_inc(ssm_taken[2], 1)
            with dve.Fori(0, B // 2) as j2:
                for i in range(2):
                    j = j2 * 2 + i
                    cv = hid[:, 2 * i:2 * i + 2]
                    dve.wait_ge(p2_psum, j * 3 + 2)
                    for tap in range(B):
                        order = B - 1 if tap == 0 else tap - 1
                        back = B - 1 - order
                        for k in range(KD):
                            w = condT[:, k, order:order + 1]
                            src = XT[:, k, cols(j, TILE - back)]
                            if tap == 0:
                                ins = V.tensor_scalar(cv[:, k], src, w, cb2[:, k:k + 1], ALU.mult, ALU.add)
                            else:
                                ins = V.scalar_tensor_tensor(cv[:, k, back:], src, w, cv[:, k, back:], ALU.mult, ALU.add)
                            ins.then_inc(conv_step[k], 1)
                        if tap < B - 1:
                            for k in range(KD):
                                dve.wait_ge(conv_step[k], j * B + tap + 1)
                    for k in range(KD):
                        dve.wait_ge(conv_step[k], j * B + B)
                    dve.sem_inc(conv_ready, 1)
                    dve.wait_ge(p2_psum, j * 3 + 1 + 6)
                    V.tensor_scalar(ssm_b[:, cols(j)], banks[0][0:NS], small2[:, 2:3], None, ALU.add).then_inc(ssm_taken[0], 1)
                    dve.wait_ge(p2_psum, j * 3 + 3 + 6)
                    V.tensor_scalar(ssm_u[:, cols(j)], banks[2][0:NS], small2[:, 4:5], dt, ALU.add, ALU.mult).then_inc(ssm_taken[2], 1)
            dve.wait_ge(ssm_taken[0], B + 1)
            dve.wait_ge(ssm_taken[2], B + 1)
            dve.wait_ge(softplus_log, 1)
            link(V.scalar_tensor_tensor(ssm_b, ssm_b, 0.0, ssm, ALU.max, ALU.add))
            link(V.tensor_tensor(ssm_b, ssm_b, ssm_u, ALU.mult))
            dve.wait_ge(ssm_taken[1], B + 1)
            for j in range(B):
                c = slice(j * TILE, (j + 1) * TILE)
                link(V.tensor_tensor_scan(ssm[:, c], decay, ssm_b[:, c], 0.0, ALU.mult, ALU.add))
                V.tensor_tensor(ssm_b[:, c], ssm[:, c], ssm_c[:, c], ALU.mult).then_inc(ssm_y, 1)
            if not upto("L2"):
                return
            dve.wait_ge(w2s_loaded, 12 * 16)
            for g in range(8):
                dve.wait_ge(uT_psum, g + 1)
                V.tensor_scalar(uT[:, g].rearrange("p k m -> p (k m)"), banks[6 + g % 2][:], 0.5 if g >= 4 else 1.0, None,
                                ALU.mult).then_inc(uT_ready, 1)
            dve.wait_ge(ssm_y, B)
            link(V.tensor_scalar(gb2[:, 0:2], gb2[:, 0:2], 0.5, None, ALU.mult))
            link(V.memset(c2, 2.0))
            for k in range(KD):
                ins = V.tensor_scalar(c2[:, k], c2[:, k], cinit[:, k:k + 1], None, ALU.mult).then_inc(cell_init, 1)
            dve.wait_ge(cell_init, 2)
            dve.sem_inc(cell_ready, 2)
            with dve.Fori(0, B) as j:
                for h in range(2):
                    n = j * 2 + h
                    c2h = c2[:, :, h * 256:(h + 1) * 256]
                    tf, ti, tg, a, b = (lstm[:, h, x] for x in range(5))
                    dve.wait_ge(gate2_ready, n * 3 + 3 + 6)
                    V.scalar_tensor_tensor(a, tf, 1.0, c2h, ALU.add, ALU.mult).then_inc(cell_step, 1)
                    V.scalar_tensor_tensor(b, ti, 1.0, tg, ALU.add, ALU.mult).then_inc(cell_step, 1)
                    dve.wait_ge(cell_step, n * 2 + 2)
                    V.scalar_tensor_tensor(c2h, a, 0.5, b, ALU.mult, ALU.add).then_inc(cell_ready, 1)
            dve.wait_ge(cpart_ready, 2)
            dve.sem_inc(o2_sum, 4)
            with dve.Fori(0, B // 2) as j2:
                for i in range(2):
                    for m in range(KD):
                        n = j2 * 4 + i * 2 + m
                        dve.wait_ge(o2_psum, n + 1)
                        dve.wait_ge(o2_added, n + 1)
                        V.tensor_tensor(y2[:, i, m], banks[i * 2 + m][:], cpart[:, m], ALU.add).then_inc(o2_sum, 1)
            if not upto("L3c"):
                return
            dve.wait_ge(w3_loaded, 6 * 16)
            link(V.tensor_scalar(ys3[:], condT[:], 1.0 / 16.0, None, ALU.mult))
            V.tensor_tensor(ysq3[:], ys3[:], ys3[:], ALU.mult).then_inc(d3_in, 1)
            V.tensor_tensor(w3sq, w3c, w3c, ALU.mult).then_inc(d3_in, 1)
            for k in range(KD):
                V.tensor_scalar(wr3b[:, k], ones[:], wr3[:, k:k + 1], None, ALU.mult).then_inc(d3_in, 1)
            dve.wait_ge(d3_psum, 1)
            link(V.tensor_scalar(d3[:].rearrange("p k b -> p (k b)"), banks[6][:, 0:KD * B], 1e-8, None, ALU.add))
            V.reciprocal(d3[:], d3[:]).then_inc(d3_recip, 1)
            dve.wait_ge(o2_added, 2 * B + 4)
            with dve.Fori(0, B // 2) as j2:
                for i in range(2):
                    j = j2 * 2 + i
                    dve.wait_ge(c3_psum, j * 2 + 2)
                    for k in range(KD):
                        V.tensor_scalar(hid[:, 2 * i + k], XT[:, k, cols(j)], ys3[:, k, bass.ds(j, 1)], None, ALU.mult).then_inc(xs3_ready, 1)
            if not upto("L3"):
                return
            S = ffn[3]
            dve.sem_inc(S["out_free"], 1)
            dve.sem_inc(rank_taken, 1)
            dve.sem_inc(o3_ready, 1)
            dve.wait_ge(before_ready, 3)
            with dve.Fori(0, B // 2) as j2:
                for i in range(2):
                    j = j2 * 2 + i
                    dve.wait_ge(s3_row, j + 1)
                    for s in range(NSUB):
                        V.tensor_tensor(smask[:, s], srow[:, s * P:(s + 1) * P], ident[:], ALU.mult).then_inc(own, 1)
                    dve.wait_ge(own, j * 5 + 4)
                    V.tensor_reduce(scol[:], smask[:], AX_X, ALU.add).then_inc(own, 1)
                    dve.wait_ge(own, j * 5 + 5)
                    for s in range(NSUB):
                        V.tensor_scalar(beats[:, 0, s], srow, scol[:, s:s + 1], None, ALU.is_lt)
                        ins = V.scalar_tensor_tensor(beats[:, 1, s], srow, scol[:, s:s + 1], before[:, s], ALU.is_equal, ALU.mult)
                    ins.then_inc(beats_ready, 1)
                    dve.wait_ge(rank_psum, j + 1)
                    V.tensor_scalar(mask3, banks[7][:], float(TOPK3), None, ALU.is_lt).then_inc(mask_ready, 1)
                    dve.wait_ge(mask_ready, j + 1)
                    dve.wait_ge(s3_th, j + 1)
                    V.scalar_tensor_tensor(gate3, th3, 1.0, mask3, ALU.add, ALU.mult).then_inc(rank_taken, 1)
                    dve.wait_ge(rank_taken, j + 2)
                    dve.wait_ge(S["hid_used"], (j + 1) * F3 + RING)
                    dve.wait_ge(o3_psum, j * 2 + 2)
                    for m in range(KD):
                        ins = V.scalar_tensor_tensor(o3[:, i, m], banks[4 + m][:], b3_down[:, m:m + 1], gate3, ALU.add, ALU.mult)
                    ins.then_inc(S["out_free"], 1)
                    dve.wait_ge(S["out_free"], j + 2)
                    V.scalar_tensor_tensor(o3[:, i], o3[:, i], 0.5, XT[:, :, cols(j)], ALU.mult, ALU.add).then_inc(o3_part, 1)
                    dve.wait_ge(o3_part, j + 1)
                    V.tensor_tensor(o3[:, i], o3[:, i], HT[:, :, cols(j)], ALU.add).then_inc(o3_ready, 1)

        @block.tensor
        def _(pe):
            pe.wait_ge(const_ready, 2)
            with pe.Fori(0, B // 2) as j2:
                for i in range(2):
                    pe.wait_ge(x_loaded[i], j2 * 16 + 16)
                    for k in range(KD):
                        pe.wait_ge(xT_copied[k], j2 * 2 + i + 1)
                        for s in range(4):
                            last = nc.tensor.transpose(banks[4 + k][:, s * P:(s + 1) * P],
                                                       xstage[:, i, s, k * P:(k + 1) * P], ident[:])
                        last.then_inc(xT_psum[k], 1)
                    last = nc.tensor.transpose(banks[7][0:P, 0:P], ident[:], ident[:])
                    last.then_inc(x_stage_free, 1)
            pe.wait_ge(cond_loaded, 16)
            for k in range(KD):
                last = nc.tensor.transpose(banks[6][:, k * B:(k + 1) * B], condrow[:, k * P:(k + 1) * P], ident[0:B, 0:B])
            last.then_inc(condT_psum, 1)
            for k in range(KD):
                pe.wait_ge(xT_copied[k], B + 1)
            pe.wait_ge(gru_w_loaded, 7 * 16)
            pe.wait_ge(gru_b_loaded, 4 * 16)
            pe.wait_ge(wsplit, NSPLIT)

            xview = XT[:].rearrange("p k (b t) -> p k t b", b=B)
            NP = STEPS // CHUNK
            W = STEPS * B

            def project(bank, g, it):
                for m in range(KD):
                    o = bank[:, m * W:(m + 1) * W]
                    nc.tensor.matmul(o, gbias[0:1, g, m * P:(m + 1) * P], ones[0:1, 0:W], start=m == 0, stop=False,
                                     skip_group_check=True)
                    for k in range(KD):
                        nc.tensor.matmul(o, wx[:, g, k, m * P:(m + 1) * P], xview[:, k, bass.ds(it * STEPS, STEPS)],
                                         start=False, stop=False, skip_group_check=True)

            def recur(bank, g, width, s, part, wait):
                for a in range(2):
                    if wait:
                        wait(a)
                    for m in range(KD):
                        for k in range(KD):
                            for w in range(2 - a):
                                last = nc.tensor.matmul(bank[:, m * width + s * B:m * width + (s + 1) * B],
                                                        wpart[:, g, w, k, m * P:(m + 1) * P],
                                                        part[:, a, k * B:(k + 1) * B],
                                                        start=False, stop=True, skip_group_check=True)
                return last

            with pe.Fori(0, TURNS) as it:
                project(banks[0], 0, it)
                for s in range(STEPS):
                    n = it * STEPS + s
                    if s % CHUNK == 0:
                        wait = lambda a: pe.wait_ge(e_part, (it * NP + s // CHUNK) * 2 + a + 1)
                    else:
                        wait = lambda a: pe.wait_ge(h_part, (n - 1) * 2 + a + 1)
                    recur(banks[0], 0, W, s, hpart, wait).then_inc(r_psum, 1)
                    if s == 0:
                        project(banks[1], 1, it)
                    recur(banks[1], 1, W, s, hpart, None).then_inc(z_psum, 1)
                    if s == 0:
                        project(banks[2], 2, it)
                        for m in range(KD):
                            nc.tensor.matmul(banks[3][:, m * NP * B:(m + 1) * NP * B], gbias[0:1, 3, m * P:(m + 1) * P],
                                             ones[0:1, 0:NP * B], start=m == 0, stop=False, skip_group_check=True)
                    recur(banks[2], 2, W, s, rhpart, lambda a: pe.wait_ge(rh_part, n * 2 + a + 1)).then_inc(c_psum, 1)
                    if (s + 1) % CHUNK == 0:
                        recur(banks[3], 3, NP * B, s // CHUNK, hpart,
                              lambda a: pe.wait_ge(h_part, n * 2 + a + 1)).then_inc(p_psum, 1)

            if not upto("L0"):
                return
            pe.wait_ge(hist_copied, 2 * TURNS + 2)

            def logits(l, src, n, first, square=None):
                for g in range(NTILE + 1):
                    if g < NTILE:
                        if g >= 2:
                            pe.wait_ge(logitT_ready, first + g - 1)
                        o = banks[6 + g % 2][0:n]
                        for k in range(KD):
                            last = nc.tensor.matmul(o, rw[:, l, k, 0:n], src[:, k, g * TILE:(g + 1) * TILE],
                                                    start=k == 0, stop=k == KD - 1 and square is None)
                        if square is not None:
                            pe.wait_ge(sq_ready, g + 1)
                            for k in range(KD):
                                last = nc.tensor.matmul(o, rsq[:, k], square[:, g % 4, k], start=False, stop=k == KD - 1)
                        last.then_inc(logit_psum, 1)
                    if g >= 1:
                        h = g - 1
                        pe.wait_ge(logitT_ready, first + h + 1)
                        for q in range(NSUB):
                            b = h * NSUB + q
                            half = NBLK // 2
                            o = (banks[5], banks[4])[b // half][:, b % half * n:(b % half + 1) * n]
                            last = nc.tensor.transpose(o, logitT[0:n, h % 2, q * P:(q + 1) * P], ident[0:n, 0:n])
                        last.then_inc(logit_turned, 1)

            def turn_gates(l):
                pe.wait_ge(gates_ready, l + 1)
                flat_w = r_w.rearrange("p b e -> p (b e)")
                for g in range(NTILE):
                    w = NSUB * E
                    last = nc.tensor.transpose(banks[6 + g // 4][0:w, g % 4 * P:(g % 4 + 1) * P], flat_w[:, g * w:(g + 1) * w], ident[:])
                    if g % 4 == 3:
                        last.then_inc(gT_psum, 1)

            def ffn_tile(S, n, src, up, down, j, out_extra=None):
                c0 = j * n
                for f in range(n + LAG):
                    if f < n:
                        pe.wait_ge(S["hid_ready"], c0 + f + 1)
                        for k in range(KD):
                            last = nc.tensor.matmul(banks[f % RING][:], up(f, k), src(k), start=k == 0, stop=k == KD - 1)
                        last.then_inc(S["up_psum"], 1)
                    h = f - LAG
                    if h == 0:
                        pe.wait_ge(S["out_free"], j + 1)
                        if out_extra:
                            out_extra()
                    if h >= 0:
                        pe.wait_ge(S["hid_ready"], c0 + h + 1 + RING)
                        for m in range(KD):
                            last = nc.tensor.matmul(banks[4 + m][:], down(h, m), hid[:, h % RING],
                                                    start=h == 0 and not out_extra, stop=h == n - 1)
                        last.then_inc(S["hid_used"], 1)

            half_of = lambda m: slice(m * P, (m + 1) * P)
            pe.wait_ge(rw_loaded, 9 * 16)
            logits(0, HT, E, 0)
            turn_gates(0)
            pe.sem_inc(ffn[0]["hid_used"], RING)
            with pe.Fori(0, E // 2) as e2:
                for i in range(2):
                    with pe.Fori(0, NTILE) as j:
                        pe.wait_ge(w0_loaded[i], e2 * 64 + 64)
                        ffn_tile(ffn[0], F0, lambda k: HT[:, k, cols(j)], lambda f, k: w0_up[i][:, k, f * P:(f + 1) * P],
                                 lambda h, m: w0_down[i][:, h, half_of(m)], (e2 * 2 + i) * NTILE + j)
            if not upto("L1c"):
                return
            pe.wait_ge(cent_ready, 1)
            for k in range(KD):
                nc.tensor.transpose(banks[3][:, 64 + k * 2 * E:64 + k * 2 * E + E], cent[:, half_of(k)], ident[0:E, 0:E])
                last = nc.tensor.transpose(banks[3][:, 64 + k * 2 * E + E:64 + (k + 1) * 2 * E], route[:, half_of(k)], ident[0:E, 0:E])
            last.then_inc(cent_psum, 1)
            pe.wait_ge(rw_ready, 1)
            for k in range(KD):
                last = nc.tensor.matmul(banks[3][0:E, 0:B], rcond[:, k], condT[:, k], start=k == 0, stop=k == KD - 1)
            last.then_inc(rcol_psum, 1)
            pe.wait_ge(ffn[0]["out_done"], E * NTILE)
            logits(1, XT, E, NTILE)
            turn_gates(1)
            pe.wait_ge(w1_loaded, 5 * 16)
            pe.wait_ge(wsh_ready, 1)
            S = ffn[1]
            pe.sem_inc(S["hid_used"], RING)
            with pe.Fori(0, NTILE) as j:
                def chunk_of(u):
                    return u // 2 if u < 2 * FS else u - FS

                def up_unit(u):
                    if u < RING:
                        pe.wait_ge(S["hid_ready"], j * N1C + u + 1)
                    else:
                        pe.wait_ge(S["hid_ready"], j * N1C + chunk_of(u - RING) + 1 + RING)
                    for k in range(KD):
                        if u < 2 * FS:
                            w = (wsh1, wsh3)[u % 2][:, k, u // 2 * P:(u // 2 + 1) * P]
                        else:
                            e, f = divmod(u - 2 * FS, FE)
                            w = w1e[:, e, k, f * P:(f + 1) * P]
                        last = nc.tensor.matmul(banks[u % RING][:], w, XT[:, k, cols(j)], start=k == 0, stop=k == KD - 1)
                    last.then_inc(S["up_psum"], 1)

                def down_chunk(h):
                    if h == 0:
                        pe.wait_ge(S["out_free"], j + 1)
                    pe.wait_ge(S["hid_ready"], j * N1C + h + 1 + RING)
                    for m in range(KD):
                        if h < FS:
                            w = wsh2[:, h, half_of(m)]
                        else:
                            e, f = divmod(h - FS, FE)
                            w = w2e[:, e, f, half_of(m)]
                        last = nc.tensor.matmul(banks[4 + m][:], w, hid[:, h % RING], start=h == 0, stop=h == N1C - 1)
                    last.then_inc(S["hid_used"], 1)

                todo = 0
                for u in range(NU1):
                    up_unit(u)
                    while todo <= chunk_of(u) - (1 if u < 2 * FS else LAG):
                        down_chunk(todo)
                        todo += 1
                while todo < N1C:
                    down_chunk(todo)
                    todo += 1
            if not upto("L1"):
                return
            pe.wait_ge(ffn[1]["out_done"], NTILE)
            logits(2, HT, RL, 2 * NTILE, WB[:, 5760:9856].rearrange("p (n k c) -> p n k c", n=4, k=KD))
            turn_gates(2)
            pe.wait_ge(w1f_loaded, 2 * 16)
            S = ffn[2]
            pe.sem_inc(S["hid_used"], RING)
            with pe.Fori(0, NTILE // 2) as j2:
                for i in range(2):
                    j = j2 * 2 + i

                    def bias_sum():
                        pe.wait_ge(g_loaded[i], G2 + j2 * 32 + 32)
                        for m in range(KD):
                            nc.tensor.matmul(banks[4 + m][:], v2b[:, half_of(m)], g1T[:, i], start=True, stop=False)

                    ffn_tile(S, E, lambda k: HT[:, k, cols(j)], lambda f, k: v1[:, f, k], lambda h, m: v2[:, h, half_of(m)], j,
                             bias_sum)
            if not upto("L2c"):
                return
            pe.wait_ge(ffn[2]["out_done"], NTILE)
            pe.wait_ge(w2_loaded, 3 * 16)
            pe.sem_inc(p2_psum, 6)
            with pe.Fori(0, B // 2) as j2:
                for i in range(2):
                    j = j2 * 2 + i
                    pe.wait_ge(conv_ready, j + 1)
                    for x, w in enumerate((wp2[:, :, 0:NS], wp2[:, :, NS:2 * NS], ws2)):
                        pe.wait_ge(ssm_taken[x], j + 1)
                        for k in range(KD):
                            last = nc.tensor.matmul(banks[x][0:NS], w[:, k], hid[:, 2 * i + k] if x < 2 else XT[:, k, cols(j)],
                                                    start=k == 0, stop=k == KD - 1)
                        last.then_inc(p2_psum, 1)
            for j in range(B):
                pe.wait_ge(ssm_y, j + 1)
                for m in range(KD):
                    n = j * KD + m
                    if n >= 4:
                        pe.wait_ge(z_ready2, n - 3)
                    nc.tensor.matmul(banks[n % 4][:], wo2[:, half_of(m)], ssm_b[:, j * TILE:(j + 1) * TILE], start=True, stop=True
                                     ).then_inc(y_psum, 1)
            if not upto("L2"):
                return
            pe.wait_ge(uraw_loaded, 8 * 16)
            for g in range(8):
                if g >= 2:
                    pe.wait_ge(uT_ready, g - 1)
                for ki in range(KD):
                    for ko in range(KD):
                        last = nc.tensor.transpose(banks[6 + g % 2][:, ki * D + ko * P:ki * D + (ko + 1) * P],
                                                   uraw[:, g, ko, half_of(ki)], ident[:])
                last.then_inc(uT_psum, 1)
            pe.wait_ge(uT_ready, 8)
            pe.wait_ge(z_ready2, 2 * B)
            with pe.Fori(0, B) as j:
                for h in range(2):
                    n = j * 2 + h
                    for part in range(2):
                        if part:
                            pe.wait_ge(cell_ready, n + 1)
                        for g in range(3):
                            if not part:
                                pe.wait_ge(gate2_ready, n * 3 + g + 1)
                            for m in range(KD):
                                for k in range(KD):
                                    src = c2[:, k, h * 256:(h + 1) * 256] if part else HT[:, k, bass.ds(j * TILE + h * 256, 256)]
                                    last = nc.tensor.matmul(banks[h * 3 + g][:, m * 256:(m + 1) * 256],
                                                            uT[:, g + 4 * part, k, half_of(m)], src,
                                                            start=not part and m == 0 and k == 0, stop=part == 1, skip_group_check=True)
                            if part:
                                last.then_inc(gate2_psum, 1)
            pe.wait_ge(cell_ready, 2 * B + 2)
            for m in range(KD):
                for k in range(KD):
                    last = nc.tensor.matmul(banks[6 + m][:], uT[:, 7, k, half_of(m)], c2[:, k], start=k == 0, stop=k == KD - 1)
                last.then_inc(cpart_psum, 1)
            with pe.Fori(0, B // 2) as j2:
                for i in range(2):
                    for m in range(KD):
                        pe.wait_ge(o2_sum, j2 * 4 + i * 2 + m + 1)
                        for k in range(KD):
                            last = nc.tensor.matmul(banks[i * 2 + m][:], uT[:, 3, k, half_of(m)], HT[:, k, cols(j2 * 2 + i)],
                                                    start=k == 0, stop=k == KD - 1)
                        last.then_inc(o2_psum, 1)
            if not upto("L3c"):
                return
            pe.wait_ge(d3_in, 4)
            for m in range(KD):
                for k in range(KD):
                    last = nc.tensor.matmul(banks[6][:, m * B:(m + 1) * B], w3sq[:, k, half_of(m)], ysq3[:, k],
                                            start=k == 0, stop=k == KD - 1)
            last.then_inc(d3_psum, 1)
            pe.sem_inc(c3_psum, 4)
            with pe.Fori(0, B // 2) as j2:
                for i in range(2):
                    j = j2 * 2 + i
                    pe.wait_ge(xs3_ready, j * 2 + 2)
                    for m in range(KD):
                        pe.wait_ge(c3_ready, j * 2 + m + 1)
                        for k in range(KD):
                            last = nc.tensor.matmul(banks[m][:], w3c[:, k, half_of(m)], hid[:, 2 * i + k],
                                                    start=k == 0, stop=k == KD - 1)
                        last.then_inc(c3_psum, 1)
            if not upto("L3"):
                return
            S = ffn[3]
            pe.wait_ge(c3_ready, 2 * B + 2)
            pe.wait_ge(before_ready, 3)
            pe.sem_inc(S["hid_used"], RING)
            pe.sem_inc(o3_psum, 2)

            def turn_out(h, n, slot):
                for s in (2 * h, 2 * h + 1):
                    for m in range(KD):
                        last = nc.tensor.transpose(banks[6][:, (s % 2) * D + m * P:(s % 2) * D + (m + 1) * P],
                                                   o3[:, slot, m, s * P:(s + 1) * P], ident[:])
                last.then_inc(o3_psum, 1)

            with pe.Fori(0, B // 2) as j2:
                for i in range(2):
                    j = j2 * 2 + i
                    pe.wait_ge(otok_ready, j * 2 + 2)
                    for k in range(KD):
                        last = nc.tensor.matmul(banks[6][:], wr3b[:, k], HT[:, k, cols(j)], start=k == 0, stop=k == KD - 1)
                    last.then_inc(s3_psum, 1)
                    ffn_tile(S, F3, lambda k: HT[:, k, cols(j)], lambda f, k: w3_up[:, k, f * P:(f + 1) * P],
                             lambda h, m: w3_down[:, h, half_of(m)], j)
                    pe.wait_ge(o3_ready, j + 1)
                    pe.wait_ge(s3_row, j + 1)
                    turn_out(0, j, 1 - i)
                    pe.wait_ge(beats_ready, j + 1)
                    pe.wait_ge(rank_taken, j + 1)
                    for n in range(2 * NSUB):
                        last = nc.tensor.matmul(banks[7][:], ones16[:], beats[:, n // NSUB, n % NSUB],
                                                start=n == 0, stop=n == 2 * NSUB - 1)
                    last.then_inc(rank_psum, 1)
                    pe.wait_ge(otok_ready, j * 2 + 3)
                    turn_out(1, j, 1 - i)
            pe.wait_ge(o3_ready, B + 1)
            pe.wait_ge(otok_ready, B * 2 + 2)
            turn_out(0, B, 1)
            pe.wait_ge(otok_ready, B * 2 + 3)
            turn_out(1, B, 1)


_OUT_SHAPE = (B, T, D)


def kernel(**inputs):
    from concourse import bacc as _bacc
    from concourse.bass_utils import run_bass_kernel_spmd as _run

    nc = _bacc.Bacc("TRN2", target_bir_lowering=False, num_devices=1)
    arrays, t = {}, {}
    for name, a in inputs.items():
        a = np.ascontiguousarray(a)
        arrays[f"in_{name}"] = a
        t[name] = nc.dram_tensor(f"in_{name}", a.shape, mybir.dt.from_np(a.dtype), kind="ExternalInput").ap()
    out = nc.dram_tensor("out_0", _OUT_SHAPE, F32, kind="ExternalOutput").ap()
    build_program(nc, t, out)
    return _run(nc, [arrays], core_ids=[0]).results[0]["out_0"]
```

```python
from contextlib import ExitStack

import numpy as np

import concourse.bass as bass
from concourse import mybir

F32 = mybir.dt.float32
F16 = mybir.dt.float16
U32 = mybir.dt.uint32
ALU = mybir.AluOpType
ACT = mybir.ActivationFunctionType
AX_X = mybir.AxisListType.X

P = 128
B, T, D = 8, 512, 256
KD = D // P
NTOK = B * T
STEPS = 16
TURNS = T // STEPS
CHUNK = 4
HSCALE = 256.0
WSCALE = 256.0
GSCALE = HSCALE * WSCALE
E = 8
RING = 4
TILE = 512
NTILE = NTOK // TILE
NSUB = TILE // P
FAR = -3.0e38
F0 = 1024 // P
FS = 512 // P
FE = 256 // P
N1C = FS + E * FE
NBLK = NTOK // P
F3 = 1024 // P
ET = 256
NET = (2 * NTOK // ET + E - 1 + 1) // 2 * 2
SLOTS = NET * ET
GRING = 4
TOPK3 = T // 2
NS = 64


def build_program(nc, t, out, stop=None, dbg=None):
    ctx = ExitStack()
    with ctx:
        def sb(name, shape, dt=F32):
            return ctx.enter_context(nc.sbuf_tensor(name, shape, dt))

        def sem(name):
            return ctx.enter_context(nc.semaphore(name))

        XT = sb("XT", [P, KD, NTOK])
        HT = sb("HT", [P, KD, NTOK])
        WA = sb("WA", [P, 8192])
        WB = sb("WB", [P, 11264])
        GB = sb("GB", [P, 8192])
        ident = sb("ident", [P, P])
        ones = sb("ones", [P, P])
        condrow = sb("condrow", [B, D])
        condT = sb("condT", [P, KD, B])

        banks = [ctx.enter_context(nc.psum_tensor(f"bank{i}", [P, 512], F32)) for i in range(8)]

        xstage = GB[:, 0:2048].rearrange("p (n s d) -> p n s d", n=2, s=4)
        wx = WB[:, 0:1536].rearrange("p (g k m) -> p g k m", g=3, k=KD)
        wraw = WB[:, 1536:3584].rearrange("p (g k m) -> p g k m", g=4, k=KD)
        wpart = WB[:, 4096:6144].bitcast(F16).rearrange("p (g n k m) -> p g n k m", g=4, n=2, k=KD)
        gbias = sb("gbias", [1, 4, D])
        hid = sb("hid", [P, RING, TILE])
        hidf = hid[:].rearrange("p r c -> p (r c)")
        w0 = [WB[:, i * 4096:(i + 1) * 4096] for i in range(2)]
        w0_up = [w[:, 0:2048].rearrange("p (k f) -> p k f", k=KD) for w in w0]
        w0_down = [w[:, 2048:4096].rearrange("p (f d) -> p f d", f=F0) for w in w0]
        b0_up = sb("b0_up", [P, 2, F0])
        ES = ET // P
        hid0 = hidf.rearrange("p (f c) -> p f c", f=F0)
        xrow = WA[:, 0:1024].rearrange("p (n s d) -> p n s d", n=2, s=ES)
        xgT = WA[:, 1024:2048].rearrange("p (n k c) -> p n k c", n=2, k=KD)
        yrow = WA[:, 2048:3072].rearrange("p (n s d) -> p n s d", n=2, s=ES)
        b0_row = WA[:, 3072:3584].rearrange("p (n d) -> p n d", n=2)
        hrow = WA[:, 3584:4608].rearrange("p (n d) -> p n d", n=GRING)
        grow = WA[:, 4608:6656].rearrange("p (n c d) -> p n c d", n=GRING, c=2)
        crow = WA[:, 6656:7680].rearrange("p (n d) -> p n d", n=GRING)
        zeros = WA[:, 0:4096]
        strict = sb("strict", [P, P])
        gk = sb("gk", [P, 2, NBLK])
        slots = sb("slots", [P, 2, NBLK], U32)
        etab_f = sb("etab_f", [1, 3, NET])
        etab = sb("etab", [1, NET], U32)
        xg = nc.dram_tensor("tile_rows", [SLOTS, D], F32, kind="Internal").ap()
        yg = nc.dram_tensor("expert_rows", [SLOTS, D], F32, kind="Internal").ap()
        RL = 17
        logitT = hid[0:RL, 0:2]
        gT = hid[0:NSUB * E, 2:4].rearrange("p r (g c) -> p (r g) c", c=P)
        rw = sb("rw", [P, 3, KD, RL])
        rsq = sb("rsq", [P, KD, RL])
        rcond = sb("rcond", [P, KD, E])
        rcol = sb("rcol", [E, B])
        rbias0 = sb("rbias0", [E, 1])
        rbias1 = sb("rbias1", [P, E])
        def rt(i, n=E):
            o = i * NBLK * E
            return GB[:, o:o + NBLK * n].rearrange("p (b n) -> p b n", n=n)
        r_log, r_sel, r_eq, r_mask1, r_mask2, r_w, r_tmp = (rt(i) for i in range(7))
        r_m1, r_m2, r_p1, r_p2, r_x, r_y, r_z, r_v = (rt(7 + i, 1) for i in range(8))
        r_raw = GB[:, 4096:4096 + NBLK * RL].rearrange("p (b n) -> p b n", n=RL)
        r_cnt, r_inc, r_exc = (GB[:, 4096 + i * 256:4352 + i * 256].rearrange("p (e b) -> p e b", e=E) for i in range(3))
        r_tile, r_end, r_base = (GB[:, 4864 + i * E:4872 + i * E] for i in range(3))
        NMAX = NTOK // ET
        r_step = GB[:, 4896:4896 + NMAX]
        r_more = GB[:, 4928:4928 + E * NMAX].rearrange("p (e i) -> p e i", e=E)
        prefer = sb("prefer", [P, E])
        cent = sb("cent", [E, D])
        cent_sq = sb("cent_sq", [E, D])
        cent_n = sb("cent_n", [E, 4])
        route = sb("route", [E, D])
        wsh1 = WB[:, 0:1024].rearrange("p (k f) -> p k f", k=KD)
        wsh3 = WB[:, 1024:2048].rearrange("p (k f) -> p k f", k=KD)
        wsh2 = WB[:, 2048:3072].rearrange("p (f d) -> p f d", f=FS)
        w1e = WB[:, 3072:7168].rearrange("p (e k f) -> p e k f", e=E, k=KD)
        w2e = WB[:, 7168:11264].rearrange("p (e f d) -> p e f d", e=E, f=FE)
        g1 = GB[:].rearrange("p (n e c) -> p n e c", n=2, e=E)
        v1 = WA[:, 0:2048].rearrange("p (e k f) -> p e k f", e=E, k=KD)
        v2 = WA[:, 2048:4096].rearrange("p (e d) -> p e d", e=E)
        v1b = sb("v1b", [P, E])
        v2b = sb("v2b", [E, D])
        g1T = sb("g1T", [E, 2, TILE])
        uraw = WA[:, 4096:8192].rearrange("p (g k m) -> p g k m", g=8, k=KD)
        uT = WA[:, 0:4096].rearrange("p (g k m) -> p g k m", g=8, k=KD)
        wp2 = WB[:, 5120:5376].rearrange("p (k m) -> p k m", k=KD)
        ws2 = WB[:, 5376:5504].rearrange("p (k m) -> p k m", k=KD)
        wo2 = WB[0:NS, 5504:5760]
        ssm = WB[0:NS, 6144:10240]
        ssm_c, ssm_b, ssm_u = GB[0:NS, 0:4096], GB[0:NS, 4096:8192], HT[0:NS, 0]
        small2 = sb("small2", [NS, 12])
        cb2 = sb("cb2", [P, KD])
        bo2 = sb("bo2", [P, KD])
        decay = WB[0:NS, 10240:10752]
        gb2 = sb("gb2", [P, 4, KD])
        cinit = sb("cinit", [P, KD])
        c2 = WB[:, 7168:8192].rearrange("p (k c) -> p k c", k=KD)
        lstm = GB[:, 0:5120].rearrange("p (h g k c) -> p h g k c", h=2, g=5, k=KD)
        y2 = GB[:, 5120:7168].rearrange("p (n k c) -> p n k c", n=2, k=KD)
        cpart = WB[:, 8192:9216].rearrange("p (k c) -> p k c", k=KD)
        w3_up = WB[:, 0:2048].rearrange("p (k f) -> p k f", k=KD)
        w3_down = WB[:, 2048:4096].rearrange("p (f d) -> p f d", f=F3)
        w3c = WB[:, 4096:4608].rearrange("p (k m) -> p k m", k=KD)
        w3sq = WB[:, 4608:5120].rearrange("p (k m) -> p k m", k=KD)
        b3_up = sb("b3_up", [P, F3])
        b3_down = sb("b3_down", [P, KD])
        ys3 = sb("ys3", [P, KD, B])
        ysq3 = sb("ysq3", [P, KD, B])
        d3 = sb("d3", [P, KD, B])
        wr3 = sb("wr3", [P, KD])
        wr3b = sb("wr3b", [P, KD, P])
        before = GB[:, 0:1024].bitcast(F16).rearrange("p (s c) -> p s c", s=NSUB)
        beats = GB[:, 1024:3072].bitcast(F16).rearrange("p (n s c) -> p n s c", n=2, s=NSUB)
        srow = GB[:, 3072:3584]
        th3 = GB[:, 3584:4096]
        mask3 = GB[:, 4096:4608]
        gate3 = GB[:, 4608:5120]
        o3 = GB[:, 5120:7168].rearrange("p (n k c) -> p n k c", n=2, k=KD)
        otok = GB[:, 7168:8192].rearrange("p (s d) -> p s d", s=NSUB)
        scol = sb("scol", [P, NSUB])
        smask = WB[:, 5120:5632].rearrange("p (s c) -> p s c", s=NSUB)
        ones16 = sb("ones16", [P, P], F16)
        gdram = [nc.dram_tensor(f"gates{i}", [E, NTOK], F32, kind="Internal").ap() for i in range(3)]
        unscale = sb("unscale", [P, STEPS // 2, KD, B])
        hist = sb("hist", [P, STEPS, KD * B])
        entry = sb("entry", [P, KD * B])
        entry_s = sb("entry_s", [P, KD * B])
        hpart = sb("hpart", [P, 2, KD * B], F16)
        rhpart = sb("rhpart", [P, 2, KD * B], F16)
        rfull = sb("rfull", [P, KD * B])
        gate_r = sb("gate_r", [P, KD * B])
        gate_z = sb("gate_z", [P, KD * B])
        cand = sb("cand", [P, KD * B])
        keep = sb("keep", [P, KD * B])
        keep_h = sb("keep_h", [P, KD * B])
        upd = sb("upd", [P, KD * B])

        const_ready = sem("const_ready")
        ident_zero = sem("ident_zero")
        x_loaded = [sem(f"x_loaded{i}") for i in range(2)]
        x_stage_free = sem("x_stage_free")
        xT_psum = [sem(f"xT_psum{k}") for k in range(KD)]
        xT_copied = [sem(f"xT_copied{k}") for k in range(KD)]
        gru_w_loaded = sem("gru_w_loaded")
        gru_b_loaded = sem("gru_b_loaded")
        wsplit = sem("wsplit")
        condT_psum = sem("condT_psum")
        condT_ready = sem("condT_ready")
        r_psum, z_psum, c_psum, p_psum = (sem(f"{n}_psum") for n in "rzcp")
        r_ready, z_ready, c_ready, p_ready = (sem(f"{n}_ready") for n in "rzcp")
        rh_part, rh_full = sem("rh_part"), sem("rh_full")
        h_part, h_full = sem("h_part"), sem("h_full")
        e_part, e_full = sem("e_part"), sem("e_full")
        keep_ready, keep_h_ready, upd_ready = sem("keep_ready"), sem("keep_h_ready"), sem("upd_ready")
        hist_copied = sem("hist_copied")
        dbg_done = sem("dbg_done")
        vc, ac = sem("vector_link"), sem("scalar_link")
        prefer_ready = sem("prefer_ready")
        xg_zeroed = sem("xg_zeroed")
        masks_ready, prefix_psum, slots_ready, etab_ready = (
            sem(n) for n in ("masks_ready", "prefix_psum", "slots_ready", "etab_ready"))
        row_psum, row_ready = sem("row_psum"), sem("row_ready")
        moved = [sem(f"rows_moved{i}") for i in range(GRING)]
        xrow_loaded = [sem(f"xrow_loaded{i}") for i in range(2)]
        yrow_stored = [sem(f"yrow_stored{i}") for i in range(2)]
        xgT_psum, xgT_ready = sem("xgT_psum"), sem("xgT_ready")
        weighted, crow_ready, crow_psum, x_added = (sem(n) for n in ("weighted", "crow_ready", "crow_psum", "x_added"))
        rw_loaded = sem("rw_loaded")
        rw_ready = sem("rw_ready")
        rcol_psum = sem("rcol_psum")
        rcol_ready = sem("rcol_ready")
        cent_psum = sem("cent_psum")
        logit_psum, logitT_ready, logit_turned = sem("logit_psum"), sem("logitT_ready"), sem("logit_turned")
        sq_ready = sem("sq_ready")
        gates_ready, gT_psum, gT_ready, gates_stored = (sem(n) for n in ("gates_ready", "gT_psum", "gT_ready", "gates_stored"))
        w0_loaded = [sem(f"w0_loaded{i}") for i in range(2)]
        g_loaded = [sem(f"g_loaded{i}") for i in range(2)]
        ffn = [{n: sem(f"ffn{i}_{n}") for n in ("up_psum", "hid_ready", "hid_used", "out_free") + (("act_hid", "out_done") if 1 <= i <= 2 else ())}
               for i in range(4)]
        w1_loaded, w1f_loaded, w2_loaded, w3_loaded = (sem(n) for n in ("w1_loaded", "w1f_loaded", "w2_loaded", "w3_loaded"))
        wsh_ready = sem("wsh_ready")
        p2_psum, ssm_taken, conv_ready = sem("p2_psum"), [sem(f"ssm_taken{i}") for i in range(3)], sem("conv_ready")
        softplus_log, ssm_y, y_psum, z_ready2 = sem("softplus_log"), sem("ssm_y"), sem("y_psum"), sem("z_ready2")
        param_log = sem("param_log")
        uT_psum, uT_ready = sem("uT_psum"), sem("uT_ready")
        gate2_psum, gate2_ready, cell_ready = sem("gate2_psum"), sem("gate2_ready"), sem("cell_ready")
        cpart_psum, cpart_ready = sem("cpart_psum"), sem("cpart_ready")
        o2_psum, o2_sum, o2_tanh, o2_added = (sem(n) for n in ("o2_psum", "o2_sum", "o2_tanh", "o2_added"))
        d3_psum, d3_recip, d3_ready = sem("d3_psum"), sem("d3_recip"), sem("d3_ready")
        xs3_ready, c3_psum, c3_ready = sem("xs3_ready"), sem("c3_psum"), sem("c3_ready")
        s3_psum, s3_row, s3_th, beats_ready, rank_psum, rank_taken = (
            sem(n) for n in ("s3_psum", "s3_row", "s3_th", "beats_ready", "rank_psum", "rank_taken"))
        o3_ready, o3_psum, otok_ready, stored = (sem(n) for n in ("o3_ready", "o3_psum", "otok_ready", "stored"))
        before_ready = sem("before_ready")
        exp_in, exp_done = sem("exp_in"), sem("exp_done")
        cent_sum, cent_root, cent_ready = sem("cent_sum"), sem("cent_root"), sem("cent_ready")
        norm_sum, norm_root = sem("norm_sum"), sem("norm_root")
        silu_half = sem("silu_half")
        conv_step = [sem(f"conv_step{k}") for k in range(KD)]
        cell_init, cell_step = sem("cell_init"), sem("cell_step")
        d3_in, own, mask_ready, o3_part = sem("d3_in"), sem("own"), sem("mask_ready"), sem("o3_part")
        w2s_loaded, uraw_loaded = sem("w2s_loaded"), sem("uraw_loaded")

        NU1 = 2 * FS + E * FE
        G2 = 16 * NTILE // 2
        MOVED = 32 * NBLK // GRING
        LAG = 2
        STAGES = ["gru", "L0", "L1c", "L1", "L2c", "L2", "L3c", "L3"]

        def upto(stage):
            return stop is None or STAGES.index(stage) <= STAGES.index(stop)

        def cols(j, n=TILE):
            return bass.ds(j * TILE, n)

        def cols_of(b):
            return bass.ds(b * P, P)

        class Link:

            def __init__(self, eng, link_sem):
                self.eng, self.sem, self.n = eng, link_sem, 0

            def __call__(self, ins):
                ins.then_inc(self.sem, 1)
                self.n += 1
                self.eng.wait_ge(self.sem, self.n)

        NSPLIT = 4 * 3 + 4

        block = ctx.enter_context(nc.Block())

        @block.sync
        def _(sp):
            xrows = t["x"].rearrange("b (s p) d -> p b s d", p=P)
            for i in range(2):
                sp.dma_start(xstage[:, i], xrows[:, i]).then_inc(x_loaded[i], 16)
            sp.dma_start(condrow[:], t["cond_1024"]).then_inc(gru_b_loaded, 16)
            for g, n in enumerate(("Wr", "Wz", "Wh")):
                w = t["L0_cond_" + n].rearrange("(k p) m -> p k m", p=P)
                sp.dma_start(wx[:, g], w[:, 0:KD]).then_inc(gru_w_loaded, 16)
                sp.dma_start(wraw[:, g], w[:, KD:]).then_inc(gru_w_loaded, 16)
            sp.dma_start(wraw[:, 3], t["L0_cond_Wp"].rearrange("(k p) m -> p k m", p=P)).then_inc(gru_w_loaded, 16)
            for g, n in enumerate(("br", "bz", "bh", "bp")):
                sp.dma_start(gbias[0:1, g], t["L0_cond_" + n].rearrange("(a m) -> a m", a=1)).then_inc(gru_b_loaded, 16)
            with sp.Fori(1, B // 2) as j2:
                for i in range(2):
                    sp.wait_ge(x_stage_free, j2 * 2 + i - 1)
                    sp.dma_start(xstage[:, i], xrows[:, bass.ds(j2 * 2 + i, 1)]).then_inc(x_loaded[i], 16)

            def column(dst, src):
                return sp.dma_start(dst, src, allow_slow_non_contiguous=True)

            def load_expert(i, e):
                one = bass.ds(e, 1)
                sp.dma_start(w0_up[i], t["L0_ffn_w1"].rearrange("e (k p) f -> p e k f", p=P)[:, one]).then_inc(w0_loaded[i], 16)
                sp.dma_start(w0_down[i], t["L0_ffn_w2"].rearrange("e (f p) d -> p e f d", p=P)[:, one]).then_inc(w0_loaded[i], 16)
                column(b0_up[:, i], t["L0_ffn_b1"].rearrange("e (f p) -> p e f", p=P)[:, one]).then_inc(w0_loaded[i], 16)
                sp.dma_start(b0_row[:, i], t["L0_ffn_b2"][one].partition_broadcast(P)).then_inc(w0_loaded[i], 16)

            sp.dma_start(rw[:, 0, :, 0:E], t["L0_ffn_gate_w"].rearrange("(k p) e -> p k e", p=P)).then_inc(rw_loaded, 16)
            column(rbias0[:], t["L0_ffn_gate_b"].rearrange("(e a) -> e a", a=1)).then_inc(rw_loaded, 16)
            r1 = t["L1_cond_router_W"].rearrange("(h k p) e -> p h k e", p=P, h=2)
            sp.dma_start(rw[:, 1, :, 0:E], r1[:, 0]).then_inc(rw_loaded, 16)
            sp.dma_start(rcond[:], r1[:, 1]).then_inc(rw_loaded, 16)
            sp.dma_start(rbias1[:], t["L1_cond_router_bias"].rearrange("(a e) -> a e", a=1).partition_broadcast(P)).then_inc(rw_loaded, 16)
            sp.dma_start(cent[:], t["L1_ffn_centroids"]).then_inc(rw_loaded, 16)
            sp.dma_start(route[:], t["L1_ffn_w_route"]).then_inc(rw_loaded, 16)
            column(v1b[:], t["L1_ffn_b1"].rearrange("e p -> p e")).then_inc(rw_loaded, 16)
            sp.dma_start(v2b[:], t["L1_ffn_b2"]).then_inc(rw_loaded, 16)
            halves = lambda name: t[name].rearrange("(k p) -> p k", p=P)
            col = lambda name, a, n: t[name].rearrange("(p a) -> p a", a=1)[a:a + n]
            column(cb2[:], halves("L2_cond_conv_b")).then_inc(w2s_loaded, 16)
            column(bo2[:], halves("L2_cond_bo")).then_inc(w2s_loaded, 16)
            for i, (name, a) in enumerate((("L2_cond_A_log", 0), ("L2_cond_dt_log", 0), ("L2_cond_bp", 0),
                                           ("L2_cond_bp", NS), ("L2_cond_bs", 0))):
                column(small2[:, i:i + 1], col(name, a, NS)).then_inc(w2s_loaded, 16)
            for g, name in enumerate(("bf", "bi", "bc", "bo")):
                column(gb2[:, g], halves("L2_ffn_" + name)).then_inc(w2s_loaded, 16)
            column(cinit[:], halves("L2_ffn_in_c")).then_inc(w2s_loaded, 16)
            column(b3_up[:], t["L3_ffn_b1"].rearrange("(f p) -> p f", p=P)).then_inc(w3_loaded, 16)
            column(b3_down[:], halves("L3_ffn_b2")).then_inc(w3_loaded, 16)
            column(wr3[:], halves("L3_ffn_w_router")).then_inc(w3_loaded, 16)

            def finish(src, waits):
                for sm, v in waits:
                    sp.wait_ge(sm, v)
                sp.dma_start(dbg, src).then_inc(dbg_done, 16)
                sp.wait_ge(dbg_done, 16)

            sp.wait_ge(prefer_ready, E + 8)
            zrows = xg.rearrange("(p n) d -> p (n d)", p=P)
            for i in range(SLOTS * D // P // 4096):
                sp.dma_start(zrows[:, i * 4096:(i + 1) * 4096], zeros).then_inc(xg_zeroed, 16)
            if stop == "gru":
                finish(HT[:], [(hist_copied, 2 * TURNS + 2)])
                return

            def load_tile(i, n, wait):
                if wait:
                    sp.wait_ge(xgT_psum, n - 1)
                sp.dma_start(xrow[:, i], xg.rearrange("(n s p) d -> p n s d", p=P, s=ES)[:, bass.ds(n, 1)]).then_inc(xrow_loaded[i], 16)
                if wait:
                    sp.wait_ge(ffn[0]["out_free"], n)
                load_expert(i, sp.value_load(etab[0:1, bass.ds(n, 1)], min_val=0, max_val=E - 1))

            sp.wait_ge(etab_ready, 1)
            for q in range(GRING):
                sp.wait_ge(moved[q], MOVED)
            for i in range(2):
                load_tile(i, i, False)
            with sp.Fori(1, NET // 2) as n2:
                for i in range(2):
                    load_tile(i, n2 * 2 + i, True)
            sp.wait_ge(ffn[0]["out_free"], NET + 1)
            for dst, name in ((wsh1, "w1"), (wsh3, "w3"), (wsh2, "w2")):
                sp.dma_start(dst, t["L1_cond_" + name].rearrange("(k p) f -> p k f", p=P)).then_inc(w1_loaded, 16)
            sp.dma_start(w1e, t["L1_cond_W1e"].rearrange("e (k p) f -> p e k f", p=P)).then_inc(w1_loaded, 16)
            sp.dma_start(w2e, t["L1_cond_W2e"].rearrange("e (f p) d -> p e f d", p=P)).then_inc(w1_loaded, 16)

            def store_gates(l):
                sp.wait_ge(gT_ready, 2 * l)
                rows = gdram[l].rearrange("e (g q c) -> q e g c", q=NSUB, c=P)
                for q in range(NSUB):
                    sp.dma_start(rows[q], gT[q * E:(q + 1) * E]).then_inc(gates_stored, 16)
                sp.wait_ge(gates_stored, 16 * NSUB * l)

            def load_gates(l, i, j):
                src = gdram[l][:, cols(j)]
                sp.dma_start(g1[:, i], src.partition_broadcast(P)).then_inc(g_loaded[i], 16)
                if l == 2:
                    sp.dma_start(g1T[:, i], src).then_inc(g_loaded[i], 16)

            sp.wait_ge(x_added, NBLK)
            if stop == "L0":
                return finish(XT[:], [])
            sp.dma_start(v1, t["L1_ffn_w1"].rearrange("e (k p) f -> p e k f", p=P)).then_inc(w1f_loaded, 16)
            sp.dma_start(v2, t["L1_ffn_w2"].rearrange("e p d -> p e d")).then_inc(w1f_loaded, 16)
            for g, name in enumerate(("wf", "wi", "wc", "wo", "uf", "ui", "uc", "uo")):
                sp.dma_start(uraw[:, g], t["L2_ffn_" + name].rearrange("(k p) m -> p k m", p=P)).then_inc(uraw_loaded, 16)
            for l, f in ((1, 1), (2, 2)):
                store_gates(l)
                for i in range(2):
                    load_gates(l, i, i)
                with sp.Fori(1, NTILE // 2) as j2:
                    for i in range(2):
                        sp.wait_ge(ffn[f]["out_done"], j2 * 2 + i - 1)
                        load_gates(l, i, j2 * 2 + i)
                sp.wait_ge(ffn[f]["out_done"], NTILE)
                if l == 1:
                    if stop == "L1c":
                        return finish(HT[:], [])
                    sp.dma_start(w3_up, t["L3_ffn_W1"].rearrange("(k p) f -> p k f", p=P)).then_inc(w3_loaded, 16)
                    sp.dma_start(w3_down, t["L3_ffn_W2"].rearrange("(f p) d -> p f d", p=P)).then_inc(w3_loaded, 16)
                    sp.dma_start(w3c, t["L3_cond_weight"].rearrange("(k p) d -> p k d", p=P)).then_inc(w3_loaded, 16)
                    sp.dma_start(wp2, t["L2_cond_Wp"].rearrange("(k p) d -> p k d", p=P)).then_inc(w2_loaded, 16)
                    sp.dma_start(ws2, t["L2_cond_Ws"].rearrange("(k p) d -> p k d", p=P)).then_inc(w2_loaded, 16)
                    sp.dma_start(wo2, t["L2_cond_Wo"]).then_inc(w2_loaded, 16)
            if stop == "L1":
                return finish(XT[:], [])
            if stop == "L2c":
                return finish(HT[:], [(z_ready2, 2 * B)])
            if stop == "L2":
                return finish(XT[:], [(o2_added, 2 * B + 4)])
            if stop == "L3c":
                return finish(HT[:], [(c3_ready, 2 * B + 2)])
            sp.sem_inc(stored, 32)
            orows = out.rearrange("b (s p) d -> p b s d", p=P)
            with sp.Fori(0, B) as j:
                sp.wait_ge(otok_ready, j * 2 + 6)
                sp.dma_start(orows[:, bass.ds(j, 1)], otok).then_inc(stored, 16)
            sp.wait_ge(stored, B * 16 + 32)

        @block.gpsimd
        def _(pool):
            nc.gpsimd.memset(ident[:], 0.0).then_inc(ident_zero, 1)
            nc.gpsimd.memset(ones[:], 1.0).then_inc(const_ready, 1)
            for e in range(E):
                nc.gpsimd.memset(prefer[:, e:e + 1], float(E - e)).then_inc(prefer_ready, 1)
            nc.gpsimd.memset(unscale[:], 1.0 / HSCALE).then_inc(prefer_ready, 1)
            nc.gpsimd.memset(rw[:, 2], 0.0).then_inc(prefer_ready, 1)
            nc.gpsimd.memset(rsq[:], 0.0).then_inc(prefer_ready, 1)
            nc.gpsimd.memset(ones16[:], 1.0).then_inc(prefer_ready, 1)
            nc.gpsimd.memset(strict[:], 1.0).then_inc(prefer_ready, 1)
            nc.gpsimd.memset(zeros, 0.0).then_inc(prefer_ready, 1)
            pool.wait_ge(prefer_ready, E + 6)
            nc.gpsimd.affine_select(out=strict[:], in_=strict[:], compare_op=ALU.is_gt, fill=0.0, base=0,
                                    pattern=[[1, P]], channel_multiplier=-1).then_inc(prefer_ready, 1)
            nc.gpsimd.memset(rsq[:, :, RL - 1:RL], 1.0).then_inc(prefer_ready, 1)
            pool.wait_ge(ident_zero, 1)
            nc.gpsimd.affine_select(out=ident[:], in_=ident[:], compare_op=ALU.not_equal, fill=1.0, base=0,
                                    pattern=[[-1, P]], channel_multiplier=1).then_inc(const_ready, 1)
            pool.sem_inc(hist_copied, 2)
            hview = HT[:].rearrange("p k (b t) -> p t k b", b=B)
            with pool.Fori(0, TURNS) as it:
                for half in range(2):
                    n = STEPS // 2
                    pool.wait_ge(h_full, it * STEPS + (half + 1) * n)
                    nc.gpsimd.tensor_tensor(hview[:, bass.ds(it * STEPS + half * n, n)],
                                            hist[:, half * n:(half + 1) * n].rearrange("p s (k b) -> p s k b", k=KD),
                                            unscale[:], ALU.mult).then_inc(hist_copied, 1)
            if not upto("L0"):
                return

            pool.wait_ge(slots_ready, 2)
            pool.wait_ge(xg_zeroed, 16 * (SLOTS * D // P // 4096))
            for b in range(NBLK):
                q = b % GRING
                pool.wait_ge(row_ready, b + 1)
                for c in range(2):
                    nc.gpsimd.indirect_dma_start(xg, bass.IndirectOffsetOnAxis(ap=slots[:, c, b:b + 1], axis=0),
                                                 hrow[:, q], None).then_inc(moved[q], 16)
            yrows = yg.rearrange("(n s p) d -> p n s d", p=P, s=ES)
            with pool.Fori(0, NET // 2) as n2:
                for i in range(2):
                    pool.wait_ge(ffn[0]["out_free"], n2 * 2 + i + 2)
                    nc.gpsimd.dma_start(yrows[:, bass.ds(n2 * 2 + i, 1)], yrow[:, i]).then_inc(yrow_stored[i], 16)
            for i in range(2):
                pool.wait_ge(yrow_stored[i], 16 * (NET // 2))
            pool.sem_inc(crow_ready, GRING)
            for b in range(NBLK):
                q = b % GRING
                pool.wait_ge(crow_ready, b + 1)
                for c in range(2):
                    nc.gpsimd.indirect_dma_start(grow[:, q, c], None, yg,
                                                 bass.IndirectOffsetOnAxis(ap=slots[:, c, b:b + 1], axis=0)).then_inc(moved[q], 16)
            if upto("L2"):
                pool.sem_inc(o2_added, 4)
                with pool.Fori(0, NTILE // 2) as j2:
                    for i in range(2):
                        for m in range(KD):
                            n = j2 * 4 + i * 2 + m
                            pool.wait_ge(o2_tanh, n + 1)
                            x_t = XT[:, m, cols(j2 * 2 + i)]
                            nc.gpsimd.tensor_tensor(x_t, x_t, y2[:, i, m], ALU.add).then_inc(o2_added, 1)
            if upto("L3"):
                pool.wait_ge(o2_added, 2 * B + 4)
                nc.gpsimd.memset(before[:], 1.0).then_inc(before_ready, 1)
                nc.gpsimd.memset(o3[:, 1], 0.0).then_inc(before_ready, 1)
                pool.wait_ge(before_ready, 2)
                nc.gpsimd.affine_select(out=before, in_=before, compare_op=ALU.is_gt, fill=0.0, base=0,
                                        pattern=[[-P, NSUB], [1, TILE]], channel_multiplier=-1).then_inc(before_ready, 1)

        @block.scalar
        def _(act):
            act.sem_inc(xT_copied[1], 1)
            xv = XT[:]
            with act.Fori(0, B) as j:
                act.wait_ge(xT_psum[1], j + 1)
                nc.scalar.copy(xv[:, 1, bass.ds(j * T, T)], banks[5][:]).then_inc(xT_copied[1], 1)
            bank = {"r": banks[0], "z": banks[1], "c": banks[2]}

            def gate_in(b, s):
                return b[:, 0:2 * STEPS * B].rearrange("p (m c) -> p m c", m=KD)[:, :, s * B:(s + 1) * B]

            def flat(x):
                return x[:].rearrange("p (k b) -> p k b", k=KD)

            with act.Fori(0, TURNS) as it:
                for s in range(STEPS):
                    n = it * STEPS + s + 1
                    act.wait_ge(r_psum, n)
                    nc.scalar.activation(flat(gate_r), gate_in(bank["r"], s), ACT.Tanh, scale=0.5 / GSCALE).then_inc(r_ready, 1)
                    act.wait_ge(z_psum, n)
                    nc.scalar.activation(flat(gate_z), gate_in(bank["z"], s), ACT.Tanh, scale=0.5 / GSCALE).then_inc(z_ready, 1)
                    act.wait_ge(c_psum, n)
                    nc.scalar.activation(flat(cand), gate_in(bank["c"], s), ACT.Tanh, scale=1.0 / GSCALE).then_inc(c_ready, 1)
                    if (s + 1) % CHUNK == 0:
                        q = s // CHUNK
                        act.wait_ge(p_psum, it * (STEPS // CHUNK) + q + 1)
                        pin = banks[3][:, 0:KD * (STEPS // CHUNK) * B].rearrange("p (m c) -> p m c", m=KD)
                        nc.scalar.activation(flat(entry), pin[:, :, q * B:(q + 1) * B], ACT.Tanh, scale=1.0 / GSCALE).then_inc(p_ready, 1)

            if not upto("L0"):
                return
            link = Link(act, ac)

            def routing_copies(l, first, square=None):
                for g in range(NTILE):
                    act.wait_ge(logit_psum, first + g + 1)
                    if square and g + 4 < NTILE:
                        square(g + 4)
                    if g >= 2:
                        act.wait_ge(logit_turned, first + g - 1)
                    n = RL if l == 2 else E
                    dst, src = logitT[0:n, g % 2], banks[6 + g % 2][0:n]
                    if l == 0:
                        i = nc.scalar.activation(dst, src, ACT.Identity, bias=rbias0[:])
                    elif l == 1:
                        i = nc.scalar.activation(dst, src, ACT.Sigmoid, bias=rcol[:, g:g + 1])
                    else:
                        i = nc.scalar.activation(dst, src, ACT.Identity)
                    i.then_inc(logitT_ready, 1)

            def gates_copy(l):
                for h in range(2):
                    act.wait_ge(gT_psum, 2 * l + h - 1)
                    nc.scalar.copy(gT[:, h * 4:h * 4 + 4], banks[6 + h][0:NSUB * E].rearrange("p (g c) -> p g c", c=P)
                                   ).then_inc(gT_ready, 1)

            def hidden(S, n, count, func, bias, done):
                act.wait_ge(S["up_psum"], count + 1)
                act.wait_ge(S["hid_used"], count + 1)
                nc.scalar.activation(hid[:, n], banks[n][:], func, bias=bias).then_inc(S[done], 1)

            act.wait_ge(rw_loaded, 9 * 16)
            routing_copies(0, 0)
            act.wait_ge(exp_in, 1)
            nc.scalar.activation(r_y, r_x, ACT.Exp).then_inc(exp_done, 1)
            act.wait_ge(xg_zeroed, 16 * (SLOTS * D // P // 4096))
            for b in range(NBLK):
                q = b % GRING
                act.wait_ge(row_psum, b + 1)
                if b >= GRING:
                    act.wait_ge(moved[q], 32 * (b // GRING))
                nc.scalar.copy(hrow[:, q], banks[q][:, 0:D]).then_inc(row_ready, 1)
            act.sem_inc(ffn[0]["hid_ready"], RING)
            S = ffn[0]
            with act.Fori(0, NET // 2) as n2:
                for i in range(2):
                    act.wait_ge(w0_loaded[i], n2 * 64 + 64)
                    for f in range(F0):
                        count = (n2 * 2 + i) * F0 + f
                        act.wait_ge(S["up_psum"], count + 1)
                        act.wait_ge(S["hid_used"], count + 1)
                        nc.scalar.activation(hid0[:, f], banks[f % RING][:, 0:ET], ACT.Gelu, bias=b0_up[:, i, f:f + 1]
                                             ).then_inc(S["hid_ready"], 1)
            if not upto("L1c"):
                return
            act.wait_ge(cent_sum, 1)
            nc.scalar.activation(cent_n[:, 1:2], cent_n[:, 0:1], ACT.Sqrt).then_inc(cent_root, 1)
            act.wait_ge(rcol_ready, 1)
            act.wait_ge(x_added, NBLK)
            routing_copies(1, NTILE)
            gates_copy(1)
            act.wait_ge(gates_stored, 16 * NSUB)
            with act.Fori(0, NTILE) as j:
                for f in range(FS):
                    act.wait_ge(ffn[1]["up_psum"], j * NU1 + 2 * f + 1)
                    act.wait_ge(ffn[1]["hid_used"], j * N1C + f + 1)
                    nc.scalar.activation(hid[:, f % RING], banks[2 * f % RING][:], ACT.Tanh, scale=0.5).then_inc(ffn[1]["act_hid"], 1)
                for f in range(FS, N1C):
                    act.wait_ge(ffn[1]["up_psum"], j * NU1 + FS + f + 1)
                    act.wait_ge(ffn[1]["hid_used"], j * N1C + f + 1)
                    nc.scalar.activation(hid[:, f % RING], banks[f % RING][:], ACT.Gelu).then_inc(ffn[1]["act_hid"], 1)
            if not upto("L1"):
                return
            act.wait_ge(ffn[1]["out_done"], NTILE)
            sqt = WB[:, 5760:9856].rearrange("p (n k c) -> p n k c", n=4, k=KD)

            def square(g):
                for k in range(KD):
                    i = nc.scalar.activation(sqt[:, g % 4, k], HT[:, k, g * TILE:(g + 1) * TILE], ACT.Square)
                i.then_inc(sq_ready, 1)

            for g in range(4):
                square(g)
            routing_copies(2, 2 * NTILE, square)
            act.wait_ge(norm_sum, 1)
            nc.scalar.activation(r_y, r_x, ACT.Sqrt).then_inc(norm_root, 1)
            act.wait_ge(exp_in, 2)
            nc.scalar.activation(r_eq, r_sel, ACT.Exp).then_inc(exp_done, 1)
            gates_copy(2)
            act.wait_ge(gates_stored, 2 * 16 * NSUB)
            with act.Fori(0, NTILE) as j:
                for f in range(E):
                    hidden(ffn[2], f % RING, j * E + f, ACT.Gelu, v1b[:, f:f + 1], "act_hid")
            if not upto("L2c"):
                return
            act.wait_ge(w2s_loaded, 12 * 16)
            link(nc.scalar.activation(small2[:, 5:7], small2[:, 0:2], ACT.Abs))
            link(nc.scalar.activation(small2[:, 5:7], small2[:, 5:7], ACT.Exp, scale=-1.0))
            nc.scalar.activation(small2[:, 5:7], small2[:, 5:7], ACT.Ln, bias=1.0).then_inc(param_log, 1)
            act.sem_inc(ssm_taken[1], 1)
            with act.Fori(0, B) as j:
                act.wait_ge(p2_psum, j * 3 + 2 + 6)
                nc.scalar.activation(ssm_c[:, cols(j)], banks[1][0:NS], ACT.Tanh, bias=small2[:, 3:4]).then_inc(ssm_taken[1], 1)
            act.wait_ge(ssm_taken[0], B + 1)
            link(nc.scalar.activation(ssm[:], ssm_b[:], ACT.Abs))
            link(nc.scalar.activation(ssm[:], ssm[:], ACT.Exp, scale=-1.0))
            nc.scalar.activation(ssm[:], ssm[:], ACT.Ln, bias=1.0).then_inc(softplus_log, 1)
            for j in range(B):
                for m in range(KD):
                    n = j * KD + m
                    act.wait_ge(y_psum, n + 1)
                    nc.scalar.activation(HT[:, m, j * TILE:(j + 1) * TILE], banks[n % 4][:], ACT.Identity,
                                         bias=bo2[:, m:m + 1]).then_inc(z_ready2, 1)
            if not upto("L2"):
                return
            act.wait_ge(cell_ready, 2)
            act.sem_inc(gate2_ready, 6)
            with act.Fori(0, B) as j:
                for h in range(2):
                    for g in range(3):
                        act.wait_ge(gate2_psum, j * 6 + h * 3 + g + 1)
                        for m in range(KD):
                            i = nc.scalar.activation(lstm[:, h, g, m], banks[h * 3 + g][:, m * 256:(m + 1) * 256], ACT.Tanh,
                                                     scale=0.5 if g < 2 else 1.0, bias=gb2[:, g, m:m + 1])
                        i.then_inc(gate2_ready, 1)
            for m in range(KD):
                act.wait_ge(cpart_psum, m + 1)
                nc.scalar.activation(cpart[:, m], banks[6 + m][:], ACT.Identity, bias=gb2[:, 3, m:m + 1]).then_inc(cpart_ready, 1)
            with act.Fori(0, B // 2) as j2:
                for i in range(2):
                    for m in range(KD):
                        act.wait_ge(o2_sum, j2 * 4 + i * 2 + m + 1 + 4)
                        nc.scalar.activation(y2[:, i, m], y2[:, i, m], ACT.Tanh).then_inc(o2_tanh, 1)
            if not upto("L3c"):
                return
            act.wait_ge(d3_recip, 1)
            nc.scalar.activation(d3[:], d3[:], ACT.Sqrt).then_inc(d3_ready, 1)
            act.wait_ge(d3_ready, 1)
            act.sem_inc(c3_ready, 2)
            with act.Fori(0, B) as j:
                for m in range(KD):
                    act.wait_ge(c3_psum, j * 2 + m + 1 + 4)
                    nc.scalar.activation(HT[:, m, cols(j)], banks[m][:], ACT.Identity, scale=d3[:, m, bass.ds(j, 1)]).then_inc(c3_ready, 1)
            if not upto("L3"):
                return
            S = ffn[3]
            act.sem_inc(S["hid_ready"], RING)
            act.sem_inc(otok_ready, 2)
            with act.Fori(0, B) as j:
                act.wait_ge(s3_psum, j + 1)
                act.wait_ge(rank_taken, j + 1)
                nc.scalar.copy(srow, banks[6][:]).then_inc(s3_row, 1)
                act.wait_ge(s3_row, j + 1)
                nc.scalar.activation(th3, srow, ACT.Tanh, scale=0.5).then_inc(s3_th, 1)
                for f in range(F3):
                    hidden(S, f % RING, j * F3 + f, ACT.Gelu_apprx_tanh, b3_up[:, f:f + 1], "hid_ready")
                for h in range(2):
                    act.wait_ge(o3_psum, j * 2 + h + 3)
                    if h == 0:
                        act.wait_ge(stored, j * 16 + 16)
                    nc.scalar.copy(otok[:, 2 * h:2 * h + 2], banks[6][:].rearrange("p (s d) -> p s d", s=2)).then_inc(otok_ready, 1)
            for h in range(2):
                act.wait_ge(o3_psum, B * 2 + h + 3)
                if h == 0:
                    act.wait_ge(stored, B * 16 + 16)
                nc.scalar.copy(otok[:, 2 * h:2 * h + 2], banks[6][:].rearrange("p (s d) -> p s d", s=2)).then_inc(otok_ready, 1)

        @block.vector
        def _(dve):
            dve.sem_inc(xT_copied[0], 1)
            with dve.Fori(0, B) as j:
                dve.wait_ge(xT_psum[0], j + 1)
                nc.vector.tensor_copy(XT[:, 0, bass.ds(j * T, T)], banks[4][:]).then_inc(xT_copied[0], 1)
            dve.wait_ge(gru_w_loaded, 7 * 16)
            done = 0
            for g in range(4):
                nc.vector.tensor_scalar(wraw[:, g], wraw[:, g], WSCALE / (2 if g == 2 else 1), None, ALU.mult).then_inc(wsplit, 1)
                done += 1
                dve.wait_ge(wsplit, done)
                nc.vector.tensor_copy(wpart[:, g, 0], wraw[:, g]).then_inc(wsplit, 1)
                done += 1
                dve.wait_ge(wsplit, done)
                nc.vector.tensor_tensor(wpart[:, g, 1], wraw[:, g], wpart[:, g, 0], ALU.subtract).then_inc(wsplit, 1)
                done += 1
            for g in range(3):
                nc.vector.tensor_scalar(wx[:, g], wx[:, g], GSCALE, None, ALU.mult).then_inc(wsplit, 1)
            dve.wait_ge(gru_b_loaded, 5 * 16)
            nc.vector.tensor_scalar(gbias[:], gbias[:], GSCALE, None, ALU.mult).then_inc(wsplit, 1)
            dve.wait_ge(condT_psum, 1)
            nc.vector.tensor_copy(condT[:].rearrange("p k b -> p (k b)"), banks[6][:, 0:KD * B]).then_inc(condT_ready, 1)
            nc.vector.tensor_copy(entry[:], banks[6][:, 0:KD * B]).then_inc(p_ready, 1)

            def split_entry(n):
                dve.wait_ge(p_ready, n)
                nc.vector.tensor_scalar(hpart[:, 0], entry[:], HSCALE, None, ALU.mult).then_inc(e_part, 1)
                nc.vector.tensor_scalar(entry_s[:], entry[:], HSCALE, None, ALU.mult).then_inc(e_full, 1)
                dve.wait_ge(e_full, n)
                nc.vector.tensor_tensor(hpart[:, 1], entry_s[:], hpart[:, 0], ALU.subtract).then_inc(e_part, 1)

            NP = STEPS // CHUNK
            split_entry(1)
            with dve.Fori(0, TURNS) as it:
                for s in range(STEPS):
                    n = it * STEPS + s
                    h = entry_s[:] if s % CHUNK == 0 else hist[:, s - 1]
                    dve.wait_ge(r_ready, n + 1)
                    nc.vector.scalar_tensor_tensor(rhpart[:, 0], gate_r[:], 1.0, h, ALU.add, ALU.mult).then_inc(rh_part, 1)
                    nc.vector.scalar_tensor_tensor(rfull[:], gate_r[:], 1.0, h, ALU.add, ALU.mult).then_inc(rh_full, 1)
                    dve.wait_ge(rh_full, n + 1)
                    nc.vector.tensor_tensor(rhpart[:, 1], rfull[:], rhpart[:, 0], ALU.subtract).then_inc(rh_part, 1)
                    dve.wait_ge(z_ready, n + 1)
                    nc.vector.tensor_scalar(keep[:], gate_z[:], -0.5, 0.5, ALU.mult, ALU.add).then_inc(keep_ready, 1)
                    dve.wait_ge(keep_ready, n + 1)
                    nc.vector.tensor_tensor(keep_h[:], keep[:], h, ALU.mult).then_inc(keep_h_ready, 1)
                    if s % (STEPS // 2) == 0:
                        dve.wait_ge(hist_copied, it * 2 + 1 + s // (STEPS // 2))
                    dve.wait_ge(c_ready, n + 1)
                    nc.vector.scalar_tensor_tensor(upd[:], gate_z[:], 1.0, cand[:], ALU.add, ALU.mult).then_inc(upd_ready, 1)
                    dve.wait_ge(upd_ready, n + 1)
                    nc.vector.scalar_tensor_tensor(hpart[:, 0], upd[:], 0.5 * HSCALE, keep_h[:], ALU.mult, ALU.add).then_inc(h_part, 1)
                    nc.vector.scalar_tensor_tensor(hist[:, s], upd[:], 0.5 * HSCALE, keep_h[:], ALU.mult, ALU.add).then_inc(h_full, 1)
                    dve.wait_ge(h_full, n + 1)
                    nc.vector.tensor_tensor(hpart[:, 1], hist[:, s], hpart[:, 0], ALU.subtract).then_inc(h_part, 1)
                    if (s + 1) % CHUNK == 0:
                        split_entry(it * NP + (s // CHUNK + 2))

            if not upto("L0"):
                return
            link = Link(dve, vc)
            V = nc.vector
            wide = lambda x: x.to_broadcast([P, NBLK, E])
            pref = prefer[:].rearrange("p (a e) -> p a e", a=1).to_broadcast([P, NBLK, E])

            def top2(x):
                for m, p, mask in ((r_m1, r_p1, r_mask1), (r_m2, r_p2, r_mask2)):
                    link(V.tensor_reduce(m, x, AX_X, ALU.max))
                    link(V.tensor_tensor(r_eq, x, wide(m), ALU.is_equal))
                    link(V.tensor_tensor(r_tmp, r_eq, pref, ALU.mult))
                    link(V.tensor_reduce(p, r_tmp, AX_X, ALU.max))
                    link(V.tensor_tensor(mask, r_tmp, wide(p), ALU.is_equal))
                    if m is r_m1:
                        link(V.scalar_tensor_tensor(r_sel, mask, FAR, x, ALU.mult, ALU.add))
                        x = r_sel

            def take_logits(l, dst, n):
                dve.wait_ge(logit_turned, (l + 1) * NTILE)
                half = NBLK // 2
                for h, bank in ((0, banks[5]), (1, banks[4])):
                    link(V.tensor_copy(dst[:, h * half:(h + 1) * half], bank[:, 0:half * n].rearrange("p (b n) -> p b n", n=n)))

            dve.wait_ge(prefer_ready, E + 8)
            take_logits(0, r_log, E)
            top2(r_log)
            V.tensor_tensor(r_x, r_m2, r_m1, ALU.subtract).then_inc(exp_in, 1)
            V.tensor_tensor(r_w, r_mask1, r_mask2, ALU.add).then_inc(masks_ready, 1)
            dve.wait_ge(exp_done, 1)
            link(V.tensor_scalar(r_z, r_y, 1.0, None, ALU.add))
            g_1, g_2 = (gk[:, c].rearrange("p (b a) -> p b a", a=1) for c in range(2))
            link(V.reciprocal(g_1, r_z))
            link(V.tensor_tensor(g_2, g_1, r_y, ALU.mult))
            by_expert = lambda x: x.rearrange("p (b e) -> p e b", e=E)
            by_block = lambda x: x.rearrange("p e b -> p b e")
            dve.wait_ge(prefix_psum, 1)
            link(V.tensor_copy(r_cnt, by_expert(banks[7][:, 0:NBLK * E])))
            for e in range(E):
                link(V.tensor_tensor_scan(r_inc[:, e], ones[:, 0:NBLK], r_cnt[:, e], 0.0, ALU.mult, ALU.add))
            link(V.tensor_tensor(r_exc, r_inc, r_cnt, ALU.subtract))
            total = r_inc[:, :, NBLK - 1:NBLK]
            link(V.tensor_tensor_scan(r_step, ones[:, 0:NMAX], ones[:, 0:NMAX], 0.0, ALU.mult, ALU.add))
            link(V.tensor_scalar(r_step, r_step, -1.0, float(ET), ALU.add, ALU.mult))
            link(V.tensor_tensor(r_more, total.to_broadcast([P, E, NMAX]),
                                 r_step.rearrange("p (a i) -> p a i", a=1).to_broadcast([P, E, NMAX]), ALU.is_gt))
            link(V.tensor_reduce(r_tile.rearrange("p (e a) -> p e a", a=1), r_more, AX_X, ALU.add))
            link(V.tensor_scalar(r_tile, r_tile, float(ET), None, ALU.mult))
            link(V.tensor_tensor_scan(r_end, ones[:, 0:E], r_tile, 0.0, ALU.mult, ALU.add))
            link(V.tensor_tensor(r_base, r_end, r_tile, ALU.subtract))
            link(V.tensor_tensor(r_eq, banks[6][:, 0:NBLK * E].rearrange("p (b e) -> p b e", e=E), by_block(r_exc), ALU.add))
            link(V.tensor_tensor(r_sel, r_eq, r_base.rearrange("p (a e) -> p a e", a=1).to_broadcast([P, NBLK, E]), ALU.add))
            for c, mask in enumerate((r_mask1, r_mask2)):
                link(V.tensor_tensor(r_tmp, r_sel, mask, ALU.mult))
                link(V.tensor_reduce(r_y, r_tmp, AX_X, ALU.add))
                V.tensor_copy(slots[:, c].rearrange("p (b a) -> p b a", a=1), r_y).then_inc(slots_ready, 1)
                dve.wait_ge(slots_ready, c + 1)
            one = lambda i: etab_f[:, i]
            link(V.tensor_tensor_scan(one(0), ones[0:1, 0:NET], ones[0:1, 0:NET], 0.0, ALU.mult, ALU.add))
            link(V.tensor_scalar(one(1), one(0), float(ET), None, ALU.mult))
            link(V.memset(one(2), 0.0))
            for e in range(E - 1):
                link(V.scalar_tensor_tensor(one(2), one(1), r_end[0:1, e:e + 1], one(2), ALU.is_gt, ALU.add))
            V.tensor_copy(etab[:], one(2)).then_inc(etab_ready, 1)

            S = ffn[0]
            dve.sem_inc(S["out_free"], 1)
            dve.wait_ge(xgT_psum, 1)
            flat = lambda x: x.rearrange("p k c -> p (k c)")
            V.tensor_copy(flat(xgT[:, 0]), banks[6][:]).then_inc(xgT_ready, 1)

            def tile_rows(i, n, n2, first=False, last=False):
                if not last:
                    dve.wait_ge(xgT_psum, n + 2)
                    V.tensor_copy(flat(xgT[:, 1 - i]), banks[6][:]).then_inc(xgT_ready, 1)
                dve.wait_ge(w0_loaded[i], n2 * 64 + 64)
                if not first:
                    dve.wait_ge(yrow_stored[i], n2 * 16)
                dve.wait_ge(S["hid_used"], n * F0 + 2 * F0)
                for m in range(ES):
                    ins = V.tensor_tensor(yrow[:, i, m], banks[4 + m][:, 0:D], b0_row[:, i], ALU.add)
                ins.then_inc(S["out_free"], 1)

            for i in range(2):
                tile_rows(i, i, 0, first=True)
            with dve.Fori(1, NET // 2 - 1) as n2:
                for i in range(2):
                    tile_rows(i, n2 * 2 + i, n2)
            for i in range(2):
                tile_rows(i, NET - 2 + i, NET // 2 - 1, last=i == 1)
            with dve.Fori(0, NBLK // GRING) as b4:
                for q in range(GRING):
                    b = b4 * GRING + q
                    dve.wait_ge(moved[q], MOVED + b4 * 32 + 32)
                    V.tensor_scalar(crow[:, q], grow[:, q, 0], gk[:, 0, bass.ds(b, 1)], None, ALU.mult).then_inc(weighted, 1)
                    dve.wait_ge(weighted, b + 1)
                    V.scalar_tensor_tensor(crow[:, q], grow[:, q, 1], gk[:, 1, bass.ds(b, 1)], crow[:, q], ALU.mult, ALU.add
                                           ).then_inc(crow_ready, 1)
                    dve.wait_ge(crow_psum, b + 1)
                    x_t = XT[:, :, cols_of(b)]
                    V.tensor_tensor(x_t, x_t, banks[6 + q % 2][:, 0:D].rearrange("p (k c) -> p k c", k=KD), ALU.add).then_inc(x_added, 1)
            if not upto("L1c"):
                return
            link(V.tensor_tensor(cent_sq[:], cent[:], cent[:], ALU.mult))
            link(V.tensor_reduce(cent_n[:, 0:1], cent_sq[:], AX_X, ALU.add))
            V.tensor_copy(cent_n[:, 2:3], cent_n[:, 0:1]).then_inc(cent_sum, 1)
            dve.wait_ge(cent_root, 1)
            link(V.tensor_scalar(cent_n[:, 2:3], cent_n[:, 1:2], 1e-12, None, ALU.max))
            link(V.reciprocal(cent_n[:, 3:4], cent_n[:, 2:3]))
            V.tensor_scalar(cent[:], cent[:], cent_n[:, 3:4], None, ALU.mult).then_inc(cent_ready, 1)
            dve.wait_ge(cent_psum, 1)
            for k in range(KD):
                i = V.tensor_copy(rw[:, 2, k, 0:2 * E], banks[3][:, 64 + k * 2 * E:64 + (k + 1) * 2 * E])
            i.then_inc(rw_ready, 1)
            dve.wait_ge(rcol_psum, 1)
            V.tensor_copy(rcol[:], banks[3][0:E, 0:B]).then_inc(rcol_ready, 1)
            dve.wait_ge(w1_loaded, 5 * 16)
            V.tensor_scalar(wsh2, wsh2, 0.5, None, ALU.mult).then_inc(wsh_ready, 1)

            take_logits(1, r_log, E)
            bias = rbias1[:].rearrange("p (a e) -> p a e", a=1).to_broadcast([P, NBLK, E])
            link(V.tensor_tensor(r_w, r_log, bias, ALU.add))
            top2(r_w)
            link(V.tensor_tensor(r_mask1, r_mask1, r_mask2, ALU.add))
            link(V.tensor_tensor(r_sel, r_mask1, r_log, ALU.mult))
            link(V.tensor_reduce(r_x, r_sel, AX_X, ALU.add))
            link(V.tensor_scalar(r_y, r_x, 1e-9, None, ALU.is_gt))
            link(V.tensor_scalar(r_z, r_x, 1e-9, None, ALU.add))
            link(V.reciprocal(r_x, r_z))
            link(V.tensor_tensor(r_x, r_x, r_y, ALU.mult))
            link(V.tensor_scalar(r_y, r_y, -0.5, 0.5, ALU.mult, ALU.add))
            link(V.tensor_tensor(r_sel, r_sel, wide(r_x), ALU.mult))
            link(V.tensor_tensor(r_tmp, r_mask1, wide(r_y), ALU.mult))
            V.tensor_tensor(r_w, r_sel, r_tmp, ALU.add).then_inc(gates_ready, 1)

            S = ffn[1]
            dve.sem_inc(S["out_free"], 1)
            dve.sem_inc(S["hid_ready"], RING)
            with dve.Fori(0, NTILE // 2) as j2:
                for i in range(2):
                    j = j2 * 2 + i
                    for f in range(FS):
                        dve.wait_ge(S["act_hid"], j * N1C + f + 1)
                        V.scalar_tensor_tensor(hid[:, f % RING], hid[:, f % RING], 1.0, banks[2 * f % RING][:], ALU.add,
                                               ALU.mult).then_inc(silu_half, 1)
                        dve.wait_ge(silu_half, j * FS + f + 1)
                        dve.wait_ge(S["up_psum"], j * NU1 + 2 * f + 2)
                        V.tensor_tensor(hid[:, f % RING], hid[:, f % RING], banks[(2 * f + 1) % RING][:], ALU.mult
                                        ).then_inc(S["hid_ready"], 1)
                    dve.wait_ge(g_loaded[i], j2 * 16 + 16)
                    for f in range(FS, N1C):
                        dve.wait_ge(S["act_hid"], j * N1C + f + 1)
                        V.tensor_tensor(hid[:, f % RING], hid[:, f % RING], g1[:, i, (f - FS) // FE], ALU.mult
                                        ).then_inc(S["hid_ready"], 1)
                    dve.wait_ge(S["hid_used"], (j + 1) * N1C + RING)
                    for m in range(KD):
                        ins = V.tensor_scalar(HT[:, m, cols(j)], banks[4 + m][:], 1.0 / 3.0, None, ALU.mult)
                    ins.then_inc(S["out_free"], 1)
                    dve.wait_ge(S["out_free"], j + 2)
                    dve.sem_inc(S["out_done"], 1)
            if not upto("L1"):
                return
            take_logits(2, r_raw, RL)
            V.tensor_copy(r_x, r_raw[:, :, RL - 1:RL]).then_inc(norm_sum, 1)
            dve.wait_ge(norm_root, 1)
            link(V.tensor_scalar(r_z, r_y, 1e-12, None, ALU.max))
            link(V.reciprocal(r_x, r_z))
            link(V.tensor_tensor(r_tmp, r_raw[:, :, 0:E], wide(r_x), ALU.mult))
            link(V.tensor_tensor(r_log, r_tmp, r_raw[:, :, E:2 * E], ALU.add))
            top2(r_log)
            link(V.tensor_tensor(r_mask1, r_log, wide(r_m2), ALU.is_ge))
            V.tensor_tensor(r_sel, r_log, wide(r_m1), ALU.subtract).then_inc(exp_in, 1)
            dve.wait_ge(exp_done, 2)
            link(V.tensor_tensor(r_tmp, r_eq, r_mask1, ALU.mult))
            link(V.tensor_reduce(r_x, r_tmp, AX_X, ALU.add))
            link(V.reciprocal(r_y, r_x))
            V.tensor_tensor(r_w, r_tmp, wide(r_y), ALU.mult).then_inc(gates_ready, 1)

            S = ffn[2]
            dve.sem_inc(S["out_free"], 1)
            dve.sem_inc(S["hid_ready"], RING)
            with dve.Fori(0, NTILE // 2) as j2:
                for i in range(2):
                    j = j2 * 2 + i
                    dve.wait_ge(g_loaded[i], G2 + j2 * 32 + 32)
                    for f in range(E):
                        dve.wait_ge(S["act_hid"], j * E + f + 1)
                        V.tensor_tensor(hid[:, f % RING], hid[:, f % RING], g1[:, i, f], ALU.mult).then_inc(S["hid_ready"], 1)
                    dve.wait_ge(S["hid_used"], (j + 1) * E + RING)
                    for m in range(KD):
                        x_t = XT[:, m, cols(j)]
                        ins = V.tensor_tensor(x_t, x_t, banks[4 + m][:], ALU.add)
                    ins.then_inc(S["out_free"], 1)
                    dve.wait_ge(S["out_free"], j + 2)
                    dve.sem_inc(S["out_done"], 1)
            if not upto("L2c"):
                return
            dve.wait_ge(param_log, 1)
            link(V.tensor_scalar(small2[:, 7:9], small2[:, 0:2], 0.0, None, ALU.max))
            link(V.tensor_tensor(small2[:, 7:9], small2[:, 7:9], small2[:, 5:7], ALU.add))
            link(V.tensor_tensor(small2[:, 9:10], small2[:, 7:8], small2[:, 8:9], ALU.mult))
            link(V.tensor_scalar(small2[:, 10:11], small2[:, 9:10], -1.0, 1.0, ALU.mult, ALU.add))
            link(V.memset(decay[:], 1.0))
            link(V.tensor_scalar(decay[:], decay[:], small2[:, 10:11], None, ALU.mult))
            dt = small2[:, 8:9]
            dve.sem_inc(ssm_taken[0], 1)
            dve.sem_inc(ssm_taken[2], 1)
            with dve.Fori(0, B // 2) as j2:
                for i in range(2):
                    j = j2 * 2 + i
                    cv = hid[:, 2 * i:2 * i + 2]
                    dve.wait_ge(p2_psum, j * 3 + 2)
                    for tap in range(B):
                        order = B - 1 if tap == 0 else tap - 1
                        back = B - 1 - order
                        for k in range(KD):
                            w = condT[:, k, order:order + 1]
                            src = XT[:, k, cols(j, TILE - back)]
                            if tap == 0:
                                ins = V.tensor_scalar(cv[:, k], src, w, cb2[:, k:k + 1], ALU.mult, ALU.add)
                            else:
                                ins = V.scalar_tensor_tensor(cv[:, k, back:], src, w, cv[:, k, back:], ALU.mult, ALU.add)
                            ins.then_inc(conv_step[k], 1)
                        if tap < B - 1:
                            for k in range(KD):
                                dve.wait_ge(conv_step[k], j * B + tap + 1)
                    for k in range(KD):
                        dve.wait_ge(conv_step[k], j * B + B)
                    dve.sem_inc(conv_ready, 1)
                    dve.wait_ge(p2_psum, j * 3 + 1 + 6)
                    V.tensor_scalar(ssm_b[:, cols(j)], banks[0][0:NS], small2[:, 2:3], None, ALU.add).then_inc(ssm_taken[0], 1)
                    dve.wait_ge(p2_psum, j * 3 + 3 + 6)
                    V.tensor_scalar(ssm_u[:, cols(j)], banks[2][0:NS], small2[:, 4:5], dt, ALU.add, ALU.mult).then_inc(ssm_taken[2], 1)
            dve.wait_ge(ssm_taken[0], B + 1)
            dve.wait_ge(ssm_taken[2], B + 1)
            dve.wait_ge(softplus_log, 1)
            link(V.scalar_tensor_tensor(ssm_b, ssm_b, 0.0, ssm, ALU.max, ALU.add))
            link(V.tensor_tensor(ssm_b, ssm_b, ssm_u, ALU.mult))
            dve.wait_ge(ssm_taken[1], B + 1)
            for j in range(B):
                c = slice(j * TILE, (j + 1) * TILE)
                link(V.tensor_tensor_scan(ssm[:, c], decay, ssm_b[:, c], 0.0, ALU.mult, ALU.add))
                V.tensor_tensor(ssm_b[:, c], ssm[:, c], ssm_c[:, c], ALU.mult).then_inc(ssm_y, 1)
            if not upto("L2"):
                return
            dve.wait_ge(w2s_loaded, 12 * 16)
            for g in range(8):
                dve.wait_ge(uT_psum, g + 1)
                V.tensor_scalar(uT[:, g].rearrange("p k m -> p (k m)"), banks[6 + g % 2][:], 0.5 if g >= 4 else 1.0, None,
                                ALU.mult).then_inc(uT_ready, 1)
            dve.wait_ge(ssm_y, B)
            link(V.tensor_scalar(gb2[:, 0:2], gb2[:, 0:2], 0.5, None, ALU.mult))
            link(V.memset(c2, 2.0))
            for k in range(KD):
                ins = V.tensor_scalar(c2[:, k], c2[:, k], cinit[:, k:k + 1], None, ALU.mult).then_inc(cell_init, 1)
            dve.wait_ge(cell_init, 2)
            dve.sem_inc(cell_ready, 2)
            with dve.Fori(0, B) as j:
                for h in range(2):
                    n = j * 2 + h
                    c2h = c2[:, :, h * 256:(h + 1) * 256]
                    tf, ti, tg, a, b = (lstm[:, h, x] for x in range(5))
                    dve.wait_ge(gate2_ready, n * 3 + 3 + 6)
                    V.scalar_tensor_tensor(a, tf, 1.0, c2h, ALU.add, ALU.mult).then_inc(cell_step, 1)
                    V.scalar_tensor_tensor(b, ti, 1.0, tg, ALU.add, ALU.mult).then_inc(cell_step, 1)
                    dve.wait_ge(cell_step, n * 2 + 2)
                    V.scalar_tensor_tensor(c2h, a, 0.5, b, ALU.mult, ALU.add).then_inc(cell_ready, 1)
            dve.wait_ge(cpart_ready, 2)
            dve.sem_inc(o2_sum, 4)
            with dve.Fori(0, B // 2) as j2:
                for i in range(2):
                    for m in range(KD):
                        n = j2 * 4 + i * 2 + m
                        dve.wait_ge(o2_psum, n + 1)
                        dve.wait_ge(o2_added, n + 1)
                        V.tensor_tensor(y2[:, i, m], banks[i * 2 + m][:], cpart[:, m], ALU.add).then_inc(o2_sum, 1)
            if not upto("L3c"):
                return
            dve.wait_ge(w3_loaded, 6 * 16)
            link(V.tensor_scalar(ys3[:], condT[:], 1.0 / 16.0, None, ALU.mult))
            V.tensor_tensor(ysq3[:], ys3[:], ys3[:], ALU.mult).then_inc(d3_in, 1)
            V.tensor_tensor(w3sq, w3c, w3c, ALU.mult).then_inc(d3_in, 1)
            for k in range(KD):
                V.tensor_scalar(wr3b[:, k], ones[:], wr3[:, k:k + 1], None, ALU.mult).then_inc(d3_in, 1)
            dve.wait_ge(d3_psum, 1)
            link(V.tensor_scalar(d3[:].rearrange("p k b -> p (k b)"), banks[6][:, 0:KD * B], 1e-8, None, ALU.add))
            V.reciprocal(d3[:], d3[:]).then_inc(d3_recip, 1)
            dve.wait_ge(o2_added, 2 * B + 4)
            with dve.Fori(0, B // 2) as j2:
                for i in range(2):
                    j = j2 * 2 + i
                    dve.wait_ge(c3_psum, j * 2 + 2)
                    for k in range(KD):
                        V.tensor_scalar(hid[:, 2 * i + k], XT[:, k, cols(j)], ys3[:, k, bass.ds(j, 1)], None, ALU.mult).then_inc(xs3_ready, 1)
            if not upto("L3"):
                return
            S = ffn[3]
            dve.sem_inc(S["out_free"], 1)
            dve.sem_inc(rank_taken, 1)
            dve.sem_inc(o3_ready, 1)
            dve.wait_ge(before_ready, 3)
            with dve.Fori(0, B // 2) as j2:
                for i in range(2):
                    j = j2 * 2 + i
                    dve.wait_ge(s3_row, j + 1)
                    for s in range(NSUB):
                        V.tensor_tensor(smask[:, s], srow[:, s * P:(s + 1) * P], ident[:], ALU.mult).then_inc(own, 1)
                    dve.wait_ge(own, j * 5 + 4)
                    V.tensor_reduce(scol[:], smask[:], AX_X, ALU.add).then_inc(own, 1)
                    dve.wait_ge(own, j * 5 + 5)
                    for s in range(NSUB):
                        V.tensor_scalar(beats[:, 0, s], srow, scol[:, s:s + 1], None, ALU.is_lt)
                        ins = V.scalar_tensor_tensor(beats[:, 1, s], srow, scol[:, s:s + 1], before[:, s], ALU.is_equal, ALU.mult)
                    ins.then_inc(beats_ready, 1)
                    dve.wait_ge(rank_psum, j + 1)
                    V.tensor_scalar(mask3, banks[7][:], float(TOPK3), None, ALU.is_lt).then_inc(mask_ready, 1)
                    dve.wait_ge(mask_ready, j + 1)
                    dve.wait_ge(s3_th, j + 1)
                    V.scalar_tensor_tensor(gate3, th3, 1.0, mask3, ALU.add, ALU.mult).then_inc(rank_taken, 1)
                    dve.wait_ge(rank_taken, j + 2)
                    dve.wait_ge(S["hid_used"], (j + 1) * F3 + RING)
                    dve.wait_ge(o3_psum, j * 2 + 2)
                    for m in range(KD):
                        ins = V.scalar_tensor_tensor(o3[:, i, m], banks[4 + m][:], b3_down[:, m:m + 1], gate3, ALU.add, ALU.mult)
                    ins.then_inc(S["out_free"], 1)
                    dve.wait_ge(S["out_free"], j + 2)
                    V.scalar_tensor_tensor(o3[:, i], o3[:, i], 0.5, XT[:, :, cols(j)], ALU.mult, ALU.add).then_inc(o3_part, 1)
                    dve.wait_ge(o3_part, j + 1)
                    V.tensor_tensor(o3[:, i], o3[:, i], HT[:, :, cols(j)], ALU.add).then_inc(o3_ready, 1)

        @block.tensor
        def _(pe):
            pe.wait_ge(const_ready, 2)
            with pe.Fori(0, B // 2) as j2:
                for i in range(2):
                    pe.wait_ge(x_loaded[i], j2 * 16 + 16)
                    for k in range(KD):
                        pe.wait_ge(xT_copied[k], j2 * 2 + i + 1)
                        for s in range(4):
                            last = nc.tensor.transpose(banks[4 + k][:, s * P:(s + 1) * P],
                                                       xstage[:, i, s, k * P:(k + 1) * P], ident[:])
                        last.then_inc(xT_psum[k], 1)
                    last = nc.tensor.transpose(banks[7][0:P, 0:P], ident[:], ident[:])
                    last.then_inc(x_stage_free, 1)
            pe.wait_ge(gru_b_loaded, 5 * 16)
            for k in range(KD):
                last = nc.tensor.transpose(banks[6][:, k * B:(k + 1) * B], condrow[:, k * P:(k + 1) * P], ident[0:B, 0:B])
            last.then_inc(condT_psum, 1)
            for k in range(KD):
                pe.wait_ge(xT_copied[k], B + 1)
            pe.wait_ge(gru_w_loaded, 7 * 16)
            pe.wait_ge(gru_b_loaded, 5 * 16)
            pe.wait_ge(wsplit, NSPLIT)

            xview = XT[:].rearrange("p k (b t) -> p k t b", b=B)
            NP = STEPS // CHUNK
            W = STEPS * B

            def project(bank, g, it):
                for m in range(KD):
                    o = bank[:, m * W:(m + 1) * W]
                    nc.tensor.matmul(o, gbias[0:1, g, m * P:(m + 1) * P], ones[0:1, 0:W], start=m == 0, stop=False,
                                     skip_group_check=True)
                    for k in range(KD):
                        nc.tensor.matmul(o, wx[:, g, k, m * P:(m + 1) * P], xview[:, k, bass.ds(it * STEPS, STEPS)],
                                         start=False, stop=False, skip_group_check=True)

            def recur(bank, g, width, s, part, wait):
                for a in range(2):
                    if wait:
                        wait(a)
                    for m in range(KD):
                        for k in range(KD):
                            for w in range(2 - a):
                                last = nc.tensor.matmul(bank[:, m * width + s * B:m * width + (s + 1) * B],
                                                        wpart[:, g, w, k, m * P:(m + 1) * P],
                                                        part[:, a, k * B:(k + 1) * B],
                                                        start=False, stop=True, skip_group_check=True)
                return last

            with pe.Fori(0, TURNS) as it:
                project(banks[0], 0, it)
                for s in range(STEPS):
                    n = it * STEPS + s
                    if s % CHUNK == 0:
                        wait = lambda a: pe.wait_ge(e_part, (it * NP + s // CHUNK) * 2 + a + 1)
                    else:
                        wait = lambda a: pe.wait_ge(h_part, (n - 1) * 2 + a + 1)
                    recur(banks[0], 0, W, s, hpart, wait).then_inc(r_psum, 1)
                    if s == 0:
                        project(banks[1], 1, it)
                    recur(banks[1], 1, W, s, hpart, None).then_inc(z_psum, 1)
                    if s == 0:
                        project(banks[2], 2, it)
                        for m in range(KD):
                            nc.tensor.matmul(banks[3][:, m * NP * B:(m + 1) * NP * B], gbias[0:1, 3, m * P:(m + 1) * P],
                                             ones[0:1, 0:NP * B], start=m == 0, stop=False, skip_group_check=True)
                    recur(banks[2], 2, W, s, rhpart, lambda a: pe.wait_ge(rh_part, n * 2 + a + 1)).then_inc(c_psum, 1)
                    if (s + 1) % CHUNK == 0:
                        recur(banks[3], 3, NP * B, s // CHUNK, hpart,
                              lambda a: pe.wait_ge(h_part, n * 2 + a + 1)).then_inc(p_psum, 1)

            if not upto("L0"):
                return
            pe.wait_ge(hist_copied, 2 * TURNS + 2)

            def logits(l, src, n, first, square=None):
                for g in range(NTILE + 1):
                    if g < NTILE:
                        if g >= 2:
                            pe.wait_ge(logitT_ready, first + g - 1)
                        o = banks[6 + g % 2][0:n]
                        for k in range(KD):
                            last = nc.tensor.matmul(o, rw[:, l, k, 0:n], src[:, k, g * TILE:(g + 1) * TILE],
                                                    start=k == 0, stop=k == KD - 1 and square is None)
                        if square is not None:
                            pe.wait_ge(sq_ready, g + 1)
                            for k in range(KD):
                                last = nc.tensor.matmul(o, rsq[:, k], square[:, g % 4, k], start=False, stop=k == KD - 1)
                        last.then_inc(logit_psum, 1)
                    if g >= 1:
                        h = g - 1
                        pe.wait_ge(logitT_ready, first + h + 1)
                        for q in range(NSUB):
                            b = h * NSUB + q
                            half = NBLK // 2
                            o = (banks[5], banks[4])[b // half][:, b % half * n:(b % half + 1) * n]
                            last = nc.tensor.transpose(o, logitT[0:n, h % 2, q * P:(q + 1) * P], ident[0:n, 0:n])
                        last.then_inc(logit_turned, 1)

            def turn_gates(l):
                pe.wait_ge(gates_ready, l)
                flat_w = r_w.rearrange("p b e -> p (b e)")
                for g in range(NTILE):
                    w = NSUB * E
                    last = nc.tensor.transpose(banks[6 + g // 4][0:w, g % 4 * P:(g % 4 + 1) * P], flat_w[:, g * w:(g + 1) * w], ident[:])
                    if g % 4 == 3:
                        last.then_inc(gT_psum, 1)

            def ffn_tile(S, n, src, up, down, j, out_extra=None):
                c0 = j * n
                for f in range(n + LAG):
                    if f < n:
                        pe.wait_ge(S["hid_ready"], c0 + f + 1)
                        for k in range(KD):
                            last = nc.tensor.matmul(banks[f % RING][:], up(f, k), src(k), start=k == 0, stop=k == KD - 1)
                        last.then_inc(S["up_psum"], 1)
                    h = f - LAG
                    if h == 0:
                        pe.wait_ge(S["out_free"], j + 1)
                        if out_extra:
                            out_extra()
                    if h >= 0:
                        pe.wait_ge(S["hid_ready"], c0 + h + 1 + RING)
                        for m in range(KD):
                            last = nc.tensor.matmul(banks[4 + m][:], down(h, m), hid[:, h % RING],
                                                    start=h == 0 and not out_extra, stop=h == n - 1)
                        last.then_inc(S["hid_used"], 1)

            half_of = lambda m: slice(m * P, (m + 1) * P)
            pe.wait_ge(rw_loaded, 9 * 16)
            logits(0, HT, E, 0)
            pe.wait_ge(masks_ready, 1)
            flat_w = r_w.rearrange("p b e -> p (b e)")
            nc.tensor.matmul(banks[6][:, 0:NBLK * E], strict[:], flat_w, start=True, stop=True)
            nc.tensor.matmul(banks[7][:, 0:NBLK * E], ones[:], flat_w, start=True, stop=True).then_inc(prefix_psum, 1)
            for b in range(NBLK):
                if b >= GRING:
                    pe.wait_ge(row_ready, b - GRING + 1)
                for k in range(KD):
                    last = nc.tensor.transpose(banks[b % GRING][:, half_of(k)], HT[:, k, b * P:(b + 1) * P], ident[:])
                last.then_inc(row_psum, 1)

            S = ffn[0]
            pe.sem_inc(S["hid_used"], F0)

            def turn_tile(i, n2):
                pe.wait_ge(xrow_loaded[i], n2 * 16 + 16)
                for k in range(KD):
                    for s in range(ES):
                        last = nc.tensor.transpose(banks[6][:, k * ET + s * P:k * ET + (s + 1) * P], xrow[:, i, s, half_of(k)], ident[:])
                last.then_inc(xgT_psum, 1)

            def expert_tile(i, n, last_tile, n2):
                c0 = n * F0
                pe.wait_ge(w0_loaded[i], n2 * 64 + 64)
                pe.wait_ge(xgT_ready, n + 1)
                for f in range(F0 + LAG):
                    if f < F0:
                        pe.wait_ge(S["hid_ready"], c0 + f + 1)
                        for k in range(KD):
                            last = nc.tensor.matmul(banks[f % RING][:, 0:ET], w0_up[i][:, k, f * P:(f + 1) * P], xgT[:, i, k],
                                                    start=k == 0, stop=k == KD - 1)
                        last.then_inc(S["up_psum"], 1)
                    if f == F0 and not last_tile:
                        turn_tile(1 - i, n2 + i)
                    h = f - LAG
                    if h == 0:
                        pe.wait_ge(S["out_free"], n + 1)
                    if h >= 0:
                        pe.wait_ge(S["hid_ready"], c0 + h + 1 + RING)
                        for m in range(ES):
                            last = nc.tensor.matmul(banks[4 + m][:, 0:D], hid0[:, h, half_of(m)], w0_down[i][:, h],
                                                    start=h == 0, stop=h == F0 - 1)
                        last.then_inc(S["hid_used"], 1)

            turn_tile(0, 0)
            with pe.Fori(0, NET // 2 - 1) as n2:
                for i in range(2):
                    expert_tile(i, n2 * 2 + i, False, n2)
            for i in range(2):
                expert_tile(i, NET - 2 + i, i == 1, NET // 2 - 1)
            with pe.Fori(0, NBLK // GRING) as b4:
                for q in range(GRING):
                    pe.wait_ge(crow_ready, b4 * GRING + q + 1 + GRING)
                    for k in range(KD):
                        last = nc.tensor.transpose(banks[6 + q % 2][:, half_of(k)], crow[:, q, half_of(k)], ident[:])
                    last.then_inc(crow_psum, 1)
            if not upto("L1c"):
                return
            pe.wait_ge(cent_ready, 1)
            for k in range(KD):
                nc.tensor.transpose(banks[3][:, 64 + k * 2 * E:64 + k * 2 * E + E], cent[:, half_of(k)], ident[0:E, 0:E])
                last = nc.tensor.transpose(banks[3][:, 64 + k * 2 * E + E:64 + (k + 1) * 2 * E], route[:, half_of(k)], ident[0:E, 0:E])
            last.then_inc(cent_psum, 1)
            pe.wait_ge(rw_ready, 1)
            for k in range(KD):
                last = nc.tensor.matmul(banks[3][0:E, 0:B], rcond[:, k], condT[:, k], start=k == 0, stop=k == KD - 1)
            last.then_inc(rcol_psum, 1)
            pe.wait_ge(x_added, NBLK)
            logits(1, XT, E, NTILE)
            turn_gates(1)
            pe.wait_ge(w1_loaded, 5 * 16)
            pe.wait_ge(wsh_ready, 1)
            S = ffn[1]
            pe.sem_inc(S["hid_used"], RING)
            with pe.Fori(0, NTILE) as j:
                def chunk_of(u):
                    return u // 2 if u < 2 * FS else u - FS

                def up_unit(u):
                    if u < RING:
                        pe.wait_ge(S["hid_ready"], j * N1C + u + 1)
                    else:
                        pe.wait_ge(S["hid_ready"], j * N1C + chunk_of(u - RING) + 1 + RING)
                    for k in range(KD):
                        if u < 2 * FS:
                            w = (wsh1, wsh3)[u % 2][:, k, u // 2 * P:(u // 2 + 1) * P]
                        else:
                            e, f = divmod(u - 2 * FS, FE)
                            w = w1e[:, e, k, f * P:(f + 1) * P]
                        last = nc.tensor.matmul(banks[u % RING][:], w, XT[:, k, cols(j)], start=k == 0, stop=k == KD - 1)
                    last.then_inc(S["up_psum"], 1)

                def down_chunk(h):
                    if h == 0:
                        pe.wait_ge(S["out_free"], j + 1)
                    pe.wait_ge(S["hid_ready"], j * N1C + h + 1 + RING)
                    for m in range(KD):
                        if h < FS:
                            w = wsh2[:, h, half_of(m)]
                        else:
                            e, f = divmod(h - FS, FE)
                            w = w2e[:, e, f, half_of(m)]
                        last = nc.tensor.matmul(banks[4 + m][:], w, hid[:, h % RING], start=h == 0, stop=h == N1C - 1)
                    last.then_inc(S["hid_used"], 1)

                todo = 0
                for u in range(NU1):
                    up_unit(u)
                    while todo <= chunk_of(u) - (1 if u < 2 * FS else LAG):
                        down_chunk(todo)
                        todo += 1
                while todo < N1C:
                    down_chunk(todo)
                    todo += 1
            if not upto("L1"):
                return
            pe.wait_ge(ffn[1]["out_done"], NTILE)
            logits(2, HT, RL, 2 * NTILE, WB[:, 5760:9856].rearrange("p (n k c) -> p n k c", n=4, k=KD))
            turn_gates(2)
            pe.wait_ge(w1f_loaded, 2 * 16)
            S = ffn[2]
            pe.sem_inc(S["hid_used"], RING)
            with pe.Fori(0, NTILE // 2) as j2:
                for i in range(2):
                    j = j2 * 2 + i

                    def bias_sum():
                        pe.wait_ge(g_loaded[i], G2 + j2 * 32 + 32)
                        for m in range(KD):
                            nc.tensor.matmul(banks[4 + m][:], v2b[:, half_of(m)], g1T[:, i], start=True, stop=False)

                    ffn_tile(S, E, lambda k: HT[:, k, cols(j)], lambda f, k: v1[:, f, k], lambda h, m: v2[:, h, half_of(m)], j,
                             bias_sum)
            if not upto("L2c"):
                return
            pe.wait_ge(ffn[2]["out_done"], NTILE)
            pe.wait_ge(w2_loaded, 3 * 16)
            pe.sem_inc(p2_psum, 6)
            with pe.Fori(0, B // 2) as j2:
                for i in range(2):
                    j = j2 * 2 + i
                    pe.wait_ge(conv_ready, j + 1)
                    for x, w in enumerate((wp2[:, :, 0:NS], wp2[:, :, NS:2 * NS], ws2)):
                        pe.wait_ge(ssm_taken[x], j + 1)
                        for k in range(KD):
                            last = nc.tensor.matmul(banks[x][0:NS], w[:, k], hid[:, 2 * i + k] if x < 2 else XT[:, k, cols(j)],
                                                    start=k == 0, stop=k == KD - 1)
                        last.then_inc(p2_psum, 1)
            for j in range(B):
                pe.wait_ge(ssm_y, j + 1)
                for m in range(KD):
                    n = j * KD + m
                    if n >= 4:
                        pe.wait_ge(z_ready2, n - 3)
                    nc.tensor.matmul(banks[n % 4][:], wo2[:, half_of(m)], ssm_b[:, j * TILE:(j + 1) * TILE], start=True, stop=True
                                     ).then_inc(y_psum, 1)
            if not upto("L2"):
                return
            pe.wait_ge(uraw_loaded, 8 * 16)
            for g in range(8):
                if g >= 2:
                    pe.wait_ge(uT_ready, g - 1)
                for ki in range(KD):
                    for ko in range(KD):
                        last = nc.tensor.transpose(banks[6 + g % 2][:, ki * D + ko * P:ki * D + (ko + 1) * P],
                                                   uraw[:, g, ko, half_of(ki)], ident[:])
                last.then_inc(uT_psum, 1)
            pe.wait_ge(uT_ready, 8)
            pe.wait_ge(z_ready2, 2 * B)
            with pe.Fori(0, B) as j:
                for h in range(2):
                    n = j * 2 + h
                    for part in range(2):
                        if part:
                            pe.wait_ge(cell_ready, n + 1)
                        for g in range(3):
                            if not part:
                                pe.wait_ge(gate2_ready, n * 3 + g + 1)
                            for m in range(KD):
                                for k in range(KD):
                                    src = c2[:, k, h * 256:(h + 1) * 256] if part else HT[:, k, bass.ds(j * TILE + h * 256, 256)]
                                    last = nc.tensor.matmul(banks[h * 3 + g][:, m * 256:(m + 1) * 256],
                                                            uT[:, g + 4 * part, k, half_of(m)], src,
                                                            start=not part and m == 0 and k == 0, stop=part == 1, skip_group_check=True)
                            if part:
                                last.then_inc(gate2_psum, 1)
            pe.wait_ge(cell_ready, 2 * B + 2)
            for m in range(KD):
                for k in range(KD):
                    last = nc.tensor.matmul(banks[6 + m][:], uT[:, 7, k, half_of(m)], c2[:, k], start=k == 0, stop=k == KD - 1)
                last.then_inc(cpart_psum, 1)
            with pe.Fori(0, B // 2) as j2:
                for i in range(2):
                    for m in range(KD):
                        pe.wait_ge(o2_sum, j2 * 4 + i * 2 + m + 1)
                        for k in range(KD):
                            last = nc.tensor.matmul(banks[i * 2 + m][:], uT[:, 3, k, half_of(m)], HT[:, k, cols(j2 * 2 + i)],
                                                    start=k == 0, stop=k == KD - 1)
                        last.then_inc(o2_psum, 1)
            if not upto("L3c"):
                return
            pe.wait_ge(d3_in, 4)
            for m in range(KD):
                for k in range(KD):
                    last = nc.tensor.matmul(banks[6][:, m * B:(m + 1) * B], w3sq[:, k, half_of(m)], ysq3[:, k],
                                            start=k == 0, stop=k == KD - 1)
            last.then_inc(d3_psum, 1)
            pe.sem_inc(c3_psum, 4)
            with pe.Fori(0, B // 2) as j2:
                for i in range(2):
                    j = j2 * 2 + i
                    pe.wait_ge(xs3_ready, j * 2 + 2)
                    for m in range(KD):
                        pe.wait_ge(c3_ready, j * 2 + m + 1)
                        for k in range(KD):
                            last = nc.tensor.matmul(banks[m][:], w3c[:, k, half_of(m)], hid[:, 2 * i + k],
                                                    start=k == 0, stop=k == KD - 1)
                        last.then_inc(c3_psum, 1)
            if not upto("L3"):
                return
            S = ffn[3]
            pe.wait_ge(c3_ready, 2 * B + 2)
            pe.wait_ge(before_ready, 3)
            pe.sem_inc(S["hid_used"], RING)
            pe.sem_inc(o3_psum, 2)

            def turn_out(h, n, slot):
                for s in (2 * h, 2 * h + 1):
                    for m in range(KD):
                        last = nc.tensor.transpose(banks[6][:, (s % 2) * D + m * P:(s % 2) * D + (m + 1) * P],
                                                   o3[:, slot, m, s * P:(s + 1) * P], ident[:])
                last.then_inc(o3_psum, 1)

            with pe.Fori(0, B // 2) as j2:
                for i in range(2):
                    j = j2 * 2 + i
                    pe.wait_ge(otok_ready, j * 2 + 2)
                    for k in range(KD):
                        last = nc.tensor.matmul(banks[6][:], wr3b[:, k], HT[:, k, cols(j)], start=k == 0, stop=k == KD - 1)
                    last.then_inc(s3_psum, 1)
                    ffn_tile(S, F3, lambda k: HT[:, k, cols(j)], lambda f, k: w3_up[:, k, f * P:(f + 1) * P],
                             lambda h, m: w3_down[:, h, half_of(m)], j)
                    pe.wait_ge(o3_ready, j + 1)
                    pe.wait_ge(s3_row, j + 1)
                    turn_out(0, j, 1 - i)
                    pe.wait_ge(beats_ready, j + 1)
                    pe.wait_ge(rank_taken, j + 1)
                    for n in range(2 * NSUB):
                        last = nc.tensor.matmul(banks[7][:], ones16[:], beats[:, n // NSUB, n % NSUB],
                                                start=n == 0, stop=n == 2 * NSUB - 1)
                    last.then_inc(rank_psum, 1)
                    pe.wait_ge(otok_ready, j * 2 + 3)
                    turn_out(1, j, 1 - i)
            pe.wait_ge(o3_ready, B + 1)
            pe.wait_ge(otok_ready, B * 2 + 2)
            turn_out(0, B, 1)
            pe.wait_ge(otok_ready, B * 2 + 3)
            turn_out(1, B, 1)


_OUT_SHAPE = (B, T, D)


def kernel(**inputs):
    from concourse import bacc as _bacc
    from concourse.bass_utils import run_bass_kernel_spmd as _run

    nc = _bacc.Bacc("TRN2", target_bir_lowering=False, num_devices=1)
    arrays, t = {}, {}
    for name, a in inputs.items():
        a = np.ascontiguousarray(a)
        arrays[f"in_{name}"] = a
        t[name] = nc.dram_tensor(f"in_{name}", a.shape, mybir.dt.from_np(a.dtype), kind="ExternalInput").ap()
    out = nc.dram_tensor("out_0", _OUT_SHAPE, F32, kind="ExternalOutput").ap()
    build_program(nc, t, out)
    return _run(nc, [arrays], core_ids=[0]).results[0]["out_0"]
```

```python
from contextlib import ExitStack

import numpy as np

import concourse.bass as bass
from concourse import mybir

F32 = mybir.dt.float32
F16 = mybir.dt.float16
U32 = mybir.dt.uint32
ALU = mybir.AluOpType
ACT = mybir.ActivationFunctionType
AX_X = mybir.AxisListType.X

P = 128
B, T, D = 8, 512, 256
KD = D // P
NTOK = B * T
STEPS = 16
TURNS = T // STEPS
CHUNK = 4
HSCALE = 256.0
WSCALE = 256.0
GSCALE = HSCALE * WSCALE
E = 8
RING = 4
TILE = 512
NTILE = NTOK // TILE
NSUB = TILE // P
FAR = -3.0e38
F0 = 1024 // P
FS = 512 // P
FE = 256 // P
NBLK = NTOK // P
F3 = 1024 // P
ET = 256
NET = (2 * NTOK + E * (ET - 1)) // ET
SIDE = (NET - NET // 2, NET // 2)
SLOTS = NET * ET
GRING = 4
TOPK3 = T // 2
NS = 64


def build_program(nc, t, out):
    ctx = ExitStack()
    with ctx:
        def sb(name, shape, dt=F32):
            return ctx.enter_context(nc.sbuf_tensor(name, shape, dt))

        def sem(name):
            return ctx.enter_context(nc.semaphore(name))

        XT = sb("XT", [P, KD, NTOK])
        HT = sb("HT", [P, KD, NTOK])
        WA = sb("WA", [P, 8192])
        WB = sb("WB", [P, 11264])
        GB = sb("GB", [P, 8192])
        ident = sb("ident", [P, P])
        ones = sb("ones", [P, P])
        condrow = sb("condrow", [B, D])
        condT = sb("condT", [P, KD, B])

        banks = [ctx.enter_context(nc.psum_tensor(f"bank{i}", [P, 512], F32)) for i in range(8)]

        xstage = GB[:].rearrange("p (n s d) -> p n s d", n=B, s=NSUB)
        wx = WB[:, 0:1536].rearrange("p (g k m) -> p g k m", g=3, k=KD)
        wraw = WB[:, 1536:3584].rearrange("p (g k m) -> p g k m", g=4, k=KD)
        wpart = WB[:, 4096:6144].bitcast(F16).rearrange("p (g n k m) -> p g n k m", g=4, n=2, k=KD)
        gbias = sb("gbias", [1, 4, D])
        hid = sb("hid", [P, RING, TILE])
        hidf = hid[:].rearrange("p r c -> p (r c)")
        w0 = [WB[:, i * 4096:(i + 1) * 4096] for i in range(2)]
        w0_up = [w[:, 0:2048].rearrange("p (k f) -> p k f", k=KD) for w in w0]
        w0_down = [w[:, 2048:4096].rearrange("p (f d) -> p f d", f=F0) for w in w0]
        b0_up = sb("b0_up", [P, 2, F0])
        ES = ET // P
        hid0 = hidf.rearrange("p (f c) -> p f c", f=F0)
        xrow = WA[:, 0:1024].rearrange("p (n s d) -> p n s d", n=2, s=ES)
        xgT = WA[:, 1024:2048].rearrange("p (n k c) -> p n k c", n=2, k=KD)
        yrow = WA[:, 2048:3072].rearrange("p (n s d) -> p n s d", n=2, s=ES)
        b0_row = WA[:, 3072:3584].rearrange("p (n d) -> p n d", n=2)
        hrow = WA[:, 3584:4608].rearrange("p (n d) -> p n d", n=GRING)
        grow = WA[:, 4608:6656].rearrange("p (n c d) -> p n c d", n=GRING, c=2)
        crow = WA[:, 6656:7680].rearrange("p (n d) -> p n d", n=GRING)
        ZW = SLOTS * D // P // 4
        zeros = WA[:, 0:ZW]
        strict = sb("strict", [P, P])
        gk = sb("gk", [P, 2, NBLK])
        slots = sb("slots", [P, 2, NBLK], U32)
        etab_f = sb("etab_f", [1, 3, NET])
        etab = sb("etab", [1, NET], U32)
        xg = nc.dram_tensor("tile_rows", [SLOTS, D], F32, kind="Internal").ap()
        yg = nc.dram_tensor("expert_rows", [SLOTS, D], F32, kind="Internal").ap()
        RL = 17
        logitT = hid[0:RL, 0:2]
        gT = hid[0:NSUB * E, 2:4].rearrange("p r (g c) -> p (r g) c", c=P)
        rw = sb("rw", [P, 3, KD, RL])
        rsq = sb("rsq", [P, KD, RL])
        rcond = sb("rcond", [P, KD, E])
        rcol = sb("rcol", [E, B])
        rbias0 = sb("rbias0", [E, 1])
        rbias1 = sb("rbias1", [P, E])
        def rt(i, n=E):
            o = i * NBLK * E
            return GB[:, o:o + NBLK * n].rearrange("p (b n) -> p b n", n=n)
        r_log, r_sel, r_eq, r_mask1, r_mask2, r_w, r_tmp = (rt(i) for i in range(7))
        r_m1, r_m2, r_p1, r_p2, r_x, r_y, r_z = (rt(7 + i, 1) for i in range(7))
        r_raw = GB[:, 4096:4096 + NBLK * RL].rearrange("p (b n) -> p b n", n=RL)
        r_cnt, r_inc, r_exc = (GB[:, 4096 + i * 256:4352 + i * 256].rearrange("p (e b) -> p e b", e=E) for i in range(3))
        r_tile, r_end, r_base = (GB[:, 4864 + i * E:4872 + i * E] for i in range(3))
        NMAX = NTOK // ET
        r_step = GB[:, 4896:4896 + NMAX]
        r_more = GB[:, 4928:4928 + E * NMAX].rearrange("p (e i) -> p e i", e=E)
        prefer = sb("prefer", [P, E])
        cent = sb("cent", [E, D])
        cent_sq = sb("cent_sq", [E, D])
        cent_n = sb("cent_n", [E, 4])
        route = sb("route", [E, D])
        wsh1 = WB[:, 0:1024].rearrange("p (k f) -> p k f", k=KD)
        wsh3 = WB[:, 1024:2048].rearrange("p (k f) -> p k f", k=KD)
        wsh2 = WB[:, 2048:3072].rearrange("p (f d) -> p f d", f=FS)
        w1e = WB[:, 3072:7168].rearrange("p (e k f) -> p e k f", e=E, k=KD)
        w2e = WB[:, 7168:11264].rearrange("p (e f d) -> p e f d", e=E, f=FE)
        xblk = GB[:, 5632:6656].rearrange("p (n k c) -> p n k c", n=GRING, k=KD)
        w1_up = [GB[:, 5632 + i * 512:6144 + i * 512].rearrange("p (k f) -> p k f", k=KD) for i in range(2)]
        w1_down = [GB[:, 6656 + i * 512:7168 + i * 512].rearrange("p (f d) -> p f d", f=FE) for i in range(2)]
        g1 = GB[:].rearrange("p (n e c) -> p n e c", n=2, e=E)
        v1 = WA[:, 0:2048].rearrange("p (e k f) -> p e k f", e=E, k=KD)
        v2 = WA[:, 2048:4096].rearrange("p (e d) -> p e d", e=E)
        v1b = sb("v1b", [P, E])
        v2b = sb("v2b", [E, D])
        g1T = sb("g1T", [E, 2, TILE])
        uraw = WA[:, 4096:8192].rearrange("p (g k m) -> p g k m", g=8, k=KD)
        uT = WA[:, 0:4096].rearrange("p (g k m) -> p g k m", g=8, k=KD)
        wp2 = WB[:, 5120:5376].rearrange("p (k m) -> p k m", k=KD)
        ws2 = WB[:, 5376:5504].rearrange("p (k m) -> p k m", k=KD)
        wo2 = WB[0:NS, 5504:5760]
        ssm = WB[0:NS, 6144:10240]
        ssm_c, ssm_b, ssm_u = GB[0:NS, 0:4096], GB[0:NS, 4096:8192], HT[0:NS, 0]
        small2 = sb("small2", [NS, 12])
        cb2 = sb("cb2", [P, KD])
        bo2 = sb("bo2", [P, KD])
        decay = WB[0:NS, 10240:10752]
        gb2 = sb("gb2", [P, 4, KD])
        cinit = sb("cinit", [P, KD])
        c2 = WB[:, 7168:8192].rearrange("p (k c) -> p k c", k=KD)
        lstm = GB[:, 0:5120].rearrange("p (h g k c) -> p h g k c", h=2, g=5, k=KD)
        y2 = GB[:, 5120:7168].rearrange("p (n k c) -> p n k c", n=2, k=KD)
        cpart = WB[:, 8192:9216].rearrange("p (k c) -> p k c", k=KD)
        w3_up = WB[:, 0:2048].rearrange("p (k f) -> p k f", k=KD)
        w3_down = WB[:, 2048:4096].rearrange("p (f d) -> p f d", f=F3)
        w3c = WB[:, 4096:4608].rearrange("p (k m) -> p k m", k=KD)
        w3sq = WB[:, 4608:5120].rearrange("p (k m) -> p k m", k=KD)
        b3_up = sb("b3_up", [P, F3])
        ys3 = sb("ys3", [P, KD, B])
        ysq3 = sb("ysq3", [P, KD, B])
        d3 = sb("d3", [P, KD, B])
        wr3 = sb("wr3", [P, KD])
        wr3b = sb("wr3b", [P, KD, P])
        srow = GB[:, 0:1024].rearrange("p (n c) -> p n c", n=2)
        smask = GB[:, 1024:1536].rearrange("p (s c) -> p s c", s=NSUB)
        beats = GB[:, 1536:2560].bitcast(F16).rearrange("p (s c) -> p s c", s=NSUB)
        ties = GB[:, 2560:2816].bitcast(F16).rearrange("p (s c) -> p s c", s=NSUB)
        first_row = GB[:, 2816:2820]
        rank = GB[:, 2820:2824]
        pick = GB[:, 2824:2828]
        b3_row = WA[:, 3072:3328]
        zeros3 = WA[:, 4608:5120].rearrange("p (s d) -> p s d", s=ES)
        back = GB[:].rearrange("p (b d) -> p b d", d=D)
        scol = sb("scol", [P, NSUB])
        sgate = sb("sgate", [P, 2, NSUB])
        ones16 = sb("ones16", [P, P], F16)
        gdram = nc.dram_tensor("gates", [E, NTOK], F32, kind="Internal").ap()
        unscale = sb("unscale", [P, STEPS // 2, KD, B])
        hist = sb("hist", [P, STEPS, KD * B])
        entry = sb("entry", [P, KD * B])
        entry_s = sb("entry_s", [P, KD * B])
        hpart = sb("hpart", [P, 2, KD * B], F16)
        rhpart = sb("rhpart", [P, 2, KD * B], F16)
        rfull = sb("rfull", [P, KD * B])
        gate_r = sb("gate_r", [P, KD * B])
        gate_z = sb("gate_z", [P, KD * B])
        cand = sb("cand", [P, KD * B])
        keep = sb("keep", [P, KD * B])
        keep_h = sb("keep_h", [P, KD * B])
        upd = sb("upd", [P, KD * B])

        const_ready = sem("const_ready")
        ident_zero = sem("ident_zero")
        x_loaded = [sem(f"x_loaded{i}") for i in range(B // 2)]
        xT_psum = [sem(f"xT_psum{k}") for k in range(KD)]
        xT_copied = [sem(f"xT_copied{k}") for k in range(KD)]
        gru_w_loaded = sem("gru_w_loaded")
        gru_b_loaded = sem("gru_b_loaded")
        wsplit, wsplit_high = sem("wsplit"), sem("wsplit_high")
        condT_psum = sem("condT_psum")
        condT_ready = sem("condT_ready")
        r_psum, z_psum, c_psum, p_psum = (sem(f"{n}_psum") for n in "rzcp")
        r_ready, z_ready, c_ready, p_ready = (sem(f"{n}_ready") for n in "rzcp")
        rh_part, rh_full = sem("rh_part"), sem("rh_full")
        h_part, h_full = sem("h_part"), sem("h_full")
        e_part, e_full = sem("e_part"), sem("e_full")
        keep_ready, keep_h_ready, upd_ready = sem("keep_ready"), sem("keep_h_ready"), sem("upd_ready")
        hist_copied = sem("hist_copied")
        vc, ac = sem("vector_link"), sem("scalar_link")
        prefer_ready = sem("prefer_ready")
        xg_zeroed = sem("xg_zeroed")
        masks_ready, prefix_psum, slots_ready, etab_ready = (
            sem(n) for n in ("masks_ready", "prefix_psum", "slots_ready", "etab_ready"))
        row_psum, row_ready = sem("row_psum"), sem("row_ready")
        moved = [sem(f"rows_moved{i}") for i in range(GRING)]
        xrow_loaded = [sem(f"xrow_loaded{i}") for i in range(2)]
        yrow_stored = [sem(f"yrow_stored{i}") for i in range(2)]
        xgT_psum, xgT_ready = sem("xgT_psum"), sem("xgT_ready")
        weighted, crow_ready, crow_psum, x_added = (sem(n) for n in ("weighted", "crow_ready", "crow_psum", "x_added"))
        rw_loaded = sem("rw_loaded")
        rw_ready = sem("rw_ready")
        rcol_psum = sem("rcol_psum")
        rcol_ready = sem("rcol_ready")
        cent_psum = sem("cent_psum")
        logit_psum, logitT_ready, logit_turned = sem("logit_psum"), sem("logitT_ready"), sem("logit_turned")
        sq_ready = sem("sq_ready")
        gates_ready, gT_psum, gT_ready, gates_stored = (sem(n) for n in ("gates_ready", "gT_psum", "gT_ready", "gates_stored"))
        w0_loaded = [sem(f"w0_loaded{i}") for i in range(2)]
        g_loaded = [sem(f"g_loaded{i}") for i in range(2)]
        ffn = [{n: sem(f"ffn{i}_{n}") for n in ("up_psum", "hid_ready", "hid_used", "out_free")
                + (("act_hid", "out_done") if 1 <= i <= 2 else ())}
               for i in range(4)]
        w1_loaded, w1f_loaded, w2_loaded, w3_loaded = (sem(n) for n in ("w1_loaded", "w1f_loaded", "w2_loaded", "w3_loaded"))
        wsh_ready = sem("wsh_ready")
        xblk_ready, up_copied, down_copied = sem("xblk_ready"), sem("up_copied"), sem("down_copied")
        p2_psum, ssm_taken = sem("p2_psum"), [sem(f"ssm_taken{i}") for i in range(3)]
        softplus_log, ssm_y, y_psum, z_ready2 = sem("softplus_log"), sem("ssm_y"), sem("y_psum"), sem("z_ready2")
        param_log = sem("param_log")
        uT_psum, uT_ready = sem("uT_psum"), sem("uT_ready")
        gate2_psum, gate2_ready, cell_ready = sem("gate2_psum"), sem("gate2_ready"), sem("cell_ready")
        cpart_psum, cpart_ready = sem("cpart_psum"), sem("cpart_ready")
        o2_psum, o2_sum, o2_tanh, o2_added = (sem(n) for n in ("o2_psum", "o2_sum", "o2_tanh", "o2_added"))
        d3_psum, d3_recip, d3_ready = sem("d3_psum"), sem("d3_recip"), sem("d3_ready")
        xs3_ready, c3_psum, c3_ready = sem("xs3_ready"), sem("c3_psum"), sem("c3_ready")
        s3_psum, s3_row, s3_th, beats_ready, rank_psum, ranked = (
            sem(n) for n in ("s3_psum", "s3_row", "s3_th", "beats_ready", "rank_psum", "ranked"))
        xh_sum, base_psum, base_ready, b3_loaded, rest_zero, out_rows, stored = (
            sem(n) for n in ("xh_sum", "base_psum", "base_ready", "b3_loaded", "rest_zero", "out_rows", "stored"))
        exp_in, exp_done = sem("exp_in"), sem("exp_done")
        cent_sum, cent_root, cent_ready = sem("cent_sum"), sem("cent_root"), sem("cent_ready")
        norm_sum, norm_root = sem("norm_sum"), sem("norm_root")
        silu_half = sem("silu_half")
        conv_step = [sem(f"conv_step{k}") for k in range(KD)]
        cell_step = sem("cell_step")
        d3_in, own = sem("d3_in"), sem("own")
        w2s_loaded, uraw_loaded = sem("w2s_loaded"), sem("uraw_loaded")

        S1 = 3
        SB = 2 * FS
        NU1 = 2 * FS
        UP0 = NET * F0
        READY0 = UP0 + RING
        USED0 = UP0 + F0
        MOVED = 32 * NBLK // GRING
        ROWS3 = 2 * NET
        BLK3 = 2 * NBLK
        MOVED3 = 4 * MOVED
        HB = B // 2
        LAG = 2

        def cols(j, n=TILE):
            return bass.ds(j * TILE, n)

        def cols_of(b):
            return bass.ds(b * P, P)

        class Link:

            def __init__(self, eng, link_sem):
                self.eng, self.sem, self.n = eng, link_sem, 0

            def __call__(self, ins):
                ins.then_inc(self.sem, 1)
                self.n += 1
                self.eng.wait_ge(self.sem, self.n)

        NSPLIT = 4 + 3 + 1
        wscale = lambda g: WSCALE / (2 if g == 2 else 1)

        block = ctx.enter_context(nc.Block())

        @block.sync
        def _(sp):
            xrows = t["x"].rearrange("b (s p) d -> p b s d", p=P)
            def load_x(j):
                sp.dma_start(xstage[:, j], xrows[:, j]).then_inc(x_loaded[j // 2], 16)

            for j in range(B // 2):
                load_x(j)
            sp.dma_start(condrow[:], t["cond_1024"]).then_inc(gru_b_loaded, 16)
            for g, n in enumerate(("Wr", "Wz", "Wh")):
                w = t["L0_cond_" + n].rearrange("(k p) m -> p k m", p=P)
                sp.dma_start(wx[:, g], w[:, 0:KD]).then_inc(gru_w_loaded, 16)
                sp.dma_start(wraw[:, g], w[:, KD:]).then_inc(gru_w_loaded, 16)
            sp.dma_start(wraw[:, 3], t["L0_cond_Wp"].rearrange("(k p) m -> p k m", p=P)).then_inc(gru_w_loaded, 16)
            for g, n in enumerate(("br", "bz", "bh", "bp")):
                sp.dma_start(gbias[0:1, g], t["L0_cond_" + n].rearrange("(a m) -> a m", a=1)).then_inc(gru_b_loaded, 16)
            for j in range(B // 2, B):
                load_x(j)

            def column(dst, src):
                return sp.dma_start(dst, src, allow_slow_non_contiguous=True)

            def load_expert(i, e):
                one = bass.ds(e, 1)
                sp.dma_start(w0_up[i], t["L0_ffn_w1"].rearrange("e (k p) f -> p e k f", p=P)[:, one]).then_inc(w0_loaded[i], 16)
                sp.dma_start(w0_down[i], t["L0_ffn_w2"].rearrange("e (f p) d -> p e f d", p=P)[:, one]).then_inc(w0_loaded[i], 16)
                column(b0_up[:, i], t["L0_ffn_b1"].rearrange("e (f p) -> p e f", p=P)[:, one]).then_inc(w0_loaded[i], 16)
                sp.dma_start(b0_row[:, i], t["L0_ffn_b2"][one].partition_broadcast(P)).then_inc(w0_loaded[i], 16)

            sp.dma_start(rw[:, 0, :, 0:E], t["L0_ffn_gate_w"].rearrange("(k p) e -> p k e", p=P)).then_inc(rw_loaded, 16)
            column(rbias0[:], t["L0_ffn_gate_b"].rearrange("(e a) -> e a", a=1)).then_inc(rw_loaded, 16)
            r1 = t["L1_cond_router_W"].rearrange("(h k p) e -> p h k e", p=P, h=2)
            sp.dma_start(rw[:, 1, :, 0:E], r1[:, 0]).then_inc(rw_loaded, 16)
            sp.dma_start(rcond[:], r1[:, 1]).then_inc(rw_loaded, 16)
            sp.dma_start(rbias1[:], t["L1_cond_router_bias"].rearrange("(a e) -> a e", a=1).partition_broadcast(P)).then_inc(rw_loaded, 16)
            sp.dma_start(cent[:], t["L1_ffn_centroids"]).then_inc(rw_loaded, 16)
            sp.dma_start(route[:], t["L1_ffn_w_route"]).then_inc(rw_loaded, 16)
            column(v1b[:], t["L1_ffn_b1"].rearrange("e p -> p e")).then_inc(rw_loaded, 16)
            sp.dma_start(v2b[:], t["L1_ffn_b2"]).then_inc(rw_loaded, 16)
            halves = lambda name: t[name].rearrange("(k p) -> p k", p=P)
            col = lambda name, a, n: t[name].rearrange("(p a) -> p a", a=1)[a:a + n]
            column(cb2[:], halves("L2_cond_conv_b")).then_inc(w2s_loaded, 16)
            column(bo2[:], halves("L2_cond_bo")).then_inc(w2s_loaded, 16)
            for i, (name, a) in enumerate((("L2_cond_A_log", 0), ("L2_cond_dt_log", 0), ("L2_cond_bp", 0),
                                           ("L2_cond_bp", NS), ("L2_cond_bs", 0))):
                column(small2[:, i:i + 1], col(name, a, NS)).then_inc(w2s_loaded, 16)
            for g, name in enumerate(("bf", "bi", "bc", "bo")):
                column(gb2[:, g], halves("L2_ffn_" + name)).then_inc(w2s_loaded, 16)
            column(cinit[:], halves("L2_ffn_in_c")).then_inc(w2s_loaded, 16)
            column(b3_up[:], t["L3_ffn_b1"].rearrange("(f p) -> p f", p=P)).then_inc(w3_loaded, 16)
            column(wr3[:], halves("L3_ffn_w_router")).then_inc(w3_loaded, 16)

            sp.wait_ge(prefer_ready, E + 8)
            zrows = xg.rearrange("(p n) d -> p (n d)", p=P)
            for i in range(4):
                sp.dma_start(zrows[:, i * ZW:(i + 1) * ZW], zeros).then_inc(xg_zeroed, 16)

            def load_rows(i, n):
                sp.dma_start(xrow[:, i], xg.rearrange("(n s p) d -> p n s d", p=P, s=ES)[:, bass.ds(n, 1)]).then_inc(xrow_loaded[i], 16)

            def load_tile(i, n, wait):
                if wait:
                    sp.wait_ge(xgT_psum, n - 1)
                load_rows(i, n)
                if wait:
                    sp.wait_ge(ffn[0]["out_free"], n)
                load_expert(i, sp.value_load(etab[0:1, bass.ds(n, 1)], min_val=0, max_val=E - 1))

            sp.wait_ge(etab_ready, 1)
            for q in range(GRING):
                sp.wait_ge(moved[q], MOVED)
            for i in range(2):
                load_tile(i, i, False)
            with sp.Fori(1, NET // 2) as n2:
                for i in range(2):
                    load_tile(i, n2 * 2 + i, True)
            load_tile(0, NET - 1, True)
            sp.wait_ge(ffn[0]["out_free"], NET + 1)
            for dst, name in ((wsh1, "w1"), (wsh3, "w3"), (wsh2, "w2")):
                sp.dma_start(dst, t["L1_cond_" + name].rearrange("(k p) f -> p k f", p=P)).then_inc(w1_loaded, 16)

            def store_gates():
                sp.wait_ge(gT_ready, 2)
                rows = gdram.rearrange("e (g q c) -> q e g c", q=NSUB, c=P)
                for q in range(NSUB):
                    sp.dma_start(rows[q], gT[q * E:(q + 1) * E]).then_inc(gates_stored, 16)
                sp.wait_ge(gates_stored, 16 * NSUB)

            def load_gates(i, j):
                src = gdram[:, cols(j)]
                sp.dma_start(g1[:, i], src.partition_broadcast(P)).then_inc(g_loaded[i], 16)
                sp.dma_start(g1T[:, i], src).then_inc(g_loaded[i], 16)

            sp.wait_ge(x_added, NBLK)
            sp.dma_start(w1e, t["L1_cond_W1e"].rearrange("e (k p) f -> p e k f", p=P)).then_inc(w1_loaded, 16)
            sp.dma_start(w2e, t["L1_cond_W2e"].rearrange("e (f p) d -> p e f d", p=P)).then_inc(w1_loaded, 16)

            for q in range(GRING):
                sp.wait_ge(moved[q], 3 * MOVED)
            for i in range(2):
                load_rows(i, i)
            with sp.Fori(1, NET // 2) as n2:
                for i in range(2):
                    sp.wait_ge(xgT_psum, NET + n2 * 2 + i - 1)
                    load_rows(i, n2 * 2 + i)
            sp.wait_ge(xgT_psum, NET + NET - 2)
            load_rows(0, NET - 1)
            sp.wait_ge(x_added, 2 * NBLK)
            sp.dma_start(v1, t["L1_ffn_w1"].rearrange("e (k p) f -> p e k f", p=P)).then_inc(w1f_loaded, 16)
            sp.dma_start(v2, t["L1_ffn_w2"].rearrange("e p d -> p e d")).then_inc(w1f_loaded, 16)
            for g, name in enumerate(("wf", "wi", "wc", "wo", "uf", "ui", "uc", "uo")):
                sp.dma_start(uraw[:, g], t["L2_ffn_" + name].rearrange("(k p) m -> p k m", p=P)).then_inc(uraw_loaded, 16)
            sp.dma_start(w3_up, t["L3_ffn_W1"].rearrange("(k p) f -> p k f", p=P)).then_inc(w3_loaded, 16)
            sp.dma_start(w3_down, t["L3_ffn_W2"].rearrange("(f p) d -> p f d", p=P)).then_inc(w3_loaded, 16)
            sp.dma_start(w3c, t["L3_cond_weight"].rearrange("(k p) d -> p k d", p=P)).then_inc(w3_loaded, 16)
            sp.dma_start(wp2, t["L2_cond_Wp"].rearrange("(k p) d -> p k d", p=P)).then_inc(w2_loaded, 16)
            sp.dma_start(ws2, t["L2_cond_Ws"].rearrange("(k p) d -> p k d", p=P)).then_inc(w2_loaded, 16)
            sp.dma_start(wo2, t["L2_cond_Wo"]).then_inc(w2_loaded, 16)
            store_gates()
            for i in range(2):
                load_gates(i, i)
            with sp.Fori(1, NTILE // 2) as j2:
                for i in range(2):
                    sp.wait_ge(ffn[2]["out_done"], j2 * 2 + i - 1)
                    load_gates(i, j2 * 2 + i)
            sp.wait_ge(ffn[2]["out_done"], NTILE)
            picked = lambda x: x[0:NTOK].rearrange("(b n s p) d -> p b n s d", b=B, s=ES, p=P)
            sp.wait_ge(prefer_ready, E + 9)
            sp.dma_start(b3_row, t["L3_ffn_b2"].rearrange("(a d) -> a d", a=1).partition_broadcast(P)).then_inc(b3_loaded, 16)
            with sp.Fori(0, B) as j:
                sp.dma_start(picked(yg)[:, bass.ds(j, 1), 1], zeros3).then_inc(rest_zero, 16)
            orows = out.rearrange("b (k s p) d -> p b k s d", k=KD, p=P)

            def store_batch(j):
                sp.wait_ge(out_rows, j + 1)
                for k in range(KD):
                    sp.dma_start(orows[:, j, k], HT[:, k, j * TILE:(j + 1) * TILE]).then_inc(stored, 16)

            for j in range(B):
                for q in range(GRING):
                    sp.wait_ge(moved[q], MOVED3 + 16 * (j + 1))
                if j >= 2:
                    sp.wait_ge(xgT_psum, ROWS3 + j - 1)
                sp.dma_start(xrow[:, j % 2], picked(xg)[:, j, 0]).then_inc(xrow_loaded[j % 2], 16)
                if j >= 4:
                    store_batch(j - 4)
            for j in range(B - 4, B):
                store_batch(j)
            sp.wait_ge(stored, B * KD * 16)

        @block.gpsimd
        def _(pool):
            nc.gpsimd.memset(ident[:], 0.0).then_inc(ident_zero, 1)
            nc.gpsimd.memset(ones[:], 1.0).then_inc(const_ready, 1)
            for e in range(E):
                nc.gpsimd.memset(prefer[:, e:e + 1], float(E - e)).then_inc(prefer_ready, 1)
            nc.gpsimd.memset(unscale[:], 1.0 / HSCALE).then_inc(prefer_ready, 1)
            nc.gpsimd.memset(rw[:, 2], 0.0).then_inc(prefer_ready, 1)
            nc.gpsimd.memset(rsq[:], 0.0).then_inc(prefer_ready, 1)
            nc.gpsimd.memset(ones16[:], 1.0).then_inc(prefer_ready, 1)
            nc.gpsimd.memset(strict[:], 1.0).then_inc(prefer_ready, 1)
            nc.gpsimd.memset(zeros, 0.0).then_inc(prefer_ready, 1)
            pool.wait_ge(prefer_ready, E + 6)
            nc.gpsimd.affine_select(out=strict[:], in_=strict[:], compare_op=ALU.is_gt, fill=0.0, base=0,
                                    pattern=[[1, P]], channel_multiplier=-1).then_inc(prefer_ready, 1)
            nc.gpsimd.memset(rsq[:, :, RL - 1:RL], 1.0).then_inc(prefer_ready, 1)
            pool.wait_ge(ident_zero, 1)
            nc.gpsimd.affine_select(out=ident[:], in_=ident[:], compare_op=ALU.not_equal, fill=1.0, base=0,
                                    pattern=[[-1, P]], channel_multiplier=1).then_inc(const_ready, 1)
            pool.sem_inc(hist_copied, 2)
            hview = HT[:].rearrange("p k (b t) -> p t k b", b=B)
            with pool.Fori(0, TURNS) as it:
                for half in range(2):
                    n = STEPS // 2
                    pool.wait_ge(h_full, it * STEPS + (half + 1) * n)
                    nc.gpsimd.tensor_tensor(hview[:, bass.ds(it * STEPS + half * n, n)],
                                            hist[:, half * n:(half + 1) * n].rearrange("p s (k b) -> p s k b", k=KD),
                                            unscale[:], ALU.mult).then_inc(hist_copied, 1)

            yrows = yg.rearrange("(n s p) d -> p n s d", p=P, s=ES)

            def exchange(l):
                pool.wait_ge(slots_ready, 2 * l + 2)
                for b in range(NBLK):
                    q = b % GRING
                    pool.wait_ge(row_ready, l * NBLK + b + 1)
                    for c in range(2):
                        nc.gpsimd.indirect_dma_start(xg, bass.IndirectOffsetOnAxis(ap=slots[:, c, b:b + 1], axis=0),
                                                     hrow[:, q], None).then_inc(moved[q], 16)

                def store_tile(i, n):
                    pool.wait_ge(ffn[0]["out_free"], l * NET + n + 2)
                    nc.gpsimd.dma_start(yrows[:, bass.ds(n, 1)], yrow[:, i]).then_inc(yrow_stored[i], 16)

                with pool.Fori(0, NET // 2) as n2:
                    for i in range(2):
                        store_tile(i, n2 * 2 + i)
                store_tile(0, NET - 1)
                for i in range(2):
                    pool.wait_ge(yrow_stored[i], (l + 1) * 16 * SIDE[i])
                if l == 0:
                    pool.sem_inc(crow_ready, GRING)
                for b in range(NBLK):
                    q = b % GRING
                    pool.wait_ge(crow_ready, l * NBLK + b + 1)
                    for c in range(2):
                        nc.gpsimd.indirect_dma_start(grow[:, q, c], None, yg,
                                                     bass.IndirectOffsetOnAxis(ap=slots[:, c, b:b + 1], axis=0)).then_inc(moved[q], 16)

            pool.wait_ge(xg_zeroed, 16 * 4)
            exchange(0)
            exchange(1)
            pool.sem_inc(o2_added, 4)
            with pool.Fori(0, NTILE // 2) as j2:
                for i in range(2):
                    for m in range(KD):
                        n = j2 * 4 + i * 2 + m
                        pool.wait_ge(o2_tanh, n + 1)
                        x_t = XT[:, m, cols(j2 * 2 + i)]
                        nc.gpsimd.tensor_tensor(x_t, x_t, y2[:, i, m], ALU.add).then_inc(o2_added, 1)
            pool.wait_ge(o2_added, 2 * B + 4)
            nc.gpsimd.memset(zeros3, 0.0).then_inc(prefer_ready, 1)
            for b in range(NBLK):
                pool.wait_ge(ranked, b // NSUB + 1)
                pool.wait_ge(row_ready, BLK3 + b // 2 + 1)
                nc.gpsimd.indirect_dma_start(xg, bass.IndirectOffsetOnAxis(ap=slots[:, 0, b:b + 1], axis=0),
                                             hrow[:, b % GRING], None).then_inc(moved[b % GRING], 16)
            pool.wait_ge(rest_zero, 16 * B)
            picked = yg[0:NTOK].rearrange("(b n s p) d -> p b n s d", b=B, s=ES, p=P)
            for j in range(B):
                pool.wait_ge(ffn[3]["out_free"], j + 2)
                nc.gpsimd.dma_start(picked[:, j, 0], yrow[:, j % 2]).then_inc(yrow_stored[j % 2], 16)
                pool.wait_ge(yrow_stored[j % 2], (2 * SIDE[j % 2] + j // 2 + 1) * 16)
                for b in range(j * NSUB, (j + 1) * NSUB):
                    nc.gpsimd.indirect_dma_start(back[:, b], None, yg,
                                                 bass.IndirectOffsetOnAxis(ap=slots[:, 0, b:b + 1], axis=0)
                                                 ).then_inc(moved[b % GRING], 16)

        @block.scalar
        def _(act):
            act.wait_ge(gru_w_loaded, 7 * 16)
            for g in range(4):
                nc.scalar.mul(wpart[:, g, 0], wraw[:, g], wscale(g)).then_inc(wsplit_high, 1)
            for g in range(3):
                nc.scalar.mul(wx[:, g], wx[:, g], GSCALE).then_inc(wsplit, 1)

            def gate_in(b, s):
                return b[:, 0:2 * STEPS * B].rearrange("p (m c) -> p m c", m=KD)[:, :, s * B:(s + 1) * B]

            def flat(x):
                return x[:].rearrange("p (k b) -> p k b", k=KD)

            def gru_turn(it, r_bank, z_bank, c_bank, p_bank):
                for s in range(STEPS):
                    n = it * STEPS + s + 1
                    act.wait_ge(r_psum, n)
                    nc.scalar.activation(flat(gate_r), gate_in(r_bank, s), ACT.Tanh, scale=0.5 / GSCALE).then_inc(r_ready, 1)
                    act.wait_ge(z_psum, n)
                    nc.scalar.activation(flat(gate_z), gate_in(z_bank, s), ACT.Tanh, scale=0.5 / GSCALE).then_inc(z_ready, 1)
                    act.wait_ge(c_psum, n)
                    nc.scalar.activation(flat(cand), gate_in(c_bank, s), ACT.Tanh, scale=1.0 / GSCALE).then_inc(c_ready, 1)
                    if (s + 1) % CHUNK == 0:
                        q = s // CHUNK
                        act.wait_ge(p_psum, it * (STEPS // CHUNK) + q + 1)
                        pin = p_bank[:, 0:KD * (STEPS // CHUNK) * B].rearrange("p (m c) -> p m c", m=KD)
                        nc.scalar.activation(flat(entry), pin[:, :, q * B:(q + 1) * B], ACT.Tanh, scale=1.0 / GSCALE).then_inc(p_ready, 1)

            with act.Fori(0, TURNS // 2) as it2:
                for turn in range(2):
                    gru_turn(it2 * 2 + turn, *banks[turn * 4:turn * 4 + 4])

            link = Link(act, ac)

            def routing_copies(l, first, square=None):
                for g in range(NTILE):
                    if square and g + 1 < NTILE:
                        if g >= 3:
                            act.wait_ge(logit_psum, first + g - 2)
                        square(g + 1)
                    act.wait_ge(logit_psum, first + g + 1)
                    if g >= 2:
                        act.wait_ge(logit_turned, first + g - 1)
                    n = RL if l == 2 else E
                    dst, src = logitT[0:n, g % 2], banks[6 + g % 2][0:n]
                    if l == 0:
                        i = nc.scalar.activation(dst, src, ACT.Identity, bias=rbias0[:])
                    elif l == 1:
                        i = nc.scalar.activation(dst, src, ACT.Sigmoid, bias=rcol[:, g:g + 1])
                    else:
                        i = nc.scalar.activation(dst, src, ACT.Identity)
                    i.then_inc(logitT_ready, 1)

            def gates_copy(l):
                for h in range(2):
                    act.wait_ge(gT_psum, h + 1)
                    nc.scalar.copy(gT[:, h * 4:h * 4 + 4], banks[6 + h][0:NSUB * E].rearrange("p (g c) -> p g c", c=P)
                                   ).then_inc(gT_ready, 1)

            def hidden(S, n, count, func, bias, done):
                act.wait_ge(S["up_psum"], count + 1)
                act.wait_ge(S["hid_used"], count + 1)
                nc.scalar.activation(hid[:, n], banks[n][:], func, bias=bias).then_inc(S[done], 1)

            act.wait_ge(rw_loaded, 9 * 16)
            routing_copies(0, 0)
            act.wait_ge(exp_in, 1)
            nc.scalar.activation(r_y, r_x, ACT.Exp).then_inc(exp_done, 1)
            act.wait_ge(xg_zeroed, 16 * 4)
            for b in range(NBLK):
                q = b % GRING
                act.wait_ge(row_psum, b + 1)
                if b >= GRING:
                    act.wait_ge(moved[q], 32 * (b // GRING))
                nc.scalar.copy(hrow[:, q], banks[q][:, 0:D]).then_inc(row_ready, 1)
            act.sem_inc(ffn[0]["hid_ready"], RING)
            S = ffn[0]

            def hidden_tile(i, n2):
                act.wait_ge(w0_loaded[i], n2 * 64 + 64)
                for f in range(F0):
                    count = (n2 * 2 + i) * F0 + f
                    act.wait_ge(S["up_psum"], count + 1)
                    act.wait_ge(S["hid_used"], count + 1)
                    nc.scalar.activation(hid0[:, f], banks[f % RING][:, 0:ET], ACT.Gelu, bias=b0_up[:, i, f:f + 1]
                                         ).then_inc(S["hid_ready"], 1)

            with act.Fori(0, NET // 4) as n4:
                for x in range(4):
                    hidden_tile(x % 2, n4 * 2 + x // 2)
            for n in range(NET // 4 * 4, NET):
                hidden_tile(n % 2, n // 2)
            act.wait_ge(cent_sum, 1)
            nc.scalar.activation(cent_n[:, 1:2], cent_n[:, 0:1], ACT.Sqrt).then_inc(cent_root, 1)

            def silu_tanh(j, f):
                act.wait_ge(ffn[1]["up_psum"], j * NU1 + 2 * f + 1)
                act.wait_ge(ffn[1]["hid_used"], j * FS + f + 1)
                nc.scalar.activation(hid[:, f % RING], banks[2 * f % RING][:], ACT.Tanh, scale=0.5).then_inc(ffn[1]["act_hid"], 1)

            with act.Fori(0, S1) as j:
                for f in range(FS):
                    silu_tanh(j, f)
            act.wait_ge(rcol_ready, 1)
            act.wait_ge(x_added, NBLK)
            act.wait_ge(ffn[1]["out_done"], S1)
            routing_copies(1, NTILE)
            act.wait_ge(slots_ready, 4)

            def take_block(jj, x):
                act.wait_ge(row_psum, NBLK + jj * SB + x - GRING + 1)
                nc.scalar.copy(xblk[:, x % GRING], XT[:, :, cols_of(jj * SB + x)]).then_inc(xblk_ready, 1)

            def take_turned(jj, x):
                act.wait_ge(row_psum, NBLK + jj * SB + x + 1)
                act.wait_ge(moved[x % GRING], 2 * MOVED + (jj * (SB // GRING) + x // GRING) * 32)
                nc.scalar.copy(hrow[:, x % GRING], banks[6 + x % 2][:, 0:D]).then_inc(row_ready, 1)

            with act.Fori(0, NBLK // SB) as jj:
                j = jj + S1
                for x in range(GRING):
                    take_block(jj, x)
                silu_tanh(j, 0)
                for f in range(1, FS):
                    silu_tanh(j, f)
                    for x in (2 * f - 2, 2 * f - 1):
                        take_turned(jj, x)
                    if f < FS - 1:
                        for x in (2 * f + 2, 2 * f + 3):
                            take_block(jj, x)
                for x in (SB - 2, SB - 1):
                    take_turned(jj, x)
            for j in range(S1 + NBLK // SB, NTILE):
                for f in range(FS):
                    silu_tanh(j, f)

            def expert_of(n):
                return bass.ds(act.value_load(etab[0:1, bass.ds(n, 1)], min_val=0, max_val=E - 1), 1)

            def copy_up(i, expert):
                nc.scalar.copy(w1_up[i], w1e[:, expert]).then_inc(up_copied, 1)

            def copy_down(i, expert):
                nc.scalar.copy(w1_down[i], w2e[:, expert]).then_inc(down_copied, 1)

            def small_tile(i, n, last):
                for f in range(FE):
                    c = n * FE + f
                    act.wait_ge(S["up_psum"], UP0 + c + 1)
                    act.wait_ge(S["hid_used"], USED0 - RING + c + 1)
                    nc.scalar.activation(hid[:, i * FE + f, 0:ET], banks[i * FE + f][:, 0:ET], ACT.Gelu).then_inc(S["hid_ready"], 1)
                if last > 1:
                    copy_up(i, expert_of(n + 2))
                if last > 0:
                    following = expert_of(n + 1)
                    act.wait_ge(S["hid_used"], USED0 + n * FE)
                    copy_down(1 - i, following)

            act.wait_ge(etab_ready, 2)
            act.wait_ge(ffn[1]["out_done"], NTILE)
            S = ffn[0]
            act.wait_ge(w1_loaded, 5 * 16)
            copy_up(0, expert_of(0))
            copy_up(1, expert_of(1))
            copy_down(0, expert_of(0))
            with act.Fori(0, NET // 4) as n4:
                for x in range(4):
                    small_tile(x % 2, n4 * 4 + x, 2)
            for n in range(NET // 4 * 4, NET):
                small_tile(n % 2, n, NET - 1 - n)
            sqt = WB[:, 5760:9856].rearrange("p (n k c) -> p n k c", n=4, k=KD)

            def square(g):
                act.wait_ge(x_added, NBLK + (g + 1) * NSUB)
                for k in range(KD):
                    i = nc.scalar.activation(sqt[:, g % 4, k], HT[:, k, g * TILE:(g + 1) * TILE], ACT.Square)
                i.then_inc(sq_ready, 1)

            square(0)
            routing_copies(2, 2 * NTILE, square)
            act.wait_ge(norm_sum, 1)
            nc.scalar.activation(r_y, r_x, ACT.Sqrt).then_inc(norm_root, 1)
            act.wait_ge(exp_in, 2)
            nc.scalar.activation(r_eq, r_sel, ACT.Exp).then_inc(exp_done, 1)
            gates_copy(2)
            act.wait_ge(gates_stored, 16 * NSUB)
            with act.Fori(0, NTILE // 4) as j4:
                for j, f in ((j4 * 4 + x, f) for x in range(4) for f in range(E)):
                    hidden(ffn[2], f % RING, j * E + f, ACT.Gelu, v1b[:, f:f + 1], "act_hid")
            act.wait_ge(w2s_loaded, 12 * 16)
            link(nc.scalar.activation(small2[:, 5:7], small2[:, 0:2], ACT.Abs))
            link(nc.scalar.activation(small2[:, 5:7], small2[:, 5:7], ACT.Exp, scale=-1.0))
            nc.scalar.activation(small2[:, 5:7], small2[:, 5:7], ACT.Ln, bias=1.0).then_inc(param_log, 1)
            act.sem_inc(ssm_taken[1], 1)
            for h in range(2):
                for j in range(h * HB, (h + 1) * HB):
                    act.wait_ge(p2_psum, j * 3 + 2)
                    nc.scalar.activation(ssm_c[:, j * TILE:(j + 1) * TILE], banks[1][0:NS], ACT.Tanh, bias=small2[:, 3:4]
                                         ).then_inc(ssm_taken[1], 1)
                act.wait_ge(ssm_taken[0], (h + 1) * HB + 1)
                c = slice(h * HB * TILE, (h + 1) * HB * TILE)
                link(nc.scalar.activation(ssm[:, c], ssm_b[:, c], ACT.Abs))
                link(nc.scalar.activation(ssm[:, c], ssm[:, c], ACT.Exp, scale=-1.0))
                nc.scalar.activation(ssm[:, c], ssm[:, c], ACT.Ln, bias=1.0).then_inc(softplus_log, 1)
            for j in range(B):
                for m in range(KD):
                    n = j * KD + m
                    act.wait_ge(y_psum, n + 1)
                    nc.scalar.activation(HT[:, m, j * TILE:(j + 1) * TILE], banks[n % 4][:], ACT.Identity,
                                         bias=bo2[:, m:m + 1]).then_inc(z_ready2, 1)
            act.wait_ge(cell_ready, 2)
            act.sem_inc(gate2_ready, 6)
            with act.Fori(0, B // 4) as j4:
                for j, h in ((j4 * 4 + x, h) for x in range(4) for h in range(2)):
                    for g in range(3):
                        act.wait_ge(gate2_psum, j * 6 + h * 3 + g + 1)
                        for m in range(KD):
                            i = nc.scalar.activation(lstm[:, h, g, m], banks[h * 3 + g][:, m * 256:(m + 1) * 256], ACT.Tanh,
                                                     scale=0.5 if g < 2 else 1.0, bias=gb2[:, g, m:m + 1])
                        i.then_inc(gate2_ready, 1)
            for m in range(KD):
                act.wait_ge(cpart_psum, m + 1)
                nc.scalar.activation(cpart[:, m], banks[6 + m][:], ACT.Identity, bias=gb2[:, 3, m:m + 1]).then_inc(cpart_ready, 1)
            with act.Fori(0, B // 2) as j2:
                for i in range(2):
                    for m in range(KD):
                        act.wait_ge(o2_sum, j2 * 4 + i * 2 + m + 1 + 4)
                        nc.scalar.activation(y2[:, i, m], y2[:, i, m], ACT.Tanh).then_inc(o2_tanh, 1)
            act.wait_ge(d3_recip, 1)
            nc.scalar.activation(d3[:], d3[:], ACT.Sqrt).then_inc(d3_ready, 1)
            act.wait_ge(d3_ready, 1)
            act.sem_inc(c3_ready, 2)
            with act.Fori(0, B // 4) as j4:
                for j, m in ((j4 * 4 + x, m) for x in range(4) for m in range(KD)):
                    act.wait_ge(c3_psum, j * 2 + m + 1 + 4)
                    nc.scalar.activation(HT[:, m, cols(j)], banks[m][:], ACT.Identity, scale=d3[:, m, bass.ds(j, 1)]).then_inc(c3_ready, 1)
            def take_scores(j):
                act.wait_ge(s3_psum, j + 1)
                if j >= 2:
                    act.wait_ge(beats_ready, j - 1)
                nc.scalar.copy(srow[:, j % 2], banks[6][:]).then_inc(s3_row, 1)

            take_scores(0)
            for j in range(B):
                if j + 1 < B:
                    take_scores(j + 1)
                act.wait_ge(own, 5 * j + 5)
                if j:
                    act.wait_ge(ranked, j)
                nc.scalar.activation(sgate[:, 0], scol[:], ACT.Tanh, scale=0.5).then_inc(s3_th, 1)
                for h in range(2):
                    act.wait_ge(row_psum, BLK3 + 2 * j + h + 1)
                    if j:
                        for q in (2 * h, 2 * h + 1):
                            act.wait_ge(moved[q], MOVED3 + 16 * j)
                    nc.scalar.copy(hrow[:, 2 * h:2 * h + 2].rearrange("p n d -> p (n d)"), banks[h][:]).then_inc(row_ready, 1)
                for k in range(KD):
                    act.wait_ge(base_psum, 2 * j + k + 1)
                    nc.scalar.copy(HT[:, k, j * TILE:(j + 1) * TILE], banks[4 + k][:]).then_inc(base_ready, 1)
            S = ffn[3]
            act.sem_inc(S["hid_ready"], RING)
            with act.Fori(0, B // 4) as j4:
                for j, f in ((j4 * 4 + x, f) for x in range(4) for f in range(F3)):
                    act.wait_ge(S["up_psum"], j * F3 + f + 1)
                    act.wait_ge(S["hid_used"], j * F3 + f + 1)
                    nc.scalar.activation(hid0[:, f], banks[f % RING][:, 0:ET], ACT.Gelu_apprx_tanh, bias=b3_up[:, f:f + 1]
                                         ).then_inc(S["hid_ready"], 1)

        @block.vector
        def _(dve):
            for k in range(KD):
                dve.sem_inc(xT_copied[k], 1)
            with dve.Fori(0, B) as j:
                for k in range(KD):
                    dve.wait_ge(xT_psum[k], j + 1)
                    nc.vector.tensor_copy(XT[:, k, bass.ds(j * T, T)], banks[4 + k][:]).then_inc(xT_copied[k], 1)
            dve.wait_ge(gru_w_loaded, 7 * 16)
            for g in range(4):
                dve.wait_ge(wsplit_high, g + 1)
                nc.vector.scalar_tensor_tensor(wpart[:, g, 1], wraw[:, g], wscale(g), wpart[:, g, 0], ALU.mult, ALU.subtract
                                               ).then_inc(wsplit, 1)
            dve.wait_ge(gru_b_loaded, 5 * 16)
            nc.vector.tensor_scalar(gbias[:], gbias[:], GSCALE, None, ALU.mult).then_inc(wsplit, 1)
            dve.wait_ge(condT_psum, 1)
            nc.vector.tensor_copy(condT[:].rearrange("p k b -> p (k b)"), banks[6][:, 0:KD * B]).then_inc(condT_ready, 1)
            nc.vector.tensor_copy(entry[:], banks[6][:, 0:KD * B]).then_inc(p_ready, 1)

            def split_entry(n):
                dve.wait_ge(p_ready, n)
                nc.vector.tensor_scalar(hpart[:, 0], entry[:], HSCALE, None, ALU.mult).then_inc(e_part, 1)
                nc.vector.tensor_scalar(entry_s[:], entry[:], HSCALE, None, ALU.mult).then_inc(e_full, 1)
                dve.wait_ge(e_full, n)
                nc.vector.tensor_tensor(hpart[:, 1], entry_s[:], hpart[:, 0], ALU.subtract).then_inc(e_part, 1)

            NP = STEPS // CHUNK
            split_entry(1)
            with dve.Fori(0, TURNS) as it:
                for s in range(STEPS):
                    n = it * STEPS + s
                    h = entry_s[:] if s % CHUNK == 0 else hist[:, s - 1]
                    dve.wait_ge(r_ready, n + 1)
                    nc.vector.scalar_tensor_tensor(rhpart[:, 0], gate_r[:], 1.0, h, ALU.add, ALU.mult).then_inc(rh_part, 1)
                    nc.vector.scalar_tensor_tensor(rfull[:], gate_r[:], 1.0, h, ALU.add, ALU.mult).then_inc(rh_full, 1)
                    dve.wait_ge(rh_full, n + 1)
                    nc.vector.tensor_tensor(rhpart[:, 1], rfull[:], rhpart[:, 0], ALU.subtract).then_inc(rh_part, 1)
                    dve.wait_ge(z_ready, n + 1)
                    nc.vector.tensor_scalar(keep[:], gate_z[:], -0.5, 0.5, ALU.mult, ALU.add).then_inc(keep_ready, 1)
                    dve.wait_ge(keep_ready, n + 1)
                    nc.vector.tensor_tensor(keep_h[:], keep[:], h, ALU.mult).then_inc(keep_h_ready, 1)
                    if s % (STEPS // 2) == 0:
                        dve.wait_ge(hist_copied, it * 2 + 1 + s // (STEPS // 2))
                    dve.wait_ge(c_ready, n + 1)
                    nc.vector.scalar_tensor_tensor(upd[:], gate_z[:], 1.0, cand[:], ALU.add, ALU.mult).then_inc(upd_ready, 1)
                    dve.wait_ge(upd_ready, n + 1)
                    nc.vector.scalar_tensor_tensor(hpart[:, 0], upd[:], 0.5 * HSCALE, keep_h[:], ALU.mult, ALU.add).then_inc(h_part, 1)
                    nc.vector.scalar_tensor_tensor(hist[:, s], upd[:], 0.5 * HSCALE, keep_h[:], ALU.mult, ALU.add).then_inc(h_full, 1)
                    dve.wait_ge(h_full, n + 1)
                    nc.vector.tensor_tensor(hpart[:, 1], hist[:, s], hpart[:, 0], ALU.subtract).then_inc(h_part, 1)
                    if (s + 1) % CHUNK == 0:
                        split_entry(it * NP + (s // CHUNK + 2))

            link = Link(dve, vc)
            V = nc.vector
            wide = lambda x: x.to_broadcast([P, NBLK, E])
            pref = prefer[:].rearrange("p (a e) -> p a e", a=1).to_broadcast([P, NBLK, E])

            def top2(x):
                for m, p, mask in ((r_m1, r_p1, r_mask1), (r_m2, r_p2, r_mask2)):
                    link(V.tensor_reduce(m, x, AX_X, ALU.max))
                    link(V.tensor_tensor(r_eq, x, wide(m), ALU.is_equal))
                    link(V.tensor_tensor(r_tmp, r_eq, pref, ALU.mult))
                    link(V.tensor_reduce(p, r_tmp, AX_X, ALU.max))
                    link(V.tensor_tensor(mask, r_tmp, wide(p), ALU.is_equal))
                    if m is r_m1:
                        link(V.scalar_tensor_tensor(r_sel, mask, FAR, x, ALU.mult, ALU.add))
                        x = r_sel

            def take_logits(l, dst, n):
                dve.wait_ge(logit_turned, (l + 1) * NTILE)
                half = NBLK // 2
                for h, bank in ((0, banks[5]), (1, banks[4])):
                    link(V.tensor_copy(dst[:, h * half:(h + 1) * half], bank[:, 0:half * n].rearrange("p (b n) -> p b n", n=n)))

            def place_tokens(l):
                by_expert = lambda x: x.rearrange("p (b e) -> p e b", e=E)
                by_block = lambda x: x.rearrange("p e b -> p b e")
                dve.wait_ge(prefix_psum, l + 1)
                link(V.tensor_copy(r_cnt, by_expert(banks[7][:, 0:NBLK * E])))
                for e in range(E):
                    link(V.tensor_tensor_scan(r_inc[:, e], ones[:, 0:NBLK], r_cnt[:, e], 0.0, ALU.mult, ALU.add))
                link(V.tensor_tensor(r_exc, r_inc, r_cnt, ALU.subtract))
                total = r_inc[:, :, NBLK - 1:NBLK]
                link(V.tensor_tensor_scan(r_step, ones[:, 0:NMAX], ones[:, 0:NMAX], 0.0, ALU.mult, ALU.add))
                link(V.tensor_scalar(r_step, r_step, -1.0, float(ET), ALU.add, ALU.mult))
                link(V.tensor_tensor(r_more, total.to_broadcast([P, E, NMAX]),
                                     r_step.rearrange("p (a i) -> p a i", a=1).to_broadcast([P, E, NMAX]), ALU.is_gt))
                link(V.tensor_reduce(r_tile.rearrange("p (e a) -> p e a", a=1), r_more, AX_X, ALU.add))
                link(V.tensor_scalar(r_tile, r_tile, float(ET), None, ALU.mult))
                link(V.tensor_tensor_scan(r_end, ones[:, 0:E], r_tile, 0.0, ALU.mult, ALU.add))
                link(V.tensor_tensor(r_base, r_end, r_tile, ALU.subtract))
                link(V.tensor_tensor(r_eq, banks[6][:, 0:NBLK * E].rearrange("p (b e) -> p b e", e=E), by_block(r_exc), ALU.add))
                link(V.tensor_tensor(r_sel, r_eq, r_base.rearrange("p (a e) -> p a e", a=1).to_broadcast([P, NBLK, E]), ALU.add))
                for c, mask in enumerate((r_mask1, r_mask2)):
                    link(V.tensor_tensor(r_tmp, r_sel, mask, ALU.mult))
                    link(V.tensor_reduce(r_y, r_tmp, AX_X, ALU.add))
                    V.tensor_copy(slots[:, c].rearrange("p (b a) -> p b a", a=1), r_y).then_inc(slots_ready, 1)
                    dve.wait_ge(slots_ready, 2 * l + c + 1)
                one = lambda i: etab_f[:, i]
                link(V.tensor_tensor_scan(one(0), ones[0:1, 0:NET], ones[0:1, 0:NET], 0.0, ALU.mult, ALU.add))
                link(V.tensor_scalar(one(1), one(0), float(ET), None, ALU.mult))
                link(V.memset(one(2), 0.0))
                for e in range(E - 1):
                    link(V.scalar_tensor_tensor(one(2), one(1), r_end[0:1, e:e + 1], one(2), ALU.is_gt, ALU.add))
                V.tensor_copy(etab[:], one(2)).then_inc(etab_ready, 1)


            dve.wait_ge(prefer_ready, E + 8)
            take_logits(0, r_log, E)
            top2(r_log)
            V.tensor_tensor(r_x, r_m2, r_m1, ALU.subtract).then_inc(exp_in, 1)
            V.tensor_tensor(r_w, r_mask1, r_mask2, ALU.add).then_inc(masks_ready, 1)
            dve.wait_ge(exp_done, 1)
            link(V.tensor_scalar(r_z, r_y, 1.0, None, ALU.add))
            g_1, g_2 = (gk[:, c].rearrange("p (b a) -> p b a", a=1) for c in range(2))
            link(V.reciprocal(g_1, r_z))
            link(V.tensor_tensor(g_2, g_1, r_y, ALU.mult))
            place_tokens(0)
            S = ffn[0]
            dve.sem_inc(S["out_free"], 1)
            flat = lambda x: x.rearrange("p k c -> p (k c)")

            def first_rows(l):
                dve.wait_ge(xgT_psum, l * NET + 1)
                V.tensor_copy(flat(xgT[:, 0]), banks[6][:]).then_inc(xgT_ready, 1)

            def tile_rows(l, i, n, n2, first=False, last=False):
                if not last:
                    dve.wait_ge(xgT_psum, l * NET + n + 2)
                    V.tensor_copy(flat(xgT[:, 1 - i]), banks[6][:]).then_inc(xgT_ready, 1)
                if not first:
                    dve.wait_ge(yrow_stored[i], (l * SIDE[i] + n2) * 16)
                if l == 0:
                    dve.wait_ge(w0_loaded[i], n2 * 64 + 64)
                    dve.wait_ge(ffn[0]["hid_used"], n * F0 + 2 * F0)
                else:
                    dve.wait_ge(ffn[0]["hid_used"], USED0 + n * FE + FE)
                for m in range(ES):
                    if l == 0:
                        ins = V.tensor_tensor(yrow[:, i, m], banks[4 + m][:, 0:D], b0_row[:, i], ALU.add)
                    else:
                        ins = V.tensor_copy(yrow[:, i, m], banks[4 + m][:, 0:D])
                ins.then_inc(ffn[0]["out_free"], 1)

            def weigh_rows(l, b4, q):
                b = b4 * GRING + q
                dve.wait_ge(moved[q], (2 * l + 1) * MOVED + b4 * 32 + 32)
                V.tensor_scalar(crow[:, q], grow[:, q, 0], gk[:, 0, bass.ds(b, 1)], None, ALU.mult).then_inc(weighted, 1)
                dve.wait_ge(weighted, l * NBLK + b + 1)
                V.scalar_tensor_tensor(crow[:, q], grow[:, q, 1], gk[:, 1, bass.ds(b, 1)], crow[:, q], ALU.mult, ALU.add
                                       ).then_inc(crow_ready, 1)

            def add_block(l, b4, q, bank):
                b = b4 * GRING + q
                dve.wait_ge(crow_psum, l * NBLK + b + 1)
                dst = (XT, HT)[l][:, :, cols_of(b)]
                V.tensor_tensor(dst, dst, bank[:, 0:D].rearrange("p (k c) -> p k c", k=KD), ALU.add).then_inc(x_added, 1)

            def add_rows(l, start, stop):
                with dve.Fori(start // GRING, stop // GRING) as b4:
                    for q in range(0, GRING, 2):
                        for x in (q, q + 1):
                            weigh_rows(l, b4, x)
                        for x in (q, q + 1):
                            add_block(l, b4, x, banks[6 + x % 2] if l == 0 else banks[x])

            first_rows(0)
            for i in range(2):
                tile_rows(0, i, i, 0, first=True)
            with dve.Fori(1, NET // 2) as n2:
                for i in range(2):
                    tile_rows(0, i, n2 * 2 + i, n2)
            tile_rows(0, 0, NET - 1, NET // 2, last=True)
            add_rows(0, 0, SB)
            link(V.tensor_tensor(cent_sq[:], cent[:], cent[:], ALU.mult))
            link(V.tensor_reduce(cent_n[:, 0:1], cent_sq[:], AX_X, ALU.add))
            V.tensor_copy(cent_n[:, 2:3], cent_n[:, 0:1]).then_inc(cent_sum, 1)
            dve.wait_ge(cent_root, 1)
            link(V.tensor_scalar(cent_n[:, 2:3], cent_n[:, 1:2], 1e-12, None, ALU.max))
            link(V.reciprocal(cent_n[:, 3:4], cent_n[:, 2:3]))
            V.tensor_scalar(cent[:], cent[:], cent_n[:, 3:4], None, ALU.mult).then_inc(cent_ready, 1)
            dve.wait_ge(cent_psum, 1)
            for k in range(KD):
                i = V.tensor_copy(rw[:, 2, k, 0:2 * E], banks[3][:, 64 + k * 2 * E:64 + (k + 1) * 2 * E])
            i.then_inc(rw_ready, 1)
            dve.wait_ge(rcol_psum, 1)
            V.tensor_copy(rcol[:], banks[3][0:E, 0:B]).then_inc(rcol_ready, 1)
            dve.wait_ge(w1_loaded, 3 * 16)
            V.tensor_scalar(wsh2, wsh2, 0.5, None, ALU.mult).then_inc(wsh_ready, 1)

            S = ffn[1]
            dve.sem_inc(S["out_free"], 1)
            dve.sem_inc(S["hid_ready"], RING)

            def silu(j, f):
                dve.wait_ge(ffn[1]["act_hid"], j * FS + f + 1)
                V.scalar_tensor_tensor(hid[:, f % RING], hid[:, f % RING], 1.0, banks[2 * f % RING][:], ALU.add,
                                       ALU.mult).then_inc(silu_half, 1)
                dve.wait_ge(silu_half, j * FS + f + 1)
                dve.wait_ge(ffn[1]["up_psum"], j * NU1 + 2 * f + 2)
                V.tensor_tensor(hid[:, f % RING], hid[:, f % RING], banks[(2 * f + 1) % RING][:], ALU.mult
                                ).then_inc(ffn[1]["hid_ready"], 1)

            def shared_out(j):
                dve.wait_ge(ffn[1]["hid_used"], (j + 1) * FS + RING)
                for m in range(KD):
                    ins = V.tensor_scalar(HT[:, m, cols(j)], banks[4 + m][:], 1.0 / 3.0, None, ALU.mult)
                ins.then_inc(ffn[1]["out_free"], 1)
                dve.wait_ge(ffn[1]["out_free"], j + 2)
                dve.sem_inc(ffn[1]["out_done"], 1)

            with dve.Fori(0, S1) as j:
                block = lambda x: ((j + 1) * (SB // GRING) + x // GRING, x % GRING)
                for f in range(FS):
                    silu(j, f)
                    if f:
                        for x in (2 * f - 2, 2 * f - 1):
                            add_block(0, *block(x), banks[6 + x % 2])
                    for x in (2 * f, 2 * f + 1):
                        weigh_rows(0, *block(x))
                shared_out(j)
                for x in (SB - 2, SB - 1):
                    add_block(0, *block(x), banks[6 + x % 2])

            take_logits(1, r_log, E)
            bias = rbias1[:].rearrange("p (a e) -> p a e", a=1).to_broadcast([P, NBLK, E])
            link(V.tensor_tensor(r_w, r_log, bias, ALU.add))
            top2(r_w)
            V.tensor_tensor(r_w, r_mask1, r_mask2, ALU.add).then_inc(masks_ready, 1)
            dve.wait_ge(masks_ready, 2)
            link(V.tensor_tensor(r_sel, r_w, r_log, ALU.mult))
            link(V.tensor_reduce(r_x, r_sel, AX_X, ALU.add))
            link(V.tensor_scalar(r_y, r_x, 1e-9, None, ALU.is_gt))
            link(V.tensor_scalar(r_z, r_x, 1e-9, None, ALU.add))
            link(V.reciprocal(r_x, r_z))
            link(V.tensor_tensor(r_x, r_x, r_y, ALU.mult))
            link(V.tensor_scalar(r_y, r_y, -0.5, 0.5, ALU.mult, ALU.add))
            link(V.tensor_scalar(r_x, r_x, 1.0 / 3.0, None, ALU.mult))
            link(V.tensor_scalar(r_y, r_y, 1.0 / 3.0, None, ALU.mult))
            for c, mask in enumerate((r_mask1, r_mask2)):
                g_c = gk[:, c].rearrange("p (b a) -> p b a", a=1)
                link(V.tensor_tensor(r_tmp, r_sel, mask, ALU.mult))
                link(V.tensor_reduce(r_z, r_tmp, AX_X, ALU.add))
                link(V.tensor_tensor(r_z, r_z, r_x, ALU.mult))
                link(V.tensor_tensor(g_c, r_z, r_y, ALU.add))
            place_tokens(1)

            with dve.Fori(S1, NTILE) as j:
                for f in range(FS):
                    silu(j, f)
                shared_out(j)
            first_rows(1)
            with dve.Fori(0, NET // 2) as n2:
                for i in range(2):
                    tile_rows(1, i, n2 * 2 + i, n2)
            tile_rows(1, 0, NET - 1, NET // 2, last=True)
            add_rows(1, 0, NBLK)
            take_logits(2, r_raw, RL)
            V.tensor_copy(r_x, r_raw[:, :, RL - 1:RL]).then_inc(norm_sum, 1)
            dve.wait_ge(norm_root, 1)
            link(V.tensor_scalar(r_z, r_y, 1e-12, None, ALU.max))
            link(V.reciprocal(r_x, r_z))
            link(V.tensor_tensor(r_tmp, r_raw[:, :, 0:E], wide(r_x), ALU.mult))
            link(V.tensor_tensor(r_log, r_tmp, r_raw[:, :, E:2 * E], ALU.add))
            top2(r_log)
            link(V.tensor_tensor(r_mask1, r_log, wide(r_m2), ALU.is_ge))
            V.tensor_tensor(r_sel, r_log, wide(r_m1), ALU.subtract).then_inc(exp_in, 1)
            dve.wait_ge(exp_done, 2)
            link(V.tensor_tensor(r_tmp, r_eq, r_mask1, ALU.mult))
            link(V.tensor_reduce(r_x, r_tmp, AX_X, ALU.add))
            link(V.reciprocal(r_y, r_x))
            V.tensor_tensor(r_w, r_tmp, wide(r_y), ALU.mult).then_inc(gates_ready, 1)

            S = ffn[2]
            dve.sem_inc(S["out_free"], 1)
            dve.sem_inc(S["hid_ready"], RING)

            def conv_tap(j, tap):
                order = B - 1 if tap == 0 else tap - 1
                back = B - 1 - order
                if tap:
                    for k in range(KD):
                        dve.wait_ge(conv_step[k], j * B + tap)
                for k in range(KD):
                    w = condT[:, k, order:order + 1]
                    src = XT[:, k, cols(j, TILE - back)]
                    dst = HT[:, k, bass.ds(j * TILE + back, TILE - back)]
                    if tap == 0:
                        ins = V.tensor_scalar(dst, src, w, cb2[:, k:k + 1], ALU.mult, ALU.add)
                    else:
                        ins = V.scalar_tensor_tensor(dst, src, w, dst, ALU.mult, ALU.add)
                    ins.then_inc(conv_step[k], 1)

            def mixture_tile(i, j, j2, conv):
                dve.wait_ge(g_loaded[i], j2 * 32 + 32)
                for f in range(E):
                    dve.wait_ge(S["act_hid"], j * E + f + 1)
                    V.tensor_tensor(hid[:, f % RING], hid[:, f % RING], g1[:, i, f], ALU.mult).then_inc(S["hid_ready"], 1)
                    if conv:
                        conv_tap(j - 1, f)
                dve.wait_ge(S["hid_used"], (j + 1) * E + RING)
                for m in range(KD):
                    x_t = XT[:, m, cols(j)]
                    ins = V.tensor_tensor(x_t, x_t, banks[4 + m][:], ALU.add)
                ins.then_inc(S["out_free"], 1)
                dve.wait_ge(S["out_free"], j + 2)
                dve.sem_inc(S["out_done"], 1)

            dve.wait_ge(w2s_loaded, 12 * 16)
            for i in range(2):
                mixture_tile(i, i, 0, i == 1)
            with dve.Fori(1, NTILE // 2) as j2:
                for i in range(2):
                    mixture_tile(i, j2 * 2 + i, j2, True)
            for tap in range(B):
                conv_tap(NTILE - 1, tap)
            dve.wait_ge(param_log, 1)
            link(V.tensor_scalar(small2[:, 7:9], small2[:, 0:2], 0.0, None, ALU.max))
            link(V.tensor_tensor(small2[:, 7:9], small2[:, 7:9], small2[:, 5:7], ALU.add))
            link(V.tensor_tensor(small2[:, 9:10], small2[:, 7:8], small2[:, 8:9], ALU.mult))
            link(V.tensor_scalar(small2[:, 10:11], small2[:, 9:10], -1.0, 1.0, ALU.mult, ALU.add))
            link(V.memset(decay[:], 1.0))
            link(V.tensor_scalar(decay[:], decay[:], small2[:, 10:11], None, ALU.mult))
            dt = small2[:, 8:9]
            dve.sem_inc(ssm_taken[0], 1)
            dve.sem_inc(ssm_taken[2], 1)

            def state_space(j):
                c = slice(j * TILE, (j + 1) * TILE)
                dve.wait_ge(softplus_log, j // HB + 1)
                link(V.scalar_tensor_tensor(ssm_b[:, c], ssm_b[:, c], 0.0, ssm[:, c], ALU.max, ALU.add))
                link(V.tensor_tensor(ssm_b[:, c], ssm_b[:, c], ssm_u[:, c], ALU.mult))
                link(V.tensor_tensor_scan(ssm[:, c], decay, ssm_b[:, c], 0.0, ALU.mult, ALU.add))
                V.tensor_tensor(ssm_b[:, c], ssm[:, c], ssm_c[:, c], ALU.mult).then_inc(ssm_y, 1)

            for j in range(B):
                c = slice(j * TILE, (j + 1) * TILE)
                dve.wait_ge(p2_psum, j * 3 + 1)
                V.tensor_scalar(ssm_b[:, c], banks[0][0:NS], small2[:, 2:3], None, ALU.add).then_inc(ssm_taken[0], 1)
                dve.wait_ge(p2_psum, j * 3 + 3)
                V.tensor_scalar(ssm_u[:, c], banks[2][0:NS], small2[:, 4:5], dt, ALU.add, ALU.mult).then_inc(ssm_taken[2], 1)
                if j >= HB:
                    dve.wait_ge(ssm_taken[2], j - HB + 2)
                    dve.wait_ge(ssm_taken[1], j - HB + 2)
                    state_space(j - HB)
            dve.wait_ge(ssm_taken[2], B + 1)
            dve.wait_ge(ssm_taken[1], B + 1)
            for j in range(HB, B):
                state_space(j)
            for g in range(8):
                dve.wait_ge(uT_psum, g + 1)
                V.tensor_scalar(uT[:, g].rearrange("p k m -> p (k m)"), banks[6 + g % 2][:], 0.5 if g >= 4 else 1.0, None,
                                ALU.mult).then_inc(uT_ready, 1)
            dve.wait_ge(ssm_y, B)
            link(V.tensor_scalar(gb2[:, 0:2], gb2[:, 0:2], 0.5, None, ALU.mult))
            link(V.memset(c2, 2.0))
            for k in range(KD):
                link(V.tensor_scalar(c2[:, k], c2[:, k], cinit[:, k:k + 1], None, ALU.mult))
            dve.sem_inc(cell_ready, 2)
            with dve.Fori(0, B) as j:
                for h in range(2):
                    n = j * 2 + h
                    c2h = c2[:, :, h * 256:(h + 1) * 256]
                    tf, ti, tg, a, b = (lstm[:, h, x] for x in range(5))
                    dve.wait_ge(gate2_ready, n * 3 + 3 + 6)
                    V.scalar_tensor_tensor(a, tf, 1.0, c2h, ALU.add, ALU.mult).then_inc(cell_step, 1)
                    V.scalar_tensor_tensor(b, ti, 1.0, tg, ALU.add, ALU.mult).then_inc(cell_step, 1)
                    dve.wait_ge(cell_step, n * 2 + 2)
                    V.scalar_tensor_tensor(c2h, a, 0.5, b, ALU.mult, ALU.add).then_inc(cell_ready, 1)
            dve.wait_ge(cpart_ready, 2)
            dve.sem_inc(o2_sum, 4)
            with dve.Fori(0, B // 2) as j2:
                for i in range(2):
                    for m in range(KD):
                        n = j2 * 4 + i * 2 + m
                        dve.wait_ge(o2_psum, n + 1)
                        dve.wait_ge(o2_added, n + 1)
                        V.tensor_tensor(y2[:, i, m], banks[i * 2 + m][:], cpart[:, m], ALU.add).then_inc(o2_sum, 1)
            dve.wait_ge(w3_loaded, 5 * 16)
            link(V.tensor_scalar(ys3[:], condT[:], 1.0 / 16.0, None, ALU.mult))
            V.tensor_tensor(ysq3[:], ys3[:], ys3[:], ALU.mult).then_inc(d3_in, 1)
            V.tensor_tensor(w3sq, w3c, w3c, ALU.mult).then_inc(d3_in, 1)
            for k in range(KD):
                V.tensor_scalar(wr3b[:, k], ones[:], wr3[:, k:k + 1], None, ALU.mult).then_inc(d3_in, 1)
            dve.wait_ge(d3_psum, 1)
            link(V.tensor_scalar(d3[:].rearrange("p k b -> p (k b)"), banks[6][:, 0:KD * B], 1e-8, None, ALU.add))
            V.reciprocal(d3[:], d3[:]).then_inc(d3_recip, 1)
            dve.wait_ge(o2_added, 2 * B + 4)
            with dve.Fori(0, B // 2) as j2:
                for i in range(2):
                    j = j2 * 2 + i
                    dve.wait_ge(c3_psum, j * 2 + 2)
                    for k in range(KD):
                        V.tensor_scalar(hid[:, 2 * i + k], XT[:, k, cols(j)], ys3[:, k, bass.ds(j, 1)], None, ALU.mult).then_inc(xs3_ready, 1)
            dve.wait_ge(y_psum, 2 * B)
            link(V.memset(first_row, -float(TILE)))

            def compare(j):
                row = srow[:, j % 2]
                dve.wait_ge(s3_row, j + 1)
                for s in range(NSUB):
                    V.tensor_tensor(smask[:, s], row[:, s * P:(s + 1) * P], ident[:], ALU.mult).then_inc(own, 1)
                if j:
                    dve.wait_ge(s3_th, j)
                dve.wait_ge(own, j * 5 + 4)
                V.tensor_reduce(scol[:], smask[:], AX_X, ALU.add).then_inc(own, 1)
                x_t = XT[:, :, j * TILE:(j + 1) * TILE]
                V.tensor_tensor(x_t, x_t, HT[:, :, j * TILE:(j + 1) * TILE], ALU.add).then_inc(xh_sum, 1)
                if j:
                    take_ranks(j - 1)
                dve.wait_ge(own, j * 5 + 5)
                for s in range(NSUB):
                    own_block = row[:, s * P:(s + 1) * P]
                    V.tensor_scalar(beats[:, s, 0:(s + 1) * P], row[:, 0:(s + 1) * P], scol[:, s:s + 1], None, ALU.is_lt)
                    if s + 1 < NSUB:
                        V.tensor_scalar(beats[:, s, (s + 1) * P:], row[:, (s + 1) * P:], scol[:, s:s + 1], None, ALU.is_le)
                    ins = V.scalar_tensor_tensor(ties[:, s], own_block, scol[:, s:s + 1], strict[:], ALU.is_equal, ALU.mult)
                ins.then_inc(beats_ready, 1)

            def take_ranks(j):
                dve.wait_ge(rank_psum, j + 1)
                dve.wait_ge(s3_th, j + 1)
                link(V.tensor_scalar(first_row, first_row, float(TILE), None, ALU.add))
                link(V.tensor_scalar(pick, banks[7][:, 0:NSUB], float(TOPK3), None, ALU.is_lt))
                link(V.tensor_tensor(rank, banks[7][:, 0:NSUB], first_row, ALU.add))
                link(V.tensor_scalar(sgate[:, 1], sgate[:, 0], 0.5, 0.5, ALU.mult, ALU.add))
                link(V.tensor_tensor(gk[:, 0, j * NSUB:(j + 1) * NSUB], sgate[:, 1], pick, ALU.mult))
                V.tensor_copy(slots[:, 0, j * NSUB:(j + 1) * NSUB], rank).then_inc(ranked, 1)

            for j in range(B):
                compare(j)
            take_ranks(B - 1)

            S = ffn[3]
            dve.sem_inc(S["out_free"], 1)
            dve.wait_ge(xgT_psum, ROWS3 + 1)
            V.tensor_copy(flat(xgT[:, 0]), banks[6][:]).then_inc(xgT_ready, 1)

            def finish_batch(j):
                for q in range(NSUB):
                    dve.wait_ge(moved[q], MOVED3 + 16 * B + 16 * (j + 1))
                    at = HT[:, q // 2, j * TILE + q % 2 * D:j * TILE + (q % 2 + 1) * D]
                    b = j * NSUB + q
                    ins = V.scalar_tensor_tensor(at, back[:, b], gk[:, 0, b:b + 1], at, ALU.mult, ALU.add)
                ins.then_inc(out_rows, 1)

            dve.wait_ge(b3_loaded, 16)
            dve.wait_ge(base_ready, 2 * B)
            for j in range(B):
                if j + 1 < B:
                    dve.wait_ge(xgT_psum, ROWS3 + j + 2)
                    V.tensor_copy(flat(xgT[:, (j + 1) % 2]), banks[6][:]).then_inc(xgT_ready, 1)
                dve.wait_ge(yrow_stored[j % 2], (2 * SIDE[j % 2] + j // 2) * 16)
                dve.wait_ge(S["hid_used"], j * F3 + 2 * F3)
                for m in range(ES):
                    ins = V.tensor_tensor(yrow[:, j % 2, m], banks[4 + m][:, 0:D], b3_row, ALU.add)
                ins.then_inc(S["out_free"], 1)
                if j:
                    finish_batch(j - 1)
            finish_batch(B - 1)

        @block.tensor
        def _(pe):
            pe.wait_ge(const_ready, 2)
            for j in range(B):
                pe.wait_ge(x_loaded[j // 2], 2 * 16)
                for k in range(KD):
                    pe.wait_ge(xT_copied[k], j + 1)
                    for s in range(NSUB):
                        last = nc.tensor.transpose(banks[4 + k][:, s * P:(s + 1) * P], xstage[:, j, s, k * P:(k + 1) * P], ident[:])
                    last.then_inc(xT_psum[k], 1)
            pe.wait_ge(gru_b_loaded, 5 * 16)
            for k in range(KD):
                last = nc.tensor.transpose(banks[6][:, k * B:(k + 1) * B], condrow[:, k * P:(k + 1) * P], ident[0:B, 0:B])
            last.then_inc(condT_psum, 1)
            for k in range(KD):
                pe.wait_ge(xT_copied[k], B + 1)
            pe.wait_ge(gru_w_loaded, 7 * 16)
            pe.wait_ge(gru_b_loaded, 5 * 16)
            pe.wait_ge(wsplit, NSPLIT)

            xview = XT[:].rearrange("p k (b t) -> p k t b", b=B)
            NP = STEPS // CHUNK
            W = STEPS * B

            def projections(it, r_bank, z_bank, c_bank, p_bank):
                for g, bank in enumerate((r_bank, z_bank, c_bank)):
                    for m in range(KD):
                        o = bank[:, m * W:(m + 1) * W]
                        nc.tensor.matmul(o, gbias[0:1, g, m * P:(m + 1) * P], ones[0:1, 0:W], start=m == 0, stop=False,
                                         skip_group_check=True)
                        yield
                        for k in range(KD):
                            nc.tensor.matmul(o, wx[:, g, k, m * P:(m + 1) * P], xview[:, k, bass.ds(it * STEPS, STEPS)],
                                             start=False, stop=False, skip_group_check=True)
                            yield
                for m in range(KD):
                    nc.tensor.matmul(p_bank[:, m * NP * B:(m + 1) * NP * B], gbias[0:1, 3, m * P:(m + 1) * P],
                                     ones[0:1, 0:NP * B], start=m == 0, stop=False, skip_group_check=True)
                    yield

            def recur(bank, g, width, s, part, wait):
                for a in range(2):
                    if wait:
                        wait(a)
                    for m in range(KD):
                        for k in range(KD):
                            for w in range(2 - a):
                                last = nc.tensor.matmul(bank[:, m * width + s * B:m * width + (s + 1) * B],
                                                        wpart[:, g, w, k, m * P:(m + 1) * P],
                                                        part[:, a, k * B:(k + 1) * B],
                                                        start=False, stop=True, skip_group_check=True)
                return last

            def gru_turn(it, gates, next_gates):
                following = projections((it + 1) & (TURNS - 1), *next_gates)
                for s in range(STEPS):
                    n = it * STEPS + s
                    if s % CHUNK == 0:
                        wait = lambda a: pe.wait_ge(e_part, (it * NP + s // CHUNK) * 2 + a + 1)
                    else:
                        wait = lambda a: pe.wait_ge(h_part, (n - 1) * 2 + a + 1)
                    recur(gates[0], 0, W, s, hpart, wait).then_inc(r_psum, 1)
                    recur(gates[1], 1, W, s, hpart, None).then_inc(z_psum, 1)
                    recur(gates[2], 2, W, s, rhpart, lambda a: pe.wait_ge(rh_part, n * 2 + a + 1)).then_inc(c_psum, 1)
                    next(following, None)
                    if (s + 1) % CHUNK == 0:
                        recur(gates[3], 3, NP * B, s // CHUNK, hpart,
                              lambda a: pe.wait_ge(h_part, n * 2 + a + 1)).then_inc(p_psum, 1)
                        next(following, None)
                for _ in following:
                    pass

            for _ in projections(0, *banks[0:4]):
                pass
            with pe.Fori(0, TURNS // 2) as it2:
                for turn in range(2):
                    gru_turn(it2 * 2 + turn, banks[turn * 4:turn * 4 + 4], banks[4 - turn * 4:8 - turn * 4])

            pe.wait_ge(hist_copied, 2 * TURNS + 2)
            pe.wait_ge(p_ready, TURNS * NP + 1)

            def logits(l, src, n, first, square=None):
                for g in range(NTILE + 1):
                    if l == 2 and g < NTILE:
                        for q in range(GRING):
                            turn_added(1, g, q, banks[q])
                        pe.wait_ge(x_added, NBLK + (g + 1) * NSUB)
                    if g < NTILE:
                        if g >= 2:
                            pe.wait_ge(logitT_ready, first + g - 1)
                        o = banks[6 + g % 2][0:n]
                        for k in range(KD):
                            last = nc.tensor.matmul(o, rw[:, l, k, 0:n], src[:, k, g * TILE:(g + 1) * TILE],
                                                    start=k == 0, stop=k == KD - 1 and square is None)
                        if square is not None:
                            pe.wait_ge(sq_ready, g + 1)
                            for k in range(KD):
                                last = nc.tensor.matmul(o, rsq[:, k], square[:, g % 4, k], start=False, stop=k == KD - 1)
                        last.then_inc(logit_psum, 1)
                    if g >= 1:
                        h = g - 1
                        pe.wait_ge(logitT_ready, first + h + 1)
                        for q in range(NSUB):
                            b = h * NSUB + q
                            half = NBLK // 2
                            o = (banks[5], banks[4])[b // half][:, b % half * n:(b % half + 1) * n]
                            last = nc.tensor.transpose(o, logitT[0:n, h % 2, q * P:(q + 1) * P], ident[0:n, 0:n])
                        last.then_inc(logit_turned, 1)

            def turn_gates():
                pe.wait_ge(gates_ready, 1)
                flat_w = r_w.rearrange("p b e -> p (b e)")
                for g in range(NTILE):
                    w = NSUB * E
                    last = nc.tensor.transpose(banks[6 + g // 4][0:w, g % 4 * P:(g % 4 + 1) * P], flat_w[:, g * w:(g + 1) * w], ident[:])
                    if g % 4 == 3:
                        last.then_inc(gT_psum, 1)

            def ffn_tile(S, n, src, up, down, j, out_extra=None):
                c0 = j * n
                for f in range(n + LAG):
                    if f < n:
                        pe.wait_ge(S["hid_ready"], c0 + f + 1)
                        for k in range(KD):
                            last = nc.tensor.matmul(banks[f % RING][:], up(f, k), src(k), start=k == 0, stop=k == KD - 1)
                        last.then_inc(S["up_psum"], 1)
                    h = f - LAG
                    if h == 0:
                        pe.wait_ge(S["out_free"], j + 1)
                        if out_extra:
                            out_extra()
                    if h >= 0:
                        pe.wait_ge(S["hid_ready"], c0 + h + 1 + RING)
                        for m in range(KD):
                            last = nc.tensor.matmul(banks[4 + m][:], down(h, m), hid[:, h % RING],
                                                    start=h == 0 and not out_extra, stop=h == n - 1)
                        last.then_inc(S["hid_used"], 1)

            half_of = lambda m: slice(m * P, (m + 1) * P)
            pe.wait_ge(rw_loaded, 9 * 16)
            logits(0, HT, E, 0)
            def prefixes(l):
                pe.wait_ge(masks_ready, l + 1)
                flat_w = r_w.rearrange("p b e -> p (b e)")
                nc.tensor.matmul(banks[6][:, 0:NBLK * E], strict[:], flat_w, start=True, stop=True)
                nc.tensor.matmul(banks[7][:, 0:NBLK * E], ones[:], flat_w, start=True, stop=True).then_inc(prefix_psum, 1)

            prefixes(0)
            for b in range(NBLK):
                if b >= GRING:
                    pe.wait_ge(row_ready, b - GRING + 1)
                for k in range(KD):
                    last = nc.tensor.transpose(banks[b % GRING][:, half_of(k)], HT[:, k, b * P:(b + 1) * P], ident[:])
                last.then_inc(row_psum, 1)

            S = ffn[0]
            pe.sem_inc(S["hid_used"], F0)

            def turn_tile(l, i, n2):
                pe.wait_ge(xrow_loaded[i], (l * SIDE[i] + n2) * 16 + 16)
                for k in range(KD):
                    for s in range(ES):
                        last = nc.tensor.transpose(banks[6][:, k * ET + s * P:k * ET + (s + 1) * P], xrow[:, i, s, half_of(k)], ident[:])
                last.then_inc(xgT_psum, 1)

            def expert_tile(i, n, last_tile, n2):
                c0 = n * F0
                pe.wait_ge(w0_loaded[i], n2 * 64 + 64)
                pe.wait_ge(xgT_ready, n + 1)
                for f in range(F0 + LAG):
                    if f < F0:
                        pe.wait_ge(S["hid_ready"], c0 + f + 1)
                        for k in range(KD):
                            last = nc.tensor.matmul(banks[f % RING][:, 0:ET], w0_up[i][:, k, f * P:(f + 1) * P], xgT[:, i, k],
                                                    start=k == 0, stop=k == KD - 1)
                        last.then_inc(S["up_psum"], 1)
                    if f == F0 and not last_tile:
                        turn_tile(0, 1 - i, n2 + i)
                    h = f - LAG
                    if h == 0:
                        pe.wait_ge(S["out_free"], n + 1)
                    if h >= 0:
                        pe.wait_ge(S["hid_ready"], c0 + h + 1 + RING)
                        for m in range(ES):
                            last = nc.tensor.matmul(banks[4 + m][:, 0:D], hid0[:, h, half_of(m)], w0_down[i][:, h],
                                                    start=h == 0, stop=h == F0 - 1)
                        last.then_inc(S["hid_used"], 1)

            turn_tile(0, 0, 0)
            with pe.Fori(0, NET // 2) as n2:
                for i in range(2):
                    expert_tile(i, n2 * 2 + i, False, n2)
            expert_tile(0, NET - 1, True, NET // 2)

            def turn_added(l, b4, q, bank):
                pe.wait_ge(crow_ready, l * NBLK + b4 * GRING + q + 1 + GRING)
                for k in range(KD):
                    last = nc.tensor.transpose(bank[:, half_of(k)], crow[:, q, half_of(k)], ident[:])
                last.then_inc(crow_psum, 1)

            with pe.Fori(0, SB // GRING) as b4:
                for q in range(GRING):
                    turn_added(0, b4, q, banks[6 + q % 2])
            pe.wait_ge(cent_ready, 1)
            for k in range(KD):
                nc.tensor.transpose(banks[3][:, 64 + k * 2 * E:64 + k * 2 * E + E], cent[:, half_of(k)], ident[0:E, 0:E])
                last = nc.tensor.transpose(banks[3][:, 64 + k * 2 * E + E:64 + (k + 1) * 2 * E], route[:, half_of(k)], ident[0:E, 0:E])
            last.then_inc(cent_psum, 1)
            pe.wait_ge(rw_ready, 1)
            for k in range(KD):
                last = nc.tensor.matmul(banks[3][0:E, 0:B], rcond[:, k], condT[:, k], start=k == 0, stop=k == KD - 1)
            last.then_inc(rcol_psum, 1)
            pe.wait_ge(rcol_ready, 1)
            pe.wait_ge(x_added, SB)
            pe.wait_ge(w1_loaded, 3 * 16)
            pe.wait_ge(wsh_ready, 1)
            S = ffn[1]
            pe.sem_inc(S["hid_used"], RING)

            def up_unit(j, u):
                if u < RING:
                    pe.wait_ge(S["hid_ready"], j * FS + u // 2 + 1 + RING // 2)
                else:
                    pe.wait_ge(S["hid_ready"], j * FS + u // 2 - 1 + RING)
                for k in range(KD):
                    last = nc.tensor.matmul(banks[u % RING][:], (wsh1, wsh3)[u % 2][:, k, u // 2 * P:(u // 2 + 1) * P],
                                            XT[:, k, cols(j)], start=k == 0, stop=k == KD - 1)
                last.then_inc(S["up_psum"], 1)

            def down_chunk(j, h):
                if h == 0:
                    pe.wait_ge(S["out_free"], j + 1)
                pe.wait_ge(S["hid_ready"], j * FS + h + 1 + RING)
                for m in range(KD):
                    last = nc.tensor.matmul(banks[4 + m][:], wsh2[:, h, half_of(m)], hid[:, h % RING],
                                            start=h == 0, stop=h == FS - 1)
                last.then_inc(S["hid_used"], 1)

            def shared_tile(j, beside=None):
                for f in range(FS + 1):
                    if f < FS:
                        up_unit(j, 2 * f)
                        up_unit(j, 2 * f + 1)
                    if f >= 1:
                        down_chunk(j, f - 1)
                        if beside:
                            beside(2 * f - 2)
                            beside(2 * f - 1)

            with pe.Fori(0, S1) as j:
                shared_tile(j, lambda x: turn_added(0, (j + 1) * (SB // GRING) + x // GRING, x % GRING, banks[6 + x % 2]))
            pe.wait_ge(x_added, NBLK)
            pe.wait_ge(ffn[1]["out_done"], S1)
            logits(1, XT, E, NTILE)
            prefixes(1)
            with pe.Fori(0, NBLK // SB) as jj:

                def turn_block(x):
                    b = jj * SB + x
                    pe.wait_ge(xblk_ready, b + 1)
                    pe.wait_ge(row_ready, NBLK + b - 1)
                    for k in range(KD):
                        last = nc.tensor.transpose(banks[6 + x % 2][:, half_of(k)], xblk[:, x % GRING, k], ident[:])
                    last.then_inc(row_psum, 1)

                shared_tile(jj + S1, turn_block)
            for j in range(S1 + NBLK // SB, NTILE):
                shared_tile(j)
            pe.wait_ge(ffn[1]["out_done"], NTILE)

            def small_tile(i, n, last_tile, n2):
                U = ffn[0]
                pe.wait_ge(up_copied, n + 1)
                pe.wait_ge(xgT_ready, NET + n + 1)
                for f in range(FE):
                    pe.wait_ge(U["hid_ready"], READY0 - RING + n * FE + f + 1)
                    for k in range(KD):
                        last = nc.tensor.matmul(banks[i * FE + f][:, 0:ET], w1_up[i][:, k, f * P:(f + 1) * P], xgT[:, i, k],
                                                start=k == 0, stop=k == KD - 1)
                    last.then_inc(U["up_psum"], 1)
                if not last_tile:
                    turn_tile(1, 1 - i, n2 + i)
                pe.wait_ge(down_copied, n + 1)
                pe.wait_ge(U["out_free"], NET + n + 1)
                for h in range(FE):
                    pe.wait_ge(U["hid_ready"], READY0 + n * FE + h + 1)
                    for m in range(ES):
                        last = nc.tensor.matmul(banks[4 + m][:, 0:D], hid[:, i * FE + h, half_of(m)], w1_down[i][:, h],
                                                start=h == 0, stop=h == FE - 1)
                    last.then_inc(U["hid_used"], 1)

            turn_tile(1, 0, 0)
            with pe.Fori(0, NET // 2) as n2:
                for i in range(2):
                    small_tile(i, n2 * 2 + i, False, n2)
            small_tile(0, NET - 1, True, NET // 2)
            logits(2, HT, RL, 2 * NTILE, WB[:, 5760:9856].rearrange("p (n k c) -> p n k c", n=4, k=KD))
            turn_gates()
            pe.wait_ge(w1f_loaded, 2 * 16)
            S = ffn[2]
            pe.sem_inc(S["hid_used"], RING)
            with pe.Fori(0, NTILE // 2) as j2:
                for i in range(2):
                    j = j2 * 2 + i

                    def bias_sum():
                        pe.wait_ge(g_loaded[i], j2 * 32 + 32)
                        for m in range(KD):
                            nc.tensor.matmul(banks[4 + m][:], v2b[:, half_of(m)], g1T[:, i], start=True, stop=False)

                    ffn_tile(S, E, lambda k: HT[:, k, cols(j)], lambda f, k: v1[:, f, k], lambda h, m: v2[:, h, half_of(m)], j,
                             bias_sum)
            pe.wait_ge(ffn[2]["out_done"], NTILE)
            pe.wait_ge(w2_loaded, 3 * 16)
            for k in range(KD):
                pe.wait_ge(conv_step[k], B * NTILE)
            for j in range(B):
                for x, w in enumerate((wp2[:, :, 0:NS], wp2[:, :, NS:2 * NS], ws2)):
                    pe.wait_ge(ssm_taken[x], j + 1)
                    for k in range(KD):
                        last = nc.tensor.matmul(banks[x][0:NS], w[:, k], (HT if x < 2 else XT)[:, k, j * TILE:(j + 1) * TILE],
                                                start=k == 0, stop=k == KD - 1)
                    last.then_inc(p2_psum, 1)
            for x in range(3):
                pe.wait_ge(ssm_taken[x], B + 1)
            for j in range(B):
                pe.wait_ge(ssm_y, j + 1)
                for m in range(KD):
                    n = j * KD + m
                    if n >= 4:
                        pe.wait_ge(z_ready2, n - 3)
                    nc.tensor.matmul(banks[n % 4][:], wo2[:, half_of(m)], ssm_b[:, j * TILE:(j + 1) * TILE], start=True, stop=True
                                     ).then_inc(y_psum, 1)
            pe.wait_ge(uraw_loaded, 8 * 16)
            for g in range(8):
                if g >= 2:
                    pe.wait_ge(uT_ready, g - 1)
                for ki in range(KD):
                    for ko in range(KD):
                        last = nc.tensor.transpose(banks[6 + g % 2][:, ki * D + ko * P:ki * D + (ko + 1) * P],
                                                   uraw[:, g, ko, half_of(ki)], ident[:])
                last.then_inc(uT_psum, 1)
            pe.wait_ge(uT_ready, 8)
            pe.wait_ge(z_ready2, 2 * B)
            with pe.Fori(0, B) as j:
                for h in range(2):
                    n = j * 2 + h
                    for part in range(2):
                        if part:
                            pe.wait_ge(cell_ready, n + 1)
                        for g in range(3):
                            if not part:
                                pe.wait_ge(gate2_ready, n * 3 + g + 1)
                            for m in range(KD):
                                for k in range(KD):
                                    src = c2[:, k, h * 256:(h + 1) * 256] if part else HT[:, k, bass.ds(j * TILE + h * 256, 256)]
                                    last = nc.tensor.matmul(banks[h * 3 + g][:, m * 256:(m + 1) * 256],
                                                            uT[:, g + 4 * part, k, half_of(m)], src,
                                                            start=not part and m == 0 and k == 0, stop=part == 1, skip_group_check=True)
                            if part:
                                last.then_inc(gate2_psum, 1)
            pe.wait_ge(cell_ready, 2 * B + 2)
            for m in range(KD):
                for k in range(KD):
                    last = nc.tensor.matmul(banks[6 + m][:], uT[:, 7, k, half_of(m)], c2[:, k], start=k == 0, stop=k == KD - 1)
                last.then_inc(cpart_psum, 1)
            with pe.Fori(0, B // 2) as j2:
                for i in range(2):
                    for m in range(KD):
                        pe.wait_ge(o2_sum, j2 * 4 + i * 2 + m + 1)
                        for k in range(KD):
                            last = nc.tensor.matmul(banks[i * 2 + m][:], uT[:, 3, k, half_of(m)], HT[:, k, cols(j2 * 2 + i)],
                                                    start=k == 0, stop=k == KD - 1)
                        last.then_inc(o2_psum, 1)
            pe.wait_ge(d3_in, 4)
            for m in range(KD):
                for k in range(KD):
                    last = nc.tensor.matmul(banks[6][:, m * B:(m + 1) * B], w3sq[:, k, half_of(m)], ysq3[:, k],
                                            start=k == 0, stop=k == KD - 1)
            last.then_inc(d3_psum, 1)
            pe.sem_inc(c3_psum, 4)
            with pe.Fori(0, B // 2) as j2:
                for i in range(2):
                    j = j2 * 2 + i
                    pe.wait_ge(xs3_ready, j * 2 + 2)
                    for m in range(KD):
                        pe.wait_ge(c3_ready, j * 2 + m + 1)
                        for k in range(KD):
                            last = nc.tensor.matmul(banks[m][:], w3c[:, k, half_of(m)], hid[:, 2 * i + k],
                                                    start=k == 0, stop=k == KD - 1)
                        last.then_inc(c3_psum, 1)
            pe.wait_ge(c3_ready, 2 * B + 2)

            def scores(j):
                if j:
                    pe.wait_ge(s3_row, j)
                for k in range(KD):
                    last = nc.tensor.matmul(banks[6][:], wr3b[:, k], HT[:, k, j * TILE:(j + 1) * TILE], start=k == 0, stop=k == KD - 1)
                last.then_inc(s3_psum, 1)

            def turn_batch(j, src, h, bank):
                for s in (2 * h, 2 * h + 1):
                    for k in range(KD):
                        last = nc.tensor.transpose(bank[:, s % 2 * D + k * P:s % 2 * D + (k + 1) * P],
                                                   src[:, k, j * TILE + s * P:j * TILE + (s + 1) * P], ident[:])
                return last

            scores(0)
            for j in range(B):
                if j + 1 < B:
                    scores(j + 1)
                for h in range(2):
                    if j:
                        pe.wait_ge(row_ready, BLK3 + 2 * j + h - 1)
                    turn_batch(j, HT, h, banks[h]).then_inc(row_psum, 1)
                pe.wait_ge(xh_sum, j + 1)
                for h in range(2):
                    if j:
                        pe.wait_ge(base_ready, 2 * j + h - 1)
                    turn_batch(j, XT, h, banks[4 + h]).then_inc(base_psum, 1)
                pe.wait_ge(beats_ready, j + 1)
                if j:
                    pe.wait_ge(ranked, j)
                for c in range(NSUB):
                    o = banks[7][:, c:c + 1]
                    for s in range(NSUB):
                        nc.tensor.matmul(o, beats[:, s, c * P:(c + 1) * P], ones16[:, 0:1], start=s == 0, stop=False)
                    last = nc.tensor.matmul(o, ties[:, c], ones16[:, 0:1], start=False, stop=True)
                last.then_inc(rank_psum, 1)

            S = ffn[3]
            pe.sem_inc(S["hid_used"], F3)

            def turn_picked(j):
                pe.wait_ge(xrow_loaded[j % 2], (2 * SIDE[j % 2] + j // 2 + 1) * 16)
                for k in range(KD):
                    for s in range(ES):
                        last = nc.tensor.transpose(banks[6][:, k * ET + s * P:k * ET + (s + 1) * P], xrow[:, j % 2, s, half_of(k)], ident[:])
                last.then_inc(xgT_psum, 1)

            pe.wait_ge(row_ready, BLK3 + 2 * B)
            pe.wait_ge(base_ready, 2 * B)
            turn_picked(0)
            for j in range(B):
                pe.wait_ge(xgT_ready, ROWS3 + j + 1)
                for f in range(F3 + LAG):
                    if f < F3:
                        pe.wait_ge(S["hid_ready"], j * F3 + f + 1)
                        for k in range(KD):
                            last = nc.tensor.matmul(banks[f % RING][:, 0:ET], w3_up[:, k, f * P:(f + 1) * P], xgT[:, j % 2, k],
                                                    start=k == 0, stop=k == KD - 1)
                        last.then_inc(S["up_psum"], 1)
                    if f == F3 and j + 1 < B:
                        turn_picked(j + 1)
                    h = f - LAG
                    if h == 0:
                        pe.wait_ge(S["out_free"], j + 1)
                    if h >= 0:
                        pe.wait_ge(S["hid_ready"], j * F3 + h + 1 + RING)
                        for m in range(ES):
                            last = nc.tensor.matmul(banks[4 + m][:, 0:D], hid0[:, h, half_of(m)], w3_down[:, h],
                                                    start=h == 0, stop=h == F3 - 1)
                        last.then_inc(S["hid_used"], 1)


_OUT_SHAPE = (B, T, D)


def kernel(**inputs):
    from concourse import bacc as _bacc
    from concourse.bass_utils import run_bass_kernel_spmd as _run

    nc = _bacc.Bacc("TRN2", target_bir_lowering=False, num_devices=1)
    arrays, t = {}, {}
    for name, a in inputs.items():
        a = np.ascontiguousarray(a)
        arrays[f"in_{name}"] = a
        t[name] = nc.dram_tensor(f"in_{name}", a.shape, mybir.dt.from_np(a.dtype), kind="ExternalInput").ap()
    out = nc.dram_tensor("out_0", _OUT_SHAPE, F32, kind="ExternalOutput").ap()
    build_program(nc, t, out)
    return _run(nc, [arrays], core_ids=[0]).results[0]["out_0"]
```
